# Optimizing a Trainium2 kernel written in Bass

```python
import numpy as np
import jax
import jax.numpy as jnp

def _softmax(x, axis=-1):
    return jax.nn.softmax(x, axis=axis)

def _gelu(x):
    return jax.nn.gelu(x, approximate=True)

def _silu(x):
    return jax.nn.silu(x)

def _sigmoid(x):
    return jax.nn.sigmoid(x)

def _layernorm(x, axis=-1, eps=1e-05):
    m = jnp.mean(x, axis=axis, keepdims=True)
    v = jnp.var(x, axis=axis, keepdims=True)
    return (x - m) / jnp.sqrt(v + eps)

def _scatter_add(tgt, idx, src, axis=0):
    return tgt.at[idx].add(src)

def _segment_sum(src, seg, n):
    return jax.ops.segment_sum(src, seg, n)
kernel_name = 'mk_cond_seq_d2_seqx_r4_4821d2'

def setup_inputs(seed: int=0):
    np.random.seed(seed)
    _w = jnp.asarray

    def _rec_inputs():
        import jax
        import jax.numpy as jnp
        _rk = jax.random.key(seed)
        x = -0.0003929 + 0.9999 * jax.random.normal(jax.random.fold_in(_rk, 1), (8, 512, 256), jnp.float32)
        _lenS = 512 - jax.random.randint(jax.random.fold_in(_rk, 7), (8,), 0, max(1, 512 // 4) + 1, jnp.int32)
        _lenS2 = 512 - jax.random.randint(jax.random.fold_in(_rk, 8), (8,), 0, max(1, 512 // 4) + 1, jnp.int32)
        cond_256 = -0.0209273 + 1.04763 * jax.random.normal(jax.random.fold_in(_rk, 11), (8, 64), jnp.float32)
        return (x, cond_256)
    x, cond_256 = _rec_inputs()

    def _L0_cond_setup():
        import jax, jax.numpy as jnp
        import numpy as np
        EPS = 1e-06

        def act_quant(x):
            scale = 127.0 / jnp.clip(jnp.max(jnp.abs(x), axis=-1, keepdims=True), 1e-05, None)
            return jnp.clip(jnp.round(x * scale), -128.0, 127.0) / scale

        def weight_quant(w):
            scale = 1.0 / jnp.clip(jnp.mean(jnp.abs(w)), 1e-05, None)
            return jnp.clip(jnp.round(w * scale), -1.0, 1.0) / scale
        key = jax.random.key(seed)
        k0, k1, k2, k3, k4 = jax.random.split(key, 5)
        B, S, D, FF, C = (4, 1024, 256, 1024, 64)
        return {'x': jax.random.normal(k0, (B, S, D), jnp.float32), 'cond': jax.random.normal(k1, (B, C), jnp.float32), 'norm_w': jax.random.normal(k2, (D, C), jnp.float32) * 0.02, 'up_w': jax.random.normal(k3, (2 * FF, D), jnp.float32) * 0.02, 'down_w': jax.random.normal(k4, (D, FF), jnp.float32) * 0.02}
    _L0_cond_all = _L0_cond_setup()
    _L0_cond_in = {k: v for k, v in _L0_cond_all.items() if k in ('norm_w', 'up_w', 'down_w')}
    del _L0_cond_all

    def _L1_cond_setup():
        import jax, jax.numpy as jnp
        import numpy as np
        from math import sqrt
        D_MODEL = 256
        N_HEADS = 16
        D_T = 64
        D_HID = 4 * D_MODEL
        EPS = 1e-06

        def _rmsnorm(x):
            return x * jax.lax.rsqrt(jnp.mean(x * x, axis=-1, keepdims=True) + EPS)

        def _ada_rmsnorm(x, t, gamma_w, beta_w):
            gamma = (t @ gamma_w.T)[:, None, :]
            beta = (t @ beta_w.T)[:, None, :]
            return gamma * _rmsnorm(x) + beta

        def _attention(x, W_q, W_k, W_v, W_o):
            b, l, dm = x.shape
            d_head = dm // N_HEADS
            scale = sqrt(N_HEADS / dm)

            def split(y):
                return y.reshape(b, l, N_HEADS, d_head).transpose(0, 2, 1, 3)
            q = split(x @ W_q.T)
            k = split(x @ W_k.T)
            v = split(x @ W_v.T)
            attn = jax.nn.softmax(scale * jnp.einsum('bnqd,bnkd->bnqk', q, k), axis=-1)
            o = jnp.einsum('bnqk,bnkd->bnqd', attn, v)
            o = o.transpose(0, 2, 1, 3).reshape(b, l, dm)
            return o @ W_o.T

        def _swiglu(x, gate_w, hidden_w, out_w, out_b):
            return jax.nn.silu(x @ gate_w.T) * (x @ hidden_w.T) @ out_w.T + out_b
        key = jax.random.key(seed)
        ks = jax.random.split(key, 16)
        s = 0.02
        inp = {'x': jax.random.normal(ks[0], (4, 512, D_MODEL), dtype=jnp.float32), 't': jax.random.normal(ks[1], (4, D_T), dtype=jnp.float32), 'attn_gamma_w': jax.random.normal(ks[2], (D_MODEL, D_T), dtype=jnp.float32) * s, 'attn_beta_w': jax.random.normal(ks[3], (D_MODEL, D_T), dtype=jnp.float32) * s, 'W_q': jax.random.normal(ks[4], (D_MODEL, D_MODEL), dtype=jnp.float32) * s, 'W_k': jax.random.normal(ks[5], (D_MODEL, D_MODEL), dtype=jnp.float32) * s, 'W_v': jax.random.normal(ks[6], (D_MODEL, D_MODEL), dtype=jnp.float32) * s, 'W_o': jax.random.normal(ks[7], (D_MODEL, D_MODEL), dtype=jnp.float32) * s, 'attn_alpha_w': jax.random.normal(ks[8], (D_MODEL, D_T), dtype=jnp.float32) * s, 'ffn_gamma_w': jax.random.normal(ks[9], (D_MODEL, D_T), dtype=jnp.float32) * s, 'ffn_beta_w': jax.random.normal(ks[10], (D_MODEL, D_T), dtype=jnp.float32) * s, 'gate_w': jax.random.normal(ks[11], (D_HID, D_MODEL), dtype=jnp.float32) * s, 'hidden_w': jax.random.normal(ks[12], (D_HID, D_MODEL), dtype=jnp.float32) * s, 'out_w': jax.random.normal(ks[13], (D_MODEL, D_HID), dtype=jnp.float32) * s, 'out_b': jnp.zeros((D_MODEL,), dtype=jnp.float32), 'ffn_alpha_w': jax.random.normal(ks[14], (D_MODEL, D_T), dtype=jnp.float32) * s}
        return inp
    _L1_cond_all = _L1_cond_setup()
    _L1_cond_in = {k: v for k, v in _L1_cond_all.items() if k in ('attn_gamma_w', 'attn_beta_w', 'W_q', 'W_k', 'W_v', 'W_o', 'attn_alpha_w', 'ffn_gamma_w', 'ffn_beta_w', 'gate_w', 'hidden_w', 'out_w', 'out_b', 'ffn_alpha_w')}
    del _L1_cond_all
    return {'x': x, 'cond_256': cond_256, 'L0_cond_norm_w': _L0_cond_in['norm_w'], 'L0_cond_up_w': _L0_cond_in['up_w'], 'L0_cond_down_w': _L0_cond_in['down_w'], 'L1_cond_attn_gamma_w': _L1_cond_in['attn_gamma_w'], 'L1_cond_attn_beta_w': _L1_cond_in['attn_beta_w'], 'L1_cond_W_q': _L1_cond_in['W_q'], 'L1_cond_W_k': _L1_cond_in['W_k'], 'L1_cond_W_v': _L1_cond_in['W_v'], 'L1_cond_W_o': _L1_cond_in['W_o'], 'L1_cond_attn_alpha_w': _L1_cond_in['attn_alpha_w'], 'L1_cond_ffn_gamma_w': _L1_cond_in['ffn_gamma_w'], 'L1_cond_ffn_beta_w': _L1_cond_in['ffn_beta_w'], 'L1_cond_gate_w': _L1_cond_in['gate_w'], 'L1_cond_hidden_w': _L1_cond_in['hidden_w'], 'L1_cond_out_w': _L1_cond_in['out_w'], 'L1_cond_out_b': _L1_cond_in['out_b'], 'L1_cond_ffn_alpha_w': _L1_cond_in['ffn_alpha_w']}

def reference(x, cond_256, L0_cond_norm_w, L0_cond_up_w, L0_cond_down_w, L1_cond_attn_gamma_w, L1_cond_attn_beta_w, L1_cond_W_q, L1_cond_W_k, L1_cond_W_v, L1_cond_W_o, L1_cond_attn_alpha_w, L1_cond_ffn_gamma_w, L1_cond_ffn_beta_w, L1_cond_gate_w, L1_cond_hidden_w, L1_cond_out_w, L1_cond_out_b, L1_cond_ffn_alpha_w):
    import jax
    import jax.numpy as jnp

    def _L0_cond_ref(x, cond, norm_w, up_w, down_w):
        import jax, jax.numpy as jnp
        import numpy as np
        EPS = 1e-06

        def act_quant(x):
            scale = 127.0 / jnp.clip(jnp.max(jnp.abs(x), axis=-1, keepdims=True), 1e-05, None)
            return jnp.clip(jnp.round(x * scale), -128.0, 127.0) / scale

        def weight_quant(w):
            scale = 1.0 / jnp.clip(jnp.mean(jnp.abs(w)), 1e-05, None)
            return jnp.clip(jnp.round(w * scale), -1.0, 1.0) / scale
        scale = cond @ norm_w.T + 1.0
        ms = jnp.mean(x * x, axis=-1, keepdims=True)
        h = x * (scale[:, None, :] * jax.lax.rsqrt(ms + EPS))
        u = h @ up_w.T
        val, gate = jnp.split(u, 2, axis=-1)
        h = val * jax.nn.gelu(gate, approximate=False)
        hq = h + jax.lax.stop_gradient(act_quant(h) - h)
        wq = down_w + jax.lax.stop_gradient(weight_quant(down_w) - down_w)
        y = hq @ wq.T
        return y + x

    def _L1_cond_ref(x, t, attn_gamma_w, attn_beta_w, W_q, W_k, W_v, W_o, attn_alpha_w, ffn_gamma_w, ffn_beta_w, gate_w, hidden_w, out_w, out_b, ffn_alpha_w):
        import jax, jax.numpy as jnp
        import numpy as np
        from math import sqrt
        D_MODEL = 256
        N_HEADS = 16
        D_T = 64
        D_HID = 4 * D_MODEL
        EPS = 1e-06

        def _rmsnorm(x):
            return x * jax.lax.rsqrt(jnp.mean(x * x, axis=-1, keepdims=True) + EPS)

        def _ada_rmsnorm(x, t, gamma_w, beta_w):
            gamma = (t @ gamma_w.T)[:, None, :]
            beta = (t @ beta_w.T)[:, None, :]
            return gamma * _rmsnorm(x) + beta

        def _attention(x, W_q, W_k, W_v, W_o):
            b, l, dm = x.shape
            d_head = dm // N_HEADS
            scale = sqrt(N_HEADS / dm)

            def split(y):
                return y.reshape(b, l, N_HEADS, d_head).transpose(0, 2, 1, 3)
            q = split(x @ W_q.T)
            k = split(x @ W_k.T)
            v = split(x @ W_v.T)
            attn = jax.nn.softmax(scale * jnp.einsum('bnqd,bnkd->bnqk', q, k), axis=-1)
            o = jnp.einsum('bnqk,bnkd->bnqd', attn, v)
            o = o.transpose(0, 2, 1, 3).reshape(b, l, dm)
            return o @ W_o.T

        def _swiglu(x, gate_w, hidden_w, out_w, out_b):
            return jax.nn.silu(x @ gate_w.T) * (x @ hidden_w.T) @ out_w.T + out_b
        a_alpha = (t @ attn_alpha_w.T)[:, None, :]
        x = x + a_alpha * _attention(_ada_rmsnorm(x, t, attn_gamma_w, attn_beta_w), W_q, W_k, W_v, W_o)
        f_alpha = (t @ ffn_alpha_w.T)[:, None, :]
        return x + f_alpha * _swiglu(_ada_rmsnorm(x, t, ffn_gamma_w, ffn_beta_w), gate_w, hidden_w, out_w, out_b)
    x = _L0_cond_ref(x, cond_256, L0_cond_norm_w, L0_cond_up_w, L0_cond_down_w)
    x = _L1_cond_ref(x, cond_256, L1_cond_attn_gamma_w, L1_cond_attn_beta_w, L1_cond_W_q, L1_cond_W_k, L1_cond_W_v, L1_cond_W_o, L1_cond_attn_alpha_w, L1_cond_ffn_gamma_w, L1_cond_ffn_beta_w, L1_cond_gate_w, L1_cond_hidden_w, L1_cond_out_w, L1_cond_out_b, L1_cond_ffn_alpha_w)
    return x

_drawn_inputs = setup_inputs


def setup_inputs(seed=0):
    import zlib

    import numpy as np

    out = dict(_drawn_inputs(seed))
    spreads = {'L1_cond_out_b': (0.0, 0.1)}
    factors = {}
    for name, (base, spread) in spreads.items():
        noise = np.random.default_rng([zlib.crc32(name.encode()), seed]).standard_normal(out[name].shape)
        drawn = base * np.exp(spread * noise) if base else spread * noise
        out[name] = jnp.asarray(drawn.astype(out[name].dtype))
    for name, factor in factors.items():
        out[name] = (out[name] * factor).astype(out[name].dtype)
    return out
```

```python
import concourse.bass as bass
from concourse import mybir
from contextlib import ExitStack


def cond_seq_kernel(nc, x_tok, xT, condT, norm_wT, up_wT, down_wT, agam_wT, abet_wT, wqT, wkT, wvT, woT,
                    aalpha_wT, fgam_wT, fbet_wT, gate_wT, hidden_wT, out_wT, out_b, falpha_wT, out):
    f32 = mybir.dt.float32
    f32r = mybir.dt.float32r
    bf16 = mybir.dt.bfloat16
    ALU = mybir.AluOpType
    ACT = mybir.ActivationFunctionType
    AX = mybir.AxisListType

    P = 128
    B = condT.shape[1]
    C = condT.shape[0]
    D = norm_wT.shape[1]
    KD = D // P
    S = xT.shape[0] * P // B
    T = S // P
    FF = down_wT.shape[0]
    KF = FF // P
    NH = gate_wT.shape[1] // P
    HD = 16
    G = 4
    J = 4
    W = 512
    EPS = 1e-6
    ROUND = 1.5 * 2.0 ** 23
    QMAX = 127.0
    PARTS = ((0, 0), (0, 1), (1, 0))
    ROWS = 3 * HD
    SROWS = ROWS + 2

    ctx = ExitStack()
    with ctx:
        def sb(stack, name, shape, dt=f32):
            return stack.enter_context(nc.sbuf_tensor(name, shape, dt))

        def sem(name):
            return ctx.enter_context(nc.semaphore(name))

        def dram(name, shape):
            return nc.dram_tensor(name, shape, f32, kind="Internal").ap()

        x1_dram = dram("x1_spill", (B, T, P, D))
        xa_dram = dram("xa_spill", (B, T, P, KD, P))
        alpha_dram = dram("alpha_spill", (B, 3 * D))

        psum = [ctx.enter_context(nc.psum_tensor(f"bank{i}", [P, W], f32)) for i in range(8)]

        par = sb(ctx, "par", [P, B, 5 * KD])
        SCALE0, AGAM, ABET, FGAM, FBET = (KD * n for n in range(5))
        ident = sb(ctx, "ident", [P, P])
        identb = sb(ctx, "identb", [P, P], bf16)
        minus_half = sb(ctx, "minus_half", [P, T])
        wdeq = sb(ctx, "wdeq", [P, 1])
        gate_w = [sb(ctx, f"gate_w{i}", [P, KD, NH * P], f32r) for i in range(2)]
        hidden_w = [sb(ctx, f"hidden_w{i}", [P, KD, NH * P], f32r) for i in range(2)]
        out_w = [sb(ctx, f"out_w{i}", [P, NH, D], f32r) for i in range(2)]
        wq = [sb(ctx, f"wq{i}", [P, KD, D], f32r) for i in range(2)]
        wk = [sb(ctx, f"wk{i}", [P, KD, D], f32r) for i in range(2)]
        wv = [sb(ctx, f"wv{i}", [P, KD, D], f32r) for i in range(2)]
        wo = [sb(ctx, f"wo{i}", [P, G, D], f32r) for i in range(2)]

        phase1 = ExitStack()
        up_w = [sb(phase1, f"up_w{i}", [P, KD, 2 * FF], f32r) for i in range(2)]
        down_q = sb(phase1, "down_q", [P, KF, D], bf16)
        stage_stack = ExitStack()
        up_st = sb(stage_stack, "up_st", [P, KD, 2 * FF])
        down_st = sb(stage_stack, "down_st", [P, KF, D])
        gate_st = sb(stage_stack, "gate_st", [P, KD, NH * P])
        hidden_st = sb(stage_stack, "hidden_st", [P, KD, NH * P])
        out_st = sb(stage_stack, "out_st", [P, NH, D])
        q_st = sb(stage_stack, "q_st", [P, KD, D])
        k_st = sb(stage_stack, "k_st", [P, KD, D])
        v_st = sb(stage_stack, "v_st", [P, KD, D])
        o_st = sb(stage_stack, "o_st", [P, G, D])
        cond_sb = sb(stage_stack, "cond_sb", [C, B])
        vec_w = sb(stage_stack, "vec_w", [C, 7, D])
        outb_sb = sb(stage_stack, "outb_sb", [B, D])
        alpha_sb = sb(stage_stack, "alpha_sb", [B, 3, D])
        ones = sb(stage_stack, "ones", [P, P])
        absum = sb(stage_stack, "absum", [P, 1])
        mean = sb(stage_stack, "mean", [P, 1])
        wscale = sb(stage_stack, "wscale", [P, 1])

        small_loaded = sem("small_loaded")
        down_loaded = sem("down_loaded")
        weight_loaded = [sem(f"weight_loaded{i}") for i in range(8)]
        ostage_zeroed = sem("ostage_zeroed")
        consts_ready = sem("consts_ready")
        high_done = sem("high_done")
        vectors_done = sem("vectors_done")
        alpha_done = sem("alpha_done")
        alpha_stored = sem("alpha_stored")
        down_steps = sem("down_steps")
        mean_summed = sem("mean_summed")

        pairs = [(up_st, up_w, up_wT), (q_st, wq, wqT), (k_st, wk, wkT), (v_st, wv, wvT), (o_st, wo, woT),
                 (gate_st, gate_w, gate_wT), (hidden_st, hidden_w, hidden_wT), (out_st, out_w, out_wT)]

        xt_loaded = [sem(f"xt_loaded{t}") for t in range(T)]
        xk_loaded = [sem(f"xk_loaded{s}") for s in range(2)]
        scale_ready = sem("scale_ready")
        x_scaled = sem("x_scaled")
        x_high = sem("x_high")
        x_split = sem("x_split")
        square_done = sem("square_done")
        ms_done = sem("ms_done")
        rstd_done = sem("rstd_done")
        up_gate_done = sem("up_gate_done")
        up_val_done = sem("up_val_done")
        up_done = sem("up_done")
        gelu_done = sem("gelu_done")
        h_done = sem("h_done")
        scale_steps = sem("scale_steps")
        dequant_done = sem("dequant_done")
        rounded = sem("rounded")
        quantised = sem("quantised")
        q_transposed = sem("q_transposed")
        qT_copied = sem("qT_copied")
        down_done = sem("down_done")
        x1_done = sem("x1_done")
        x1_stored = [sem(f"x1_stored{t}") for t in range(T)]
        square2_done = sem("square2_done")
        ms2_done = sem("ms2_done")
        rstd2_done = sem("rstd2_done")
        xn_done = sem("xn_done")
        xn_transposed = sem("xn_transposed")
        xa_done = sem("xa_done")
        xa_stored = [sem(f"xa_stored{s}") for s in range(2)]
        CREDIT1 = {x_split: 1, x_scaled: 2, up_done: 2, gelu_done: 2, h_done: 2, quantised: 1, q_transposed: 2,
                   qT_copied: 1, down_done: 1, x1_done: 4, ms_done: 1, rstd_done: 2, ms2_done: 1,
                   rstd2_done: 1, xn_transposed: 1, xa_done: 1,
                   x1_stored[0]: 1, x1_stored[1]: 1, x1_stored[2]: 1, x1_stored[3]: 1,
                   xa_stored[0]: 1, xa_stored[1]: 1}

        vext_zeroed = sem("vext_zeroed")
        ones_ready = sem("ones_ready")
        xa_loaded = sem("xa_loaded")
        x1_loaded = sem("x1_loaded")
        aalpha_loaded = sem("aalpha_loaded")
        falpha_loaded = sem("falpha_loaded")
        pair_full = [sem("bank_a_full"), sem("bank_b_full")]
        pair_free = [sem("bank_a_free"), sem("bank_b_free")]
        q_in_high = sem("q_in_high")
        q_in_low = sem("q_in_low")
        f_in_high = sem("f_in_high")
        f_in_low = sem("f_in_low")
        qkv_projected = sem("qkv_projected")
        qk_high = sem("qk_high")
        stacked = sem("stacked")
        raw_full = sem("raw_full")
        raw_read = sem("raw_read")
        shift_high = sem("shift_high")
        shift_loaded = sem("shift_loaded")
        score_full = sem("score_full")
        exp_done = sem("exp_done")
        pv_done = sem("pv_done")
        o_read = sem("o_read")
        norm_steps = sem("norm_steps")
        on_done = sem("on_done")
        on_high = sem("on_high")
        on_low = sem("on_low")
        wo_done = sem("wo_done")
        x2_done = [sem(f"x2_done{m}") for m in range(2)]
        square3_done = sem("square3_done")
        ms3_done = sem("ms3_done")
        rstd3_done = sem("rstd3_done")
        xn3_done = sem("xn3_done")
        x2_biased = sem("x2_biased")
        tanh_done = sem("tanh_done")
        prod_high = sem("prod_high")
        prod_low = sem("prod_low")
        ffn_projected = sem("ffn_projected")
        y_done = sem("y_done")
        y_stored = [sem(f"y_stored{m}") for m in range(2)]
        CREDIT2 = {pair_free[0]: 1, pair_free[1]: 1, raw_read: 2, exp_done: 1, pv_done: 2, o_read: 1, on_low: 1,
                   shift_loaded: 1, ffn_projected: 2, wo_done: 1, prod_low: 1, q_in_low: 1, f_in_low: 2,
                   x2_done[0]: 1, x2_done[1]: 1, y_done: 2, y_stored[0]: 1, y_stored[1]: 1}

        def credited(s, value):
            return value + CREDIT1.get(s, CREDIT2.get(s, 0))

        def live(tile, lag):
            return tile is None or 0 <= tile - lag < B * T

        with nc.Block() as block:
            @block.sync
            def _(sp):
                sp.dma_start(up_st[:], up_wT.rearrange("(k p) n -> p k n", p=P)).then_inc(weight_loaded[0], 16)
                sp.dma_start(down_st[:], down_wT.rearrange("(k p) n -> p k n", p=P)).then_inc(down_loaded, 16)
                for n in (1, 2, 3, 5, 6, 7):
                    dst, _, src = pairs[n]
                    sp.dma_start(dst[:], src.rearrange("(k p) n -> p k n", p=P)).then_inc(weight_loaded[n], 16)
                sp.wait_ge(ostage_zeroed, 1)
                wo_rows = woT.rearrange("(g j d) n -> j d g n", g=G, j=J)
                for j in range(J):
                    sp.dma_start(o_st[32 * j:32 * j + HD, :, :], wo_rows[j]).then_inc(weight_loaded[4], 16)
                sp.wait_ge(alpha_done, 3)
                sp.dma_start(alpha_dram, alpha_sb[:].rearrange("b a n -> b (a n)")).then_inc(alpha_stored, 16)
                sp.wait_ge(alpha_stored, 16)

            @block.scalar
            def _(act):
                act.dma_start(cond_sb[:], condT).then_inc(small_loaded, 16)
                for n, w in enumerate((norm_wT, agam_wT, abet_wT, fgam_wT, fbet_wT, aalpha_wT, falpha_wT)):
                    act.dma_start(vec_w[:, n, :], w).then_inc(small_loaded, 16)
                act.dma_start(outb_sb[:], out_b.partition_broadcast(B)).then_inc(small_loaded, 16)
                for n, (src, dst, _) in enumerate(pairs):
                    act.wait_ge(weight_loaded[n], 64 if n == 4 else 16)
                    nc.scalar.activation(dst[0][:], src[:], ACT.Copy).then_inc(high_done, 1)

            @block.gpsimd
            def _(pool):
                for s, value in list(CREDIT1.items()) + list(CREDIT2.items()):
                    nc.gpsimd.sem_inc(s, value)
                nc.gpsimd.memset(o_st[:], 0.0).then_inc(ostage_zeroed, 1)
                nc.gpsimd.memset(minus_half[:], -0.5)
                nc.gpsimd.memset(ones[:], 1.0).then_inc(consts_ready, 1)
                nc.gpsimd.memset(ident[:], 0.0).then_inc(consts_ready, 1)
                nc.gpsimd.memset(identb[:], 0.0).then_inc(consts_ready, 1)
                pool.wait_ge(consts_ready, 3)
                for m in (ident, identb):
                    nc.gpsimd.affine_select(out=m[:], in_=m[:], compare_op=ALU.not_equal, fill=1.0, base=0,
                                            pattern=[[-1, P]], channel_multiplier=1).then_inc(consts_ready, 1)

            @block.tensor
            def _(pe):
                pe.wait_ge(small_loaded, 16 * 9)
                for v in range(5):
                    for k in range(KD):
                        last = nc.tensor.matmul(psum[0][:, (v * KD + k) * B:(v * KD + k + 1) * B],
                                                vec_w[:, v, k * P:(k + 1) * P], cond_sb[:], start=True, stop=True)
                last.then_inc(vectors_done, 1)
                for v in range(2):
                    last = nc.tensor.matmul(psum[1][0:B, v * D:(v + 1) * D], cond_sb[:], vec_w[:, 5 + v, :],
                                            start=True, stop=True)
                last.then_inc(vectors_done, 1)
                pe.wait_ge(consts_ready, 5)
                pe.wait_ge(down_steps, 1)
                nc.tensor.matmul(psum[2][:, 0:1], ones[:], absum[:], start=True, stop=True).then_inc(mean_summed, 1)

            @block.vector
            def _(dve):
                dve.wait_ge(vectors_done, 1)
                vectors = psum[0][:, 0:5 * KD * B].rearrange("p (v b) -> p b v", b=B)
                nc.vector.tensor_scalar(par[:, :, 0:KD], vectors[:, :, 0:KD], 1.0, None, ALU.add)
                nc.vector.tensor_copy(par[:, :, KD:], vectors[:, :, KD:])
                dve.wait_ge(vectors_done, 2)
                dve.wait_ge(small_loaded, 16 * 9)
                nc.vector.tensor_copy(alpha_sb[:, 0:2, :], psum[1][0:B, :].rearrange("b (a n) -> b a n", a=2)) \
                    .then_inc(alpha_done, 1)
                dve.wait_ge(alpha_done, 1)
                nc.vector.tensor_tensor(alpha_sb[:, 2, :], alpha_sb[:, 1, :], outb_sb[:], ALU.mult) \
                    .then_inc(alpha_done, 2)
                dve.wait_ge(down_loaded, 16)
                nc.vector.tensor_reduce(absum[:], down_st[:], AX.XY, ALU.add, apply_absolute_value=True) \
                    .then_inc(down_steps, 1)
                dve.wait_ge(mean_summed, 1)
                nc.vector.tensor_scalar(mean[:], psum[2][:, 0:1], 1.0 / (FF * D), 1e-5, ALU.mult, ALU.max) \
                    .then_inc(down_steps, 1)
                dve.wait_ge(down_steps, 2)
                nc.vector.tensor_scalar(wdeq[:], mean[:], 1.0 / QMAX, None, ALU.mult)
                nc.vector.reciprocal(wscale[:], mean[:]).then_inc(down_steps, 1)
                dve.wait_ge(down_steps, 3)
                nc.vector.tensor_scalar(down_st[:], down_st[:], wscale[:], 1.0, ALU.mult, ALU.min) \
                    .then_inc(down_steps, 1)
                dve.wait_ge(down_steps, 4)
                nc.vector.tensor_scalar(down_st[:], down_st[:], -1.0, ROUND, ALU.max, ALU.add) \
                    .then_inc(down_steps, 1)
                dve.wait_ge(down_steps, 5)
                nc.vector.tensor_scalar(down_q[:], down_st[:], ROUND, None, ALU.subtract)
                for n, (src, dst, _) in enumerate(pairs):
                    dve.wait_ge(high_done, n + 1)
                    nc.vector.tensor_tensor(dst[1][:], src[:], dst[0][:].bitcast(f32), ALU.subtract)
        stage_stack.close()

        xt = sb(phase1, "xt", [P, T, D])
        xk = sb(phase1, "xk", [P, 2, KD, P])
        cur_scale = sb(phase1, "cur_scale", [P, KD])
        xs = sb(phase1, "xs", [P, KD, P])
        xs_part = [sb(phase1, f"xs_part{i}", [P, 2, KD, P], f32r) for i in range(2)]
        square_junk = sb(phase1, "square_junk", [P, D])
        ss = sb(phase1, "ss", [P, 1])
        ms = sb(phase1, "ms", [P, 1])
        rstd = sb(phase1, "rstd", [P, 2])
        gelu = sb(phase1, "gelu", [P, 2, W])
        h = sb(phase1, "h", [P, FF])
        amax = sb(phase1, "amax", [P, 4])
        dequant = sb(phase1, "dequant", [P, 2])
        h_rounded = sb(phase1, "h_rounded", [P, FF])
        h_q = sb(phase1, "h_q", [P, 2, FF], bf16)
        qT = sb(phase1, "qT", [P, FF], bf16)
        x1t = sb(phase1, "x1t", [P, T, D])
        square_junk2 = sb(phase1, "square_junk2", [P, D])
        ss2 = sb(phase1, "ss2", [P, 1])
        ms2 = sb(phase1, "ms2", [P, 1])
        rstd2 = sb(phase1, "rstd2", [P, 1])
        xn = sb(phase1, "xn", [P, D])
        xa = sb(phase1, "xa", [P, 2, KD, P])
        gate_bank = psum[0:2]
        val_bank = psum[2:4]
        tr_bank = psum[4][:].bitcast(bf16)
        down_bank = psum[5]
        xn_bank = psum[6]

        UP, DOWN, NORM, STORE = 1, 2, 3, 4

        def back(b, t, lag):
            return b + (t - lag) // T, (t - lag) % T, b * T + (t - lag)

        def load_tile(sp, b, t, tile):
            if live(tile, 0):
                b, t, n = back(b, t, 0)
                sp.wait_ge(x1_done, credited(x1_done, n - 3))
                sp.dma_start(xt[:, t, :], x_tok[b, t * P:(t + 1) * P, :]).then_inc(xt_loaded[t], 16)
                sp.wait_ge(x_scaled, credited(x_scaled, n - 1))
                sp.dma_start(xk[:, t % 2, :, :], xT[n, :, :, :]).then_inc(xk_loaded[t % 2], 16)

        def act_tile(act, b0, t0, tile):
            if live(tile, 0):
                b, t, n = back(b0, t0, 0)
                act.wait_ge(scale_ready, b + 1)
                act.wait_ge(xk_loaded[t % 2], (b * 2 + t // 2 + 1) * 16)
                act.wait_ge(x_split, credited(x_split, n))
                for k in range(KD):
                    last = nc.scalar.activation(xs[:, k, :], xk[:, t % 2, k, :], ACT.Copy,
                                                scale=cur_scale[:, k:k + 1])
                last.then_inc(x_scaled, 1)
                act.wait_ge(xt_loaded[t], (b + 1) * 16)
                act.wait_ge(ms_done, credited(ms_done, n))
                nc.scalar.activation(square_junk[:], xt[:, t, :], ACT.Square, accum_out=ss[:]) \
                    .then_inc(square_done, 1)
            if live(tile, NORM):
                b, t, m = back(b0, t0, NORM)
                act.wait_ge(x1_done, credited(x1_done, m + 1))
                act.wait_ge(ms2_done, credited(ms2_done, m))
                act.dma_start(x1_dram[b, t, :, :], x1t[:, t, :]).then_inc(x1_stored[t], 16)
                nc.scalar.activation(square_junk2[:], x1t[:, t, :], ACT.Square, accum_out=ss2[:]) \
                    .then_inc(square2_done, 1)
            if live(tile, STORE):
                b, t, m = back(b0, t0, STORE)
                act.wait_ge(xa_done, credited(xa_done, m + 1))
                act.dma_start(xa_dram[b, t, :, :, :], xa[:, t % 2, :, :]).then_inc(xa_stored[t % 2], 16)

            def act_gelu(j):
                b, t, n = back(b0, t0, UP)
                act.wait_ge(up_gate_done, 2 * n + j + 1)
                act.wait_ge(rstd_done, credited(rstd_done, n + 1))
                act.wait_ge(h_done, credited(h_done, 2 * n + j - 1))
                nc.scalar.activation(gelu[:, j, :], gate_bank[j][:], ACT.Gelu, scale=rstd[:, t % 2:t % 2 + 1]) \
                    .then_inc(gelu_done, 1)
            if live(tile, UP):
                act_gelu(0)
            if live(tile, DOWN):
                b, t, m = back(b0, t0, DOWN)
                act.wait_ge(q_transposed, credited(q_transposed, m + 1))
                act.wait_ge(down_done, credited(down_done, m))
                nc.scalar.activation(qT[:], tr_bank[:, 0:FF], ACT.Copy).then_inc(qT_copied, 1)
            if live(tile, UP):
                act_gelu(1)

        def pool_tile(pool, b0, t0, tile):
            if live(tile, 0):
                b, t, n = back(b0, t0, 0)
                pool.wait_ge(up_done, credited(up_done, n - 1))
                pool.wait_ge(x_high, n + 1)
                nc.gpsimd.tensor_tensor(xs_part[1][:, t % 2, :, :], xs[:], xs_part[0][:, t % 2, :, :].bitcast(f32),
                                        ALU.subtract).then_inc(x_split, 1)
                pool.wait_ge(gelu_done, credited(gelu_done, 2 * n - 2))
                pool.wait_ge(h_done, credited(h_done, 2 * n - 2))
                pool.wait_ge(ms_done, credited(ms_done, n + 1))
                nc.gpsimd.tensor_tensor(rstd[:, t % 2:t % 2 + 1], ms[:], minus_half[:, 0:1], ALU.pow) \
                    .then_inc(rstd_done, 1)
            if live(tile, NORM):
                b, t, m = back(b0, t0, NORM)
                if tile is None or m > 0:
                    pool.wait_ge(xn_done, m)
                pool.wait_ge(ms2_done, credited(ms2_done, m + 1))
                nc.gpsimd.tensor_tensor(rstd2[:], ms2[:], minus_half[:, 0:1], ALU.pow).then_inc(rstd2_done, 1)

        def pe_tile(pe, b0, t0, tile):
            def up(j):
                b, t, n = back(b0, t0, UP)
                for bank, col, free, full in ((gate_bank[j], FF + j * W, gelu_done, up_gate_done),
                                              (val_bank[j], j * W, h_done, up_val_done)):
                    pe.wait_ge(free, credited(free, 2 * n + j - 1))
                    steps = [(a, m, k) for k in range(KD) for a, m in PARTS]
                    for i, (a, m, k) in enumerate(steps):
                        last = nc.tensor.matmul(bank[:], xs_part[a][:, t % 2, k, :], up_w[m][:, k, col:col + W],
                                                start=(i == 0), stop=(i == len(steps) - 1))
                    last.then_inc(full, 1)
            if live(tile, UP):
                pe.wait_ge(x_split, credited(x_split, back(b0, t0, UP)[2] + 1))
                up(0)
            if live(tile, DOWN):
                b, t, m = back(b0, t0, DOWN)
                pe.wait_ge(quantised, credited(quantised, m + 1))
                pe.wait_ge(qT_copied, credited(qT_copied, m))
                for k in range(KF):
                    last = nc.tensor.transpose(tr_bank[:, k * P:(k + 1) * P], h_q[:, t % 2, k * P:(k + 1) * P],
                                               identb[:])
                last.then_inc(q_transposed, 1)
            if live(tile, UP):
                up(1)
                nc.tensor.nop().then_inc(up_done, 1)
            if live(tile, DOWN):
                b, t, m = back(b0, t0, DOWN)
                pe.wait_ge(qT_copied, credited(qT_copied, m + 1))
                pe.wait_ge(x1_done, credited(x1_done, m))
                for k in range(KF):
                    last = nc.tensor.matmul(down_bank[:, 0:D], qT[:, k * P:(k + 1) * P], down_q[:, k, :],
                                            start=(k == 0), stop=(k == KF - 1))
                last.then_inc(down_done, 1)
            if live(tile, NORM):
                b, t, m = back(b0, t0, NORM)
                pe.wait_ge(xn_done, m + 1)
                pe.wait_ge(xa_done, credited(xa_done, m))
                for k in range(KD):
                    last = nc.tensor.transpose(xn_bank[:, k * P:(k + 1) * P], xn[:, k * P:(k + 1) * P], ident[:])
                last.then_inc(xn_transposed, 1)

        def dve_tile(dve, b0, t0, tile):
            if live(tile, 0):
                b, t, n = back(b0, t0, 0)
                if t == 0:
                    dve.wait_ge(x_scaled, credited(x_scaled, n))
                    nc.vector.tensor_scalar(cur_scale[:], par[:, b, SCALE0:SCALE0 + KD], 1.0, None, ALU.mult) \
                        .then_inc(scale_ready, 1)
                dve.wait_ge(x_scaled, credited(x_scaled, n + 1))
                dve.wait_ge(up_done, credited(up_done, n - 1))
                nc.vector.tensor_copy(xs_part[0][:, t % 2, :, :], xs[:]).then_inc(x_high, 1)
                dve.wait_ge(square_done, n + 1)
                dve.wait_ge(rstd_done, credited(rstd_done, n))
                nc.vector.tensor_scalar(ms[:], ss[:], 1.0 / D, EPS, ALU.mult, ALU.add).then_inc(ms_done, 1)
            if live(tile, NORM):
                b, t, m = back(b0, t0, NORM)
                dve.wait_ge(square2_done, m + 1)
                dve.wait_ge(rstd2_done, credited(rstd2_done, m))
                nc.vector.tensor_scalar(ms2[:], ss2[:], 1.0 / D, EPS, ALU.mult, ALU.add).then_inc(ms2_done, 1)

            def gate(j):
                b, t, n = back(b0, t0, UP)
                dve.wait_ge(up_val_done, 2 * n + j + 1)
                dve.wait_ge(gelu_done, credited(gelu_done, 2 * n + j + 1))
                nc.vector.scalar_tensor_tensor(h[:, j * W:(j + 1) * W], val_bank[j][:],
                                               rstd[:, t % 2:t % 2 + 1], gelu[:, j, :], ALU.mult, ALU.mult) \
                    .then_inc(h_done, 1)
            if live(tile, UP):
                gate(0)
            if live(tile, NORM):
                b, t, m = back(b0, t0, NORM)
                dve.wait_ge(rstd2_done, credited(rstd2_done, m + 1))
                dve.wait_ge(xn_transposed, credited(xn_transposed, m))
                nc.vector.tensor_scalar(xn[:], x1t[:, t, :], rstd2[:], None, ALU.mult).then_inc(xn_done, 1)
            if live(tile, UP):
                b, t, n = back(b0, t0, UP)
                gate(1)
                dve.wait_ge(h_done, credited(h_done, 2 * n + 2))
                nc.vector.tensor_reduce(amax[:, 0:1], h[:], AX.X, ALU.max, apply_absolute_value=True) \
                    .then_inc(scale_steps, 1)
                dve.wait_ge(scale_steps, 4 * n + 1)
                nc.vector.tensor_scalar(amax[:, 1:2], amax[:, 0:1], 1e-5, None, ALU.max).then_inc(scale_steps, 1)
                dve.wait_ge(scale_steps, 4 * n + 2)
                nc.vector.reciprocal(amax[:, 2:3], amax[:, 1:2]).then_inc(scale_steps, 1)
                nc.vector.tensor_tensor(dequant[:, t % 2:t % 2 + 1], amax[:, 1:2], wdeq[:], ALU.mult) \
                    .then_inc(dequant_done, 1)
                dve.wait_ge(scale_steps, 4 * n + 3)
                nc.vector.tensor_scalar(amax[:, 3:4], amax[:, 2:3], QMAX, None, ALU.mult).then_inc(scale_steps, 1)
                dve.wait_ge(scale_steps, 4 * n + 4)
                nc.vector.tensor_scalar(h_rounded[:], h[:], amax[:, 3:4], ROUND, ALU.mult, ALU.add) \
                    .then_inc(rounded, 1)
                dve.wait_ge(rounded, n + 1)
                dve.wait_ge(q_transposed, credited(q_transposed, n - 1))
                nc.vector.tensor_scalar(h_q[:, t % 2, :], h_rounded[:], ROUND, QMAX, ALU.subtract, ALU.min) \
                    .then_inc(quantised, 1)
            if live(tile, DOWN):
                b, t, m = back(b0, t0, DOWN)
                dve.wait_ge(down_done, credited(down_done, m + 1))
                dve.wait_ge(dequant_done, m + 1)
                if tile is None or m >= T:
                    dve.wait_ge(x1_stored[t], credited(x1_stored[t], b * 16))
                nc.vector.scalar_tensor_tensor(x1t[:, t, :], down_bank[:, 0:D], dequant[:, t % 2:t % 2 + 1],
                                               xt[:, t, :], ALU.mult, ALU.add).then_inc(x1_done, 1)
            if live(tile, NORM):
                b, t, m = back(b0, t0, NORM)
                dve.wait_ge(xn_transposed, credited(xn_transposed, m + 1))
                if tile is None or m >= 2:
                    dve.wait_ge(xa_stored[t % 2], credited(xa_stored[t % 2], (b * 2 + t // 2) * 16))
                for k in range(KD):
                    last = nc.vector.tensor_scalar(xa[:, t % 2, k, :], xn_bank[:, k * P:(k + 1) * P],
                                                   par[:, b, AGAM + k:AGAM + k + 1],
                                                   par[:, b, ABET + k:ABET + k + 1], ALU.mult, ALU.add)
                last.then_inc(xa_done, 1)

        def phase1_program(eng, tile_step):
            for t in range(T):
                tile_step(eng, 0, t, t)
            with eng.Fori(1, B) as b:
                for t in range(T):
                    tile_step(eng, b, t, None)
            for t in range(STORE):
                tile_step(eng, B, t, B * T + t)

        with nc.Block() as block:
            @block.sync
            def _(sp):
                phase1_program(sp, load_tile)

            @block.scalar
            def _(act):
                phase1_program(act, act_tile)
                for t in range(T):
                    act.wait_ge(x1_stored[t], credited(x1_stored[t], B * 16))
                for s in range(2):
                    act.wait_ge(xa_stored[s], credited(xa_stored[s], B * T // 2 * 16))

            @block.gpsimd
            def _(pool):
                phase1_program(pool, pool_tile)

            @block.tensor
            def _(pe):
                phase1_program(pe, pe_tile)

            @block.vector
            def _(dve):
                phase1_program(dve, dve_tile)
        phase1.close()

        q_stack = sb(ctx, "q_stack", [P, 2 * G, S], f32r)
        k_stack = sb(ctx, "k_stack", [P, 2 * G, S], f32r)
        v_ext = sb(ctx, "v_ext", [P, T, G * J, 32])
        probs = sb(ctx, "probs", [P, 2 * J, S])
        aalpha = sb(ctx, "aalpha", [P, D])
        falpha = sb(ctx, "falpha", [P, 2, D])
        x_in = sb(ctx, "x_in", [P, T, KD, P])
        in_part = [sb(ctx, f"in_part{i}", [P, KD, S], f32r) for i in range(2)]
        split = sb(ctx, "split", [P, 8, S], f32r)
        x1 = sb(ctx, "x1", [P, T, D])
        x2 = sb(ctx, "x2", [P, T, D])
        rowmax = sb(ctx, "rowmax", [P, J * T])
        shift = [sb(ctx, f"shift{i}", [J * T, P], f32r) for i in range(2)]
        o_sb = sb(ctx, "o_sb", [P, S])
        o_tok = sb(ctx, "o_tok", [P, S])
        inv_sum = sb(ctx, "inv_sum", [P, S // 32, 1])
        ss3 = sb(ctx, "ss3", [P, T])
        ms3 = sb(ctx, "ms3", [P, T])
        rstd3 = sb(ctx, "rstd3", [P, T])
        square_junk3 = probs[:, J:J + T * D // S, :].rearrange("p a n -> p (a n)").rearrange("p (t d) -> p t d", t=T)
        xn3 = probs[:, 0:T * D // S, :].rearrange("p a n -> p (a n)").rearrange("p (t d) -> p t d", t=T)
        scratch = [sb(ctx, f"scratch{i}", [P, W]) for i in range(2)]
        hid = [sb(ctx, f"hid{i}", [P, NH, S], f32r) for i in range(2)]
        score_bank = psum[0:3]
        raw_bank = psum[3:5]
        o_bank = psum[5]
        ab = psum[6:8]
        SOFTMAX_SCALE = HD ** -0.5
        HALF = T // 2
        USES_Q, USES_F, USES_O = 3, NH + 2, 1
        RAW = J * T + 1

        def by_token(part):
            return part[:].rearrange("p k (t n) -> p t k n", t=T)

        def qkv_act(act, b, u, first):
            act.wait_ge(xa_loaded, (b + 1) * 16)
            if not first:
                act.wait_ge(qkv_projected, b)
                act.wait_ge(ffn_projected, credited(ffn_projected, b - 1))
                act.wait_ge(wo_done, credited(wo_done, b))
            nc.scalar.activation(by_token(in_part[0]), x_in[:], ACT.Copy).then_inc(q_in_high, 1)
            for w in range(2):
                for m in range(KD):
                    act.wait_ge(pair_full[m], u + w + 1)
                    nc.scalar.activation(split[:, 4 * w + m, :], ab[m][:], ACT.Copy,
                                         scale=SOFTMAX_SCALE if w == 0 else 1.0).then_inc(qk_high, 1)

        def qkv_pool(pool, b, u, first):
            pool.wait_ge(q_in_high, b + 1)
            nc.gpsimd.tensor_tensor(by_token(in_part[1]), x_in[:], by_token(in_part[0]).bitcast(f32),
                                    ALU.subtract).then_inc(q_in_low, 1)

        def qkv_pe(pe, b, u, first):
            pe.wait_ge(q_in_low, credited(q_in_low, b + 1))
            steps = [(a, m, k) for k in range(KD) for a, m in PARTS]
            for w, weight in enumerate((wq, wk)):
                for m in range(KD):
                    pe.wait_ge(pair_free[m], credited(pair_free[m], u + w))
                    for i, (a, wp, k) in enumerate(steps):
                        last = nc.tensor.matmul(ab[m][:], weight[wp][:, k, m * P:(m + 1) * P], in_part[a][:, k, :],
                                                start=(i == 0), stop=(i == len(steps) - 1))
                    last.then_inc(pair_full[m], 1)
            for m in range(2):
                pe.wait_ge(pair_free[m], credited(pair_free[m], u + 2))
                for t in range(HALF):
                    tok = (m * HALF + t) * P
                    for i, (a, wp, k) in enumerate(steps):
                        last = nc.tensor.matmul(ab[m][:, t * D:(t + 1) * D], in_part[a][:, k, tok:tok + P],
                                                wv[wp][:, k, :], start=(i == 0), stop=(i == len(steps) - 1))
                last.then_inc(pair_full[m], 1)
            nc.tensor.nop().then_inc(qkv_projected, 1)

        def qkv_dve(dve, b, u, first):
            for w in range(2):
                for m in range(KD):
                    dve.wait_ge(qk_high, 4 * b + 2 * w + m + 1)
                    nc.vector.scalar_tensor_tensor(split[:, 4 * w + 2 + m, :], ab[m][:],
                                                   SOFTMAX_SCALE if w == 0 else 1.0,
                                                   split[:, 4 * w + m, :].bitcast(f32), ALU.mult, ALU.subtract) \
                        .then_inc(pair_free[m], 1)
            for m in range(2):
                dve.wait_ge(pair_full[m], u + 3)
                nc.vector.tensor_copy(v_ext[:, m * HALF:(m + 1) * HALF, :, 0:HD],
                                      ab[m][:].rearrange("p (t h d) -> p t h d", t=HALF, d=HD)) \
                    .then_inc(pair_free[m], 1)

        def raw_score(pe, b, g, s):
            j, qt = s // T, s % T
            half, slot = j % 2, 2 * g + j // 2
            idx = RAW * g + s
            pe.wait_ge(raw_read, credited(raw_read, b * (RAW * G) + (idx - 1)))
            rows = slice(64 * half, 64 * half + ROWS)
            nc.tensor.matmul(raw_bank[idx % 2][:], q_stack[rows, slot, qt * P:(qt + 1) * P], k_stack[rows, slot, :],
                             start=True, stop=True).then_inc(raw_full, 1)

        def maxima_transposed(pe, b, g):
            idx = RAW * g + J * T
            pe.wait_ge(raw_read, credited(raw_read, b * (RAW * G) + idx))
            nc.tensor.transpose(raw_bank[idx % 2][0:J * T, 0:P], rowmax[:], ident[:]).then_inc(raw_full, 1)

        def maxima_dve(dve, b, g, first, count):
            for s in range(first, first + count):
                j, qt = s // T, s % T
                idx = RAW * g + s
                col = (j % 2) * 8 + (j // 2) * T + qt
                dve.wait_ge(raw_full, b * (RAW * G) + (idx + 1))
                nc.vector.reduce_max(rowmax[:, col:col + 1], raw_bank[idx % 2][:], AX.X).then_inc(raw_read, 1)

        def shift_dve(dve, b, g):
            idx = RAW * g + J * T
            dve.wait_ge(raw_full, b * (RAW * G) + (idx + 1))
            dve.wait_ge(shift_loaded, credited(shift_loaded, (b * G + g) * 64))
            src = raw_bank[idx % 2][0:J * T, 0:P]
            nc.vector.tensor_scalar(shift[0][:], src, -1.0, None, ALU.mult).then_inc(shift_high, 1)
            dve.wait_ge(shift_high, b * G + (g + 1))
            nc.vector.scalar_tensor_tensor(shift[1][:], src, -1.0, shift[0][:].bitcast(f32), ALU.mult,
                                           ALU.subtract).then_inc(raw_read, 1)

        def stack_sp(sp, b, u):
            for stack, w, parts in ((q_stack, 0, (0, 0, 1)), (k_stack, 1, (0, 1, 0))):
                for m in range(2):
                    sp.wait_ge(pair_free[m], credited(pair_free[m], u + w + 1))
                for half in range(2):
                    for r, part in enumerate(parts):
                        base = 4 * w + 2 * part
                        sp.dma_start(stack[64 * half + HD * r:64 * half + HD * (r + 1), :, :].bitcast(f32),
                                     split[64 * half:64 * half + 64, base:base + 2, :].bitcast(f32)) \
                            .then_inc(stacked, 16)

        def shift_sp(sp, b, g):
            sp.wait_ge(raw_read, credited(raw_read, b * (RAW * G) + RAW * (g + 1)))
            for half in range(2):
                for part in range(2):
                    row = 64 * half + ROWS + part
                    sp.dma_start(q_stack[row:row + 1, 2 * g:2 * g + 2, :].bitcast(f32),
                                 shift[part][8 * half:8 * half + 8, :].bitcast(f32)).then_inc(shift_loaded, 16)

        def score_pe(pe, b, g, kt, j):
            half, slot = j % 2, 2 * g + j // 2
            c = 16 * g + J * kt + j
            pe.wait_ge(exp_done, credited(exp_done, b * 64 + (c - 2 if c >= 3 else 0)))
            rows = slice(64 * half, 64 * half + SROWS)
            nc.tensor.matmul(score_bank[c % 3][:], k_stack[rows, slot, kt * P:(kt + 1) * P], q_stack[rows, slot, :],
                             start=True, stop=True).then_inc(score_full, 1)

        def values_pe(pe, b, g, kt):
            pe.wait_ge(exp_done, credited(exp_done, b * 64 + (16 * g + J * (kt + 1))))
            if kt == 0:
                pe.wait_ge(o_read, credited(o_read, b * G + g))
            for j in range(J):
                last = nc.tensor.matmul(o_bank[32 * j:32 * j + 32, :], v_ext[:, kt, J * g + j, :],
                                        probs[:, (kt % 2) * J + j, :], start=(kt == 0), stop=(kt == T - 1))
            last.then_inc(pv_done, 1)

        def exp_act(act, b, g, kt):
            act.wait_ge(pv_done, credited(pv_done, b * 16 + (4 * g + kt - 1)))
            for j in range(J):
                c = 16 * g + J * kt + j
                act.wait_ge(score_full, b * 64 + (c + 1))
                nc.scalar.activation(probs[:, (kt % 2) * J + j, :], score_bank[c % 3][:], ACT.Exp) \
                    .then_inc(exp_done, 1)

        def normalise_dve(dve, b, g):
            dve.wait_ge(pv_done, credited(pv_done, b * 16 + 4 * (g + 1)))
            nc.vector.transpose(o_tok[:], o_bank[:]).then_inc(o_read, 1)
            blocks = o_tok[:].rearrange("p (q d) -> p q d", d=32)
            dve.wait_ge(o_read, credited(o_read, b * G + (g + 1)))
            nc.vector.reciprocal(inv_sum[:], blocks[:, :, HD:HD + 1]).then_inc(norm_steps, 1)
            dve.wait_ge(norm_steps, b * (2 * G) + (2 * g + 1))
            nc.vector.tensor_tensor(blocks, blocks, inv_sum[:].broadcast_to([P, S // 32, 32]), ALU.mult) \
                .then_inc(norm_steps, 1)
            dve.wait_ge(norm_steps, b * (2 * G) + (2 * g + 2))
            dve.wait_ge(on_low, credited(on_low, b * G + g))
            nc.vector.transpose(o_sb[:], o_tok[:]).then_inc(on_done, 1)

        def normalise_act(act, b, g):
            act.wait_ge(on_done, b * G + (g + 1))
            nc.scalar.activation(split[:, g, :], o_sb[:], ACT.Copy).then_inc(on_high, 1)

        def normalise_pool(pool, b, g):
            pool.wait_ge(on_high, b * G + (g + 1))
            nc.gpsimd.tensor_tensor(split[:, 4 + g, :], o_sb[:], split[:, g, :].bitcast(f32), ALU.subtract) \
                .then_inc(on_low, 1)

        def project_pe(pe, b, u):
            pe.wait_ge(on_low, credited(on_low, b * G + G))
            steps = [(a, m, g) for g in range(G) for a, m in PARTS]
            for m in range(2):
                pe.wait_ge(pair_free[m], credited(pair_free[m], u))
                for t in range(HALF):
                    tok = (m * HALF + t) * P
                    for i, (a, wp, g) in enumerate(steps):
                        last = nc.tensor.matmul(ab[m][:, t * D:(t + 1) * D], split[:, 4 * a + g, tok:tok + P],
                                                wo[wp][:, g, :], start=(i == 0), stop=(i == len(steps) - 1))
                last.then_inc(pair_full[m], 1)
            nc.tensor.nop().then_inc(wo_done, 1)

        def bank_view(m):
            return ab[m][:].rearrange("p (t n) -> p t n", t=HALF)

        def halves(tile, m):
            return tile[:, m * HALF:(m + 1) * HALF, :]

        def project_dve(dve, b, u):
            dve.wait_ge(aalpha_loaded, (b + 1) * 16)
            for m in range(2):
                dve.wait_ge(pair_full[m], u + 1)
                dve.wait_ge(y_stored[m], credited(y_stored[m], b * 16))
                nc.vector.tensor_tensor(halves(x2, m), bank_view(m), aalpha[:].unsqueeze(1).broadcast_to([P, HALF, D]),
                                        ALU.mult).then_inc(pair_free[m], 1)

        def project_pool(pool, b, u):
            pool.wait_ge(x1_loaded, (b + 1) * 16)
            for m in range(2):
                pool.wait_ge(pair_free[m], credited(pair_free[m], u + 1))
                nc.gpsimd.tensor_tensor(halves(x2, m), halves(x2, m), halves(x1, m), ALU.add).then_inc(x2_done[m], 1)

        def ffn_norm_act(act, b):
            for t in range(T):
                act.wait_ge(x2_done[t // HALF], credited(x2_done[t // HALF], b + 1))
                last = nc.scalar.activation(square_junk3[:, t, :], x2[:, t, :], ACT.Square, accum_out=ss3[:, t:t + 1])
            last.then_inc(square3_done, 1)

        def ffn_norm_dve(dve, b):
            dve.wait_ge(square3_done, b + 1)
            nc.vector.tensor_scalar(ms3[:], ss3[:], 1.0 / D, EPS, ALU.mult, ALU.add).then_inc(ms3_done, 1)
            dve.wait_ge(rstd3_done, b + 1)
            for t in range(T):
                last = nc.vector.tensor_scalar(xn3[:, t, :], x2[:, t, :], rstd3[:, t:t + 1], None, ALU.mult)
            last.then_inc(xn3_done, 1)

        def ffn_norm_pool(pool, b):
            pool.wait_ge(ms3_done, b + 1)
            nc.gpsimd.tensor_tensor(rstd3[:], ms3[:], minus_half[:], ALU.pow).then_inc(rstd3_done, 1)

        def ffn_bias_pool(pool, b):
            pool.wait_ge(falpha_loaded, (b + 1) * 16)
            pool.wait_ge(xn3_done, b + 1)
            nc.gpsimd.tensor_tensor(x2[:], x2[:], falpha[:, 1:2, :].broadcast_to([P, T, D]), ALU.add) \
                .then_inc(x2_biased, 1)

        def ffn_in_pe(pe, b, u):
            pe.wait_ge(xn3_done, b + 1)
            for k in range(KD):
                pe.wait_ge(pair_free[k], credited(pair_free[k], u))
                for t in range(T):
                    last = nc.tensor.transpose(ab[k][:, t * P:(t + 1) * P], xn3[:, t, k * P:(k + 1) * P], ident[:])
                last.then_inc(pair_full[k], 1)

        def ffn_in_dve(dve, b, u, qkv):
            dve.wait_ge(q_in_low, credited(q_in_low, qkv))
            for k in range(KD):
                dve.wait_ge(pair_full[k], u + 1)
                nc.vector.tensor_scalar(x_in[:, :, k, :], ab[k][:].rearrange("p (t n) -> p t n", t=T),
                                        par[:, b, FGAM + k:FGAM + k + 1], par[:, b, FBET + k:FBET + k + 1],
                                        ALU.mult, ALU.add).then_inc(pair_free[k], 1)

        def ffn_in_act(act, b, u, qkv):
            for k in range(KD):
                act.wait_ge(pair_free[k], credited(pair_free[k], u + 1))
            act.wait_ge(qkv_projected, qkv)
            nc.scalar.activation(by_token(in_part[0]), x_in[:], ACT.Copy).then_inc(f_in_high, 1)

        def ffn_in_pool(pool, b, u):
            pool.wait_ge(f_in_high, b + 1)
            nc.gpsimd.tensor_tensor(by_token(in_part[1]), x_in[:], by_token(in_part[0]).bitcast(f32),
                                    ALU.subtract).then_inc(f_in_low, 1)

        PIECES = [(what, f) for f in range(NH) for what in ("gate", "hidden")] + \
                 [("out", t, h) for t in range(T) for h in range(2)]

        def piece_pe(pe, b, u, piece):
            if piece[0] == "out":
                _, t, h = piece
                m = t // HALF
                if t == 0 and h == 0:
                    pe.wait_ge(prod_low, credited(prod_low, b * NH + NH))
                if t % HALF == 0 and h == 0:
                    pe.wait_ge(pair_free[m], credited(pair_free[m], u + 1 + NH))
                steps = [(a, wp, f) for f in range(NH) for a, wp in PARTS]
                n = len(steps) // 2
                for i, (a, wp, f) in list(enumerate(steps))[h * n:(h + 1) * n]:
                    last = nc.tensor.matmul(ab[m][:, (t % HALF) * D:(t % HALF + 1) * D], hid[a][:, f, t * P:(t + 1) * P],
                                            out_w[wp][:, f, :], start=(i == 0), stop=(i == len(steps) - 1))
                if t % HALF == HALF - 1 and h == 1:
                    last.then_inc(pair_full[m], 1)
                return
            f, n = piece[1], 0 if piece[0] == "gate" else 1
            pe.wait_ge(f_in_low, credited(f_in_low, b + 1))
            pe.wait_ge(pair_free[n], credited(pair_free[n], u + 1 + f))
            steps = [(a, m, k) for k in range(KD) for a, m in PARTS]
            weight = hidden_w if n else gate_w
            for i, (a, m, k) in enumerate(steps):
                last = nc.tensor.matmul(ab[n][:], weight[m][:, k, f * P:(f + 1) * P], in_part[a][:, k, :],
                                        start=(i == 0), stop=(i == len(steps) - 1))
            last.then_inc(pair_full[n], 1)
            if piece == ("hidden", NH - 1):
                nc.tensor.nop().then_inc(ffn_projected, 1)

        def piece_act(act, b, u, piece):
            if piece[0] == "gate":
                f = piece[1]
                if f == 0:
                    act.wait_ge(y_done, credited(y_done, 2 * b))
                act.wait_ge(pair_full[0], u + 1 + (f + 1))
                act.wait_ge(pair_free[1], credited(pair_free[1], u + 1 + f))
                nc.scalar.activation(scratch[0][:], ab[0][:], ACT.Tanh, scale=0.5).then_inc(tanh_done, 1)
            elif piece[0] == "hidden":
                f = piece[1]
                act.wait_ge(pair_free[1], credited(pair_free[1], u + 1 + (f + 1)))
                nc.scalar.activation(hid[0][:, f, :], scratch[1][:], ACT.Copy).then_inc(prod_high, 1)

        def piece_dve(dve, b, u, piece):
            if piece[0] == "gate":
                f = piece[1]
                dve.wait_ge(tanh_done, b * NH + (f + 1))
                nc.vector.scalar_tensor_tensor(scratch[0][:], scratch[0][:], 1.0, ab[0][:], ALU.add, ALU.mult) \
                    .then_inc(pair_free[0], 1)
            elif piece[0] == "hidden":
                f = piece[1]
                dve.wait_ge(pair_free[0], credited(pair_free[0], u + 1 + (f + 1)))
                dve.wait_ge(prod_low, credited(prod_low, b * NH + f))
                dve.wait_ge(pair_full[1], u + 1 + (f + 1))
                nc.vector.scalar_tensor_tensor(scratch[1][:], scratch[0][:], 0.5, ab[1][:], ALU.mult, ALU.mult) \
                    .then_inc(pair_free[1], 1)
            elif piece[1] % HALF == HALF - 1 and piece[2] == 1:
                m = piece[1] // HALF
                dve.wait_ge(falpha_loaded, (b + 1) * 16)
                dve.wait_ge(prod_low, credited(prod_low, b * NH + NH))
                dve.wait_ge(pair_full[m], u + 1 + NH + 1)
                nc.vector.tensor_tensor(scratch[m][:].rearrange("p (t n) -> p t n", t=HALF), bank_view(m),
                                        falpha[:, 0:1, :].broadcast_to([P, HALF, D]), ALU.mult) \
                    .then_inc(pair_free[m], 1)

        def piece_pool(pool, b, u, piece):
            if piece[0] == "hidden":
                f = piece[1]
                pool.wait_ge(prod_high, b * NH + (f + 1))
                nc.gpsimd.tensor_tensor(hid[1][:, f, :], scratch[1][:], hid[0][:, f, :].bitcast(f32), ALU.subtract) \
                    .then_inc(prod_low, 1)
            elif piece[0] == "out" and piece[1] % HALF == HALF - 1 and piece[2] == 1:
                m = piece[1] // HALF
                pool.wait_ge(x2_biased, b + 1)
                pool.wait_ge(pair_free[m], credited(pair_free[m], u + 1 + NH + 1))
                nc.gpsimd.tensor_tensor(halves(x2, m), halves(x2, m),
                                        scratch[m][:].rearrange("p (t n) -> p t n", t=HALF), ALU.add) \
                    .then_inc(y_done, 1)

        def store_act(act, b, m):
            act.wait_ge(y_done, credited(y_done, 2 * b + (m + 1)))
            act.dma_start(out[b, m * HALF * P:(m + 1) * HALF * P, :].rearrange("(t p) n -> p t n", p=P),
                          halves(x2, m)).then_inc(y_stored[m], 16)

        EARLY = 8

        PER_BATCH = USES_Q + USES_F + USES_O

        def phase2_program(eng, batch, last_ffn):
            batch(eng, 0, 0, True)
            with eng.Fori(0, B - 1) as i:
                batch(eng, i + 1, i * PER_BATCH + (USES_Q + USES_O), False)
            last_ffn(eng, B - 1, USES_Q + USES_O + (B - 1) * PER_BATCH)

        def sp_ffn_loads(sp, b):
            sp.wait_ge(y_done, credited(y_done, 2 * b))
            sp.dma_start(falpha[:], alpha_dram[b, D:3 * D].rearrange("(a n) -> a n", a=2).partition_broadcast(P)) \
                .then_inc(falpha_loaded, 16)

        def sp_batch(sp, b, u, first):
            if not first:
                sp.wait_ge(f_in_low, credited(f_in_low, b - 1))
                sp.wait_ge(q_in_low, credited(q_in_low, b))
            sp.dma_start(x_in[:], xa_dram[b].rearrange("t p k n -> p t k n")).then_inc(xa_loaded, 16)
            if not first:
                sp_ffn_loads(sp, b - 1)
                for m in range(2):
                    sp.wait_ge(x2_done[m], credited(x2_done[m], b))
            sp.dma_start(x1[:], x1_dram[b].rearrange("t p n -> p t n")).then_inc(x1_loaded, 16)
            sp.dma_start(aalpha[:], alpha_dram[b, 0:D].partition_broadcast(P)).then_inc(aalpha_loaded, 16)
            if first:
                sp.wait_ge(ones_ready, 1)
            stack_sp(sp, b, u)
            for g in range(G):
                shift_sp(sp, b, g)

        def act_batch(act, b, u, first):
            qkv_act(act, b, u, first)
            if not first:
                ffn_norm_act(act, b - 1)
                ffn_in_act(act, b - 1, u + USES_Q, b + 1)
                for n in range(EARLY):
                    piece_act(act, b - 1, u + USES_Q, PIECES[n])
            for g in range(G):
                for kt in range(T):
                    exp_act(act, b, g, kt)
                    if not first:
                        piece_act(act, b - 1, u + USES_Q, PIECES[EARLY + T * g + kt])
                    if kt == 0 and g > 0:
                        normalise_act(act, b, g - 1)
            normalise_act(act, b, G - 1)
            if not first:
                for m in range(2):
                    store_act(act, b - 1, m)

        def act_last(act, b, u):
            ffn_norm_act(act, b)
            ffn_in_act(act, b, u, B)
            for piece in PIECES:
                piece_act(act, b, u, piece)
            for m in range(2):
                store_act(act, b, m)
            for m in range(2):
                act.wait_ge(y_stored[m], credited(y_stored[m], B * 16))

        def pool_batch(pool, b, u, first):
            qkv_pool(pool, b, u, first)
            if not first:
                ffn_norm_pool(pool, b - 1)
                ffn_in_pool(pool, b - 1, u + USES_Q)
                ffn_bias_pool(pool, b - 1)
                for n in range(EARLY):
                    piece_pool(pool, b - 1, u + USES_Q, PIECES[n])
            for g in range(G):
                for kt in range(T):
                    if not first:
                        piece_pool(pool, b - 1, u + USES_Q, PIECES[EARLY + T * g + kt])
                    if kt == 0 and g > 0:
                        normalise_pool(pool, b, g - 1)
            normalise_pool(pool, b, G - 1)
            project_pool(pool, b, u + USES_Q + (0 if first else USES_F))

        def pool_last(pool, b, u):
            ffn_norm_pool(pool, b)
            ffn_in_pool(pool, b, u)
            ffn_bias_pool(pool, b)
            for piece in PIECES:
                piece_pool(pool, b, u, piece)

        def pe_batch(pe, b, u, first):
            qkv_pe(pe, b, u, first)
            if not first:
                ffn_in_pe(pe, b - 1, u + USES_Q)
            pe.wait_ge(stacked, (b + 1) * (12 * 16))
            for s in range(J * T):
                raw_score(pe, b, 0, s)
                if s % 2 == 1 and not first:
                    piece_pe(pe, b - 1, u + USES_Q, PIECES[s // 2])
            maxima_transposed(pe, b, 0)
            for m in range(2):
                pe.wait_ge(pair_free[m], credited(pair_free[m], u + USES_Q))
            for g in range(G):
                pe.wait_ge(shift_loaded, credited(shift_loaded, (b * G + (g + 1)) * 64))
                for kt in range(T):
                    for j in range(J):
                        score_pe(pe, b, g, kt, j)
                        if g + 1 < G:
                            raw_score(pe, b, g + 1, J * kt + j)
                    if kt > 0:
                        values_pe(pe, b, g, kt - 1)
                    if kt == T - 1 and g + 1 < G:
                        maxima_transposed(pe, b, g + 1)
                    if not first:
                        piece_pe(pe, b - 1, u + USES_Q, PIECES[EARLY + T * g + kt])
                values_pe(pe, b, g, T - 1)
            project_pe(pe, b, u + USES_Q + (0 if first else USES_F))

        def pe_last(pe, b, u):
            ffn_in_pe(pe, b, u)
            for piece in PIECES:
                piece_pe(pe, b, u, piece)

        def dve_batch(dve, b, u, first):
            if first:
                dve.wait_ge(ones_ready, 1)
            qkv_dve(dve, b, u, first)
            if not first:
                ffn_norm_dve(dve, b - 1)
                ffn_in_dve(dve, b - 1, u + USES_Q, b + 1)
            for s in range(0, J * T, 2):
                maxima_dve(dve, b, 0, s, 2)
                if not first:
                    piece_dve(dve, b - 1, u + USES_Q, PIECES[s // 2])
            shift_dve(dve, b, 0)
            for g in range(G):
                for kt in range(T):
                    if g + 1 < G:
                        maxima_dve(dve, b, g + 1, J * kt, J)
                        if kt == T - 1:
                            shift_dve(dve, b, g + 1)
                    if not first:
                        piece_dve(dve, b - 1, u + USES_Q, PIECES[EARLY + T * g + kt])
                normalise_dve(dve, b, g)
            project_dve(dve, b, u + USES_Q + (0 if first else USES_F))

        def dve_last(dve, b, u):
            ffn_norm_dve(dve, b)
            ffn_in_dve(dve, b, u, B)
            for piece in PIECES:
                piece_dve(dve, b, u, piece)

        with nc.Block() as block:
            @block.sync
            def _(sp):
                phase2_program(sp, sp_batch, lambda sp, b, u: sp_ffn_loads(sp, b))

            @block.scalar
            def _(act):
                phase2_program(act, act_batch, act_last)

            @block.gpsimd
            def _(pool):
                nc.gpsimd.memset(v_ext[:], 0.0).then_inc(vext_zeroed, 1)
                pool.wait_ge(vext_zeroed, 1)
                nc.gpsimd.memset(v_ext[:, :, :, HD:HD + 1], 1.0)
                nc.gpsimd.memset(k_stack[:].bitcast(f32), 1.0).then_inc(ones_ready, 1)
                phase2_program(pool, pool_batch, pool_last)

            @block.tensor
            def _(pe):
                phase2_program(pe, pe_batch, pe_last)

            @block.vector
            def _(dve):
                phase2_program(dve, dve_batch, dve_last)


def kernel(x, cond_256, L0_cond_norm_w, L0_cond_up_w, L0_cond_down_w, L1_cond_attn_gamma_w, L1_cond_attn_beta_w,
           L1_cond_W_q, L1_cond_W_k, L1_cond_W_v, L1_cond_W_o, L1_cond_attn_alpha_w, L1_cond_ffn_gamma_w,
           L1_cond_ffn_beta_w, L1_cond_gate_w, L1_cond_hidden_w, L1_cond_out_w, L1_cond_out_b,
           L1_cond_ffn_alpha_w):
    import numpy as np
    import concourse.bacc as bacc
    from concourse.bass_utils import run_bass_kernel_spmd

    x = np.asarray(x)
    batches, tokens, width = x.shape

    def t(w):
        return np.ascontiguousarray(np.asarray(w).T)

    def by_slots(w):
        w = np.asarray(w).reshape(4, 2, 2, 16, width)
        return t(w.transpose(1, 2, 3, 0, 4).reshape(width, width))

    xT = np.ascontiguousarray(x.reshape(batches * tokens // 128, 128, width // 128, 128).transpose(0, 3, 2, 1))
    arrays = {
        "x_tok": np.ascontiguousarray(x), "xT": xT, "condT": t(cond_256), "norm_wT": t(L0_cond_norm_w),
        "up_wT": t(L0_cond_up_w), "down_wT": t(L0_cond_down_w), "agam_wT": t(L1_cond_attn_gamma_w),
        "abet_wT": t(L1_cond_attn_beta_w), "wqT": by_slots(L1_cond_W_q), "wkT": by_slots(L1_cond_W_k),
        "wvT": t(L1_cond_W_v), "woT": t(L1_cond_W_o), "aalpha_wT": t(L1_cond_attn_alpha_w),
        "fgam_wT": t(L1_cond_ffn_gamma_w), "fbet_wT": t(L1_cond_ffn_beta_w), "gate_wT": t(L1_cond_gate_w),
        "hidden_wT": t(L1_cond_hidden_w), "out_wT": t(L1_cond_out_w), "out_b": np.asarray(L1_cond_out_b),
        "falpha_wT": t(L1_cond_ffn_alpha_w),
    }
    nc = bacc.Bacc("TRN2", target_bir_lowering=False, num_devices=1)
    args = [nc.dram_tensor(name, a.shape, mybir.dt.from_np(a.dtype), kind="ExternalInput").ap()
            for name, a in arrays.items()]
    out = nc.dram_tensor("out", x.shape, mybir.dt.float32, kind="ExternalOutput").ap()
    cond_seq_kernel(nc, *args, out)
    r = run_bass_kernel_spmd(nc, [arrays], core_ids=[0])
    return r.results[0]["out"]
```

```python
import concourse.bass as bass
from concourse import mybir
from contextlib import ExitStack


def cond_seq_kernel(nc, x_tok, xT, condT, norm_wT, up_wT, down_wT, agam_wT, abet_wT, wqT, wkT, wvT, woT,
                    aalpha_wT, fgam_wT, fbet_wT, gate_wT, hidden_wT, out_wT, out_b, falpha_wT, out):
    f32 = mybir.dt.float32
    f32r = mybir.dt.float32r
    bf16 = mybir.dt.bfloat16
    ALU = mybir.AluOpType
    ACT = mybir.ActivationFunctionType
    AX = mybir.AxisListType

    P = 128
    B = condT.shape[1]
    C = condT.shape[0]
    D = norm_wT.shape[1]
    KD = D // P
    S = xT.shape[0] * P // B
    T = S // P
    FF = down_wT.shape[0]
    KF = FF // P
    NH = gate_wT.shape[1] // P
    HD = 16
    G = 4
    J = 4
    W = 512
    EPS = 1e-6
    ROUND = 1.5 * 2.0 ** 23
    QMAX = 127.0
    PARTS = ((0, 0), (0, 1), (1, 0))
    ROWS = 3 * HD
    SROWS = ROWS + 2

    ctx = ExitStack()
    with ctx:
        def sb(stack, name, shape, dt=f32):
            return stack.enter_context(nc.sbuf_tensor(name, shape, dt))

        def sem(name):
            return ctx.enter_context(nc.semaphore(name))

        def dram(name, shape):
            return nc.dram_tensor(name, shape, f32, kind="Internal").ap()

        x1_dram = dram("x1_spill", (B, T, P, D))
        xa_dram = dram("xa_spill", (B, T, P, KD, P))
        alpha_dram = dram("alpha_spill", (B, 3 * D))

        psum = [ctx.enter_context(nc.psum_tensor(f"bank{i}", [P, W], f32)) for i in range(8)]

        par = sb(ctx, "par", [P, B, 5 * KD])
        SCALE0, AGAM, ABET, FGAM, FBET = (KD * n for n in range(5))
        ident = sb(ctx, "ident", [P, P])
        identb = sb(ctx, "identb", [P, P], bf16)
        minus_half = sb(ctx, "minus_half", [P, T])
        wdeq = sb(ctx, "wdeq", [P, 1])
        gate_w = [sb(ctx, f"gate_w{i}", [P, KD, NH * P], f32r) for i in range(2)]
        hidden_w = [sb(ctx, f"hidden_w{i}", [P, KD, NH * P], f32r) for i in range(2)]
        out_w = [sb(ctx, f"out_w{i}", [P, NH, D], f32r) for i in range(2)]
        wq = [sb(ctx, f"wq{i}", [P, KD, D], f32r) for i in range(2)]
        wk = [sb(ctx, f"wk{i}", [P, KD, D], f32r) for i in range(2)]
        wv = [sb(ctx, f"wv{i}", [P, KD, D], f32r) for i in range(2)]
        wo = [sb(ctx, f"wo{i}", [P, G, D], f32r) for i in range(2)]

        phase1 = ExitStack()
        up_w = [sb(phase1, f"up_w{i}", [P, KD, 2 * FF], f32r) for i in range(2)]
        down_q = sb(phase1, "down_q", [P, KF, D], bf16)
        stage_stack = ExitStack()
        up_st = sb(stage_stack, "up_st", [P, KD, 2 * FF])
        down_st = sb(stage_stack, "down_st", [P, KF, D])
        gate_st = sb(stage_stack, "gate_st", [P, KD, NH * P])
        hidden_st = sb(stage_stack, "hidden_st", [P, KD, NH * P])
        out_st = sb(stage_stack, "out_st", [P, NH, D])
        q_st = sb(stage_stack, "q_st", [P, KD, D])
        k_st = sb(stage_stack, "k_st", [P, KD, D])
        v_st = sb(stage_stack, "v_st", [P, KD, D])
        o_st = sb(stage_stack, "o_st", [P, G, D])
        cond_sb = sb(stage_stack, "cond_sb", [C, B])
        vec_w = sb(stage_stack, "vec_w", [C, 7, D])
        outb_sb = sb(stage_stack, "outb_sb", [B, D])
        alpha_sb = sb(stage_stack, "alpha_sb", [B, 3, D])
        ones = sb(stage_stack, "ones", [P, P])
        absum = sb(stage_stack, "absum", [P, 1])
        mean = sb(stage_stack, "mean", [P, 1])
        wscale = sb(stage_stack, "wscale", [P, 1])

        small_loaded = sem("small_loaded")
        down_loaded = sem("down_loaded")
        weight_loaded = [sem(f"weight_loaded{i}") for i in range(8)]
        ostage_zeroed = sem("ostage_zeroed")
        consts_ready = sem("consts_ready")
        high_done = sem("high_done")
        vectors_done = sem("vectors_done")
        alpha_done = sem("alpha_done")
        alpha_stored = sem("alpha_stored")
        down_steps = sem("down_steps")
        mean_summed = sem("mean_summed")

        pairs = [(up_st, up_w, up_wT), (q_st, wq, wqT), (k_st, wk, wkT), (v_st, wv, wvT), (o_st, wo, woT),
                 (gate_st, gate_w, gate_wT), (hidden_st, hidden_w, hidden_wT), (out_st, out_w, out_wT)]

        xt_loaded = [sem(f"xt_loaded{t}") for t in range(T)]
        xk_loaded = [sem(f"xk_loaded{s}") for s in range(2)]
        scale_ready = sem("scale_ready")
        x_scaled = sem("x_scaled")
        x_high = sem("x_high")
        x_split = sem("x_split")
        square_done = sem("square_done")
        ms_done = sem("ms_done")
        rstd_done = sem("rstd_done")
        up_gate_done = sem("up_gate_done")
        up_val_done = sem("up_val_done")
        up_done = sem("up_done")
        gelu_done = sem("gelu_done")
        h_done = sem("h_done")
        scale_steps = sem("scale_steps")
        dequant_done = sem("dequant_done")
        rounded = sem("rounded")
        quantised = sem("quantised")
        q_transposed = sem("q_transposed")
        qT_copied = sem("qT_copied")
        down_done = sem("down_done")
        x1_done = sem("x1_done")
        x1_stored = [sem(f"x1_stored{t}") for t in range(T)]
        square2_done = sem("square2_done")
        ms2_done = sem("ms2_done")
        rstd2_done = sem("rstd2_done")
        xn_done = sem("xn_done")
        xn_transposed = sem("xn_transposed")
        xa_done = sem("xa_done")
        xa_stored = [sem(f"xa_stored{s}") for s in range(2)]
        CREDIT1 = {x_split: 1, x_scaled: 2, up_done: 2, gelu_done: 2, h_done: 2, quantised: 1, q_transposed: 2,
                   qT_copied: 1, down_done: 1, x1_done: 4, ms_done: 1, rstd_done: 2, ms2_done: 1,
                   rstd2_done: 1, xn_transposed: 1, xa_done: 1,
                   x1_stored[0]: 1, x1_stored[1]: 1, x1_stored[2]: 1, x1_stored[3]: 1,
                   xa_stored[0]: 1, xa_stored[1]: 1}

        vext_zeroed = sem("vext_zeroed")
        ones_ready = sem("ones_ready")
        xa_loaded = sem("xa_loaded")
        x1_loaded = [sem(f"x1_loaded{m}") for m in range(2)]
        aalpha_loaded = sem("aalpha_loaded")
        falpha_loaded = sem("falpha_loaded")
        pair_full = [sem("bank_a_full"), sem("bank_b_full")]
        pair_free = [sem("bank_a_free"), sem("bank_b_free")]
        q_in_high = sem("q_in_high")
        q_in_low = sem("q_in_low")
        f_in_high = sem("f_in_high")
        f_in_low = sem("f_in_low")
        qkv_projected = sem("qkv_projected")
        qk_high = sem("qk_high")
        stacked = [sem(f"stacked{m}") for m in range(2)]
        raw_full = sem("raw_full")
        raw_read = sem("raw_read")
        shift_high = sem("shift_high")
        shift_loaded = sem("shift_loaded")
        score_full = sem("score_full")
        exp_done = sem("exp_done")
        pv_done = sem("pv_done")
        o_read = sem("o_read")
        norm_steps = sem("norm_steps")
        on_done = sem("on_done")
        on_high = sem("on_high")
        on_low = sem("on_low")
        wo_done = sem("wo_done")
        x2_done = [sem(f"x2_done{m}") for m in range(2)]
        square3_done = sem("square3_done")
        ms3_done = sem("ms3_done")
        rstd3_done = sem("rstd3_done")
        xn3_done = sem("xn3_done")
        x2_biased = sem("x2_biased")
        tanh_done = sem("tanh_done")
        prod_high = sem("prod_high")
        prod_low = sem("prod_low")
        ffn_projected = sem("ffn_projected")
        stack_open = sem("stack_open")
        y_done = sem("y_done")
        y_stored = [sem(f"y_stored{m}") for m in range(2)]
        CREDIT2 = {pair_free[0]: 1, pair_free[1]: 1, raw_read: 2, exp_done: 1, pv_done: 2, o_read: 1, on_low: 1,
                   shift_loaded: 1, ffn_projected: 2, wo_done: 1, prod_low: 1, q_in_low: 1, f_in_low: 2,
                   x2_done[0]: 1, x2_done[1]: 1, y_done: 2, y_stored[0]: 1, y_stored[1]: 1}

        def credited(s, value):
            return value + CREDIT1.get(s, CREDIT2.get(s, 0))

        def live(tile, lag):
            return tile is None or 0 <= tile - lag < B * T

        with nc.Block() as block:
            @block.sync
            def _(sp):
                sp.dma_start(up_st[:], up_wT.rearrange("(k p) n -> p k n", p=P)).then_inc(weight_loaded[0], 16)
                sp.dma_start(down_st[:], down_wT.rearrange("(k p) n -> p k n", p=P)).then_inc(down_loaded, 16)
                for n in (1, 2, 3, 5, 6, 7):
                    dst, _, src = pairs[n]
                    sp.dma_start(dst[:], src.rearrange("(k p) n -> p k n", p=P)).then_inc(weight_loaded[n], 16)
                sp.wait_ge(ostage_zeroed, 1)
                wo_rows = woT.rearrange("(g j d) n -> j d g n", g=G, j=J)
                for j in range(J):
                    sp.dma_start(o_st[32 * j:32 * j + HD, :, :], wo_rows[j]).then_inc(weight_loaded[4], 16)
                sp.wait_ge(alpha_done, 3)
                sp.dma_start(alpha_dram, alpha_sb[:].rearrange("b a n -> b (a n)")).then_inc(alpha_stored, 16)
                sp.wait_ge(alpha_stored, 16)

            @block.scalar
            def _(act):
                act.dma_start(cond_sb[:], condT).then_inc(small_loaded, 16)
                for n, w in enumerate((norm_wT, agam_wT, abet_wT, fgam_wT, fbet_wT, aalpha_wT, falpha_wT)):
                    act.dma_start(vec_w[:, n, :], w).then_inc(small_loaded, 16)
                act.dma_start(outb_sb[:], out_b.partition_broadcast(B)).then_inc(small_loaded, 16)
                for n, (src, dst, _) in enumerate(pairs):
                    act.wait_ge(weight_loaded[n], 64 if n == 4 else 16)
                    nc.scalar.activation(dst[0][:], src[:], ACT.Copy).then_inc(high_done, 1)

            @block.gpsimd
            def _(pool):
                for s, value in list(CREDIT1.items()) + list(CREDIT2.items()):
                    nc.gpsimd.sem_inc(s, value)
                nc.gpsimd.memset(o_st[:], 0.0).then_inc(ostage_zeroed, 1)
                nc.gpsimd.memset(minus_half[:], -0.5)
                nc.gpsimd.memset(ones[:], 1.0).then_inc(consts_ready, 1)
                nc.gpsimd.memset(ident[:], 0.0).then_inc(consts_ready, 1)
                nc.gpsimd.memset(identb[:], 0.0).then_inc(consts_ready, 1)
                pool.wait_ge(consts_ready, 3)
                for m in (ident, identb):
                    nc.gpsimd.affine_select(out=m[:], in_=m[:], compare_op=ALU.not_equal, fill=1.0, base=0,
                                            pattern=[[-1, P]], channel_multiplier=1).then_inc(consts_ready, 1)

            @block.tensor
            def _(pe):
                pe.wait_ge(small_loaded, 16 * 9)
                for v in range(5):
                    for k in range(KD):
                        last = nc.tensor.matmul(psum[0][:, (v * KD + k) * B:(v * KD + k + 1) * B],
                                                vec_w[:, v, k * P:(k + 1) * P], cond_sb[:], start=True, stop=True)
                last.then_inc(vectors_done, 1)
                for v in range(2):
                    last = nc.tensor.matmul(psum[1][0:B, v * D:(v + 1) * D], cond_sb[:], vec_w[:, 5 + v, :],
                                            start=True, stop=True)
                last.then_inc(vectors_done, 1)
                pe.wait_ge(consts_ready, 5)
                pe.wait_ge(down_steps, 1)
                nc.tensor.matmul(psum[2][:, 0:1], ones[:], absum[:], start=True, stop=True).then_inc(mean_summed, 1)

            @block.vector
            def _(dve):
                dve.wait_ge(vectors_done, 1)
                vectors = psum[0][:, 0:5 * KD * B].rearrange("p (v b) -> p b v", b=B)
                nc.vector.tensor_scalar(par[:, :, 0:KD], vectors[:, :, 0:KD], 1.0, None, ALU.add)
                nc.vector.tensor_copy(par[:, :, KD:], vectors[:, :, KD:])
                dve.wait_ge(vectors_done, 2)
                dve.wait_ge(small_loaded, 16 * 9)
                nc.vector.tensor_copy(alpha_sb[:, 0:2, :], psum[1][0:B, :].rearrange("b (a n) -> b a n", a=2)) \
                    .then_inc(alpha_done, 1)
                dve.wait_ge(alpha_done, 1)
                nc.vector.tensor_tensor(alpha_sb[:, 2, :], alpha_sb[:, 1, :], outb_sb[:], ALU.mult) \
                    .then_inc(alpha_done, 2)
                dve.wait_ge(down_loaded, 16)
                nc.vector.tensor_reduce(absum[:], down_st[:], AX.XY, ALU.add, apply_absolute_value=True) \
                    .then_inc(down_steps, 1)
                dve.wait_ge(mean_summed, 1)
                nc.vector.tensor_scalar(mean[:], psum[2][:, 0:1], 1.0 / (FF * D), 1e-5, ALU.mult, ALU.max) \
                    .then_inc(down_steps, 1)
                dve.wait_ge(down_steps, 2)
                nc.vector.tensor_scalar(wdeq[:], mean[:], 1.0 / QMAX, None, ALU.mult)
                nc.vector.reciprocal(wscale[:], mean[:]).then_inc(down_steps, 1)
                dve.wait_ge(down_steps, 3)
                nc.vector.tensor_scalar(down_st[:], down_st[:], wscale[:], 1.0, ALU.mult, ALU.min) \
                    .then_inc(down_steps, 1)
                dve.wait_ge(down_steps, 4)
                nc.vector.tensor_scalar(down_st[:], down_st[:], -1.0, ROUND, ALU.max, ALU.add) \
                    .then_inc(down_steps, 1)
                dve.wait_ge(down_steps, 5)
                nc.vector.tensor_scalar(down_q[:], down_st[:], ROUND, None, ALU.subtract)
                for n, (src, dst, _) in enumerate(pairs):
                    dve.wait_ge(high_done, n + 1)
                    nc.vector.tensor_tensor(dst[1][:], src[:], dst[0][:].bitcast(f32), ALU.subtract)
        stage_stack.close()

        xt = sb(phase1, "xt", [P, T, D])
        xk = sb(phase1, "xk", [P, 2, KD, P])
        cur_scale = sb(phase1, "cur_scale", [P, KD])
        xs = sb(phase1, "xs", [P, KD, P])
        xs_part = [sb(phase1, f"xs_part{i}", [P, 2, KD, P], f32r) for i in range(2)]
        square_junk = sb(phase1, "square_junk", [P, D])
        ss = sb(phase1, "ss", [P, 1])
        ms = sb(phase1, "ms", [P, 1])
        rstd = sb(phase1, "rstd", [P, 2])
        gelu = sb(phase1, "gelu", [P, 2, W])
        h = sb(phase1, "h", [P, FF])
        amax = sb(phase1, "amax", [P, 4])
        dequant = sb(phase1, "dequant", [P, 2])
        h_rounded = sb(phase1, "h_rounded", [P, FF])
        h_q = sb(phase1, "h_q", [P, 2, FF], bf16)
        qT = sb(phase1, "qT", [P, FF], bf16)
        x1t = sb(phase1, "x1t", [P, T, D])
        square_junk2 = sb(phase1, "square_junk2", [P, D])
        ss2 = sb(phase1, "ss2", [P, 1])
        ms2 = sb(phase1, "ms2", [P, 1])
        rstd2 = sb(phase1, "rstd2", [P, 1])
        xn = sb(phase1, "xn", [P, D])
        xa = sb(phase1, "xa", [P, 2, KD, P])
        gate_bank = psum[0:2]
        val_bank = psum[2:4]
        tr_bank = psum[4][:].bitcast(bf16)
        down_bank = psum[5]
        xn_bank = psum[6]

        UP, DOWN, NORM, STORE = 1, 2, 3, 4

        def back(b, t, lag):
            return b + (t - lag) // T, (t - lag) % T, b * T + (t - lag)

        def load_tile(sp, b, t, tile):
            if live(tile, 0):
                b, t, n = back(b, t, 0)
                sp.wait_ge(x1_done, credited(x1_done, n - 3))
                sp.dma_start(xt[:, t, :], x_tok[b, t * P:(t + 1) * P, :]).then_inc(xt_loaded[t], 16)
                sp.wait_ge(x_scaled, credited(x_scaled, n - 1))
                sp.dma_start(xk[:, t % 2, :, :], xT[n, :, :, :]).then_inc(xk_loaded[t % 2], 16)

        def act_tile(act, b0, t0, tile):
            if live(tile, 0):
                b, t, n = back(b0, t0, 0)
                act.wait_ge(scale_ready, b + 1)
                act.wait_ge(xk_loaded[t % 2], (b * 2 + t // 2 + 1) * 16)
                act.wait_ge(x_split, credited(x_split, n))
                for k in range(KD):
                    last = nc.scalar.activation(xs[:, k, :], xk[:, t % 2, k, :], ACT.Copy,
                                                scale=cur_scale[:, k:k + 1])
                last.then_inc(x_scaled, 1)
                act.wait_ge(xt_loaded[t], (b + 1) * 16)
                act.wait_ge(ms_done, credited(ms_done, n))
                nc.scalar.activation(square_junk[:], xt[:, t, :], ACT.Square, accum_out=ss[:]) \
                    .then_inc(square_done, 1)
            if live(tile, NORM):
                b, t, m = back(b0, t0, NORM)
                act.wait_ge(x1_done, credited(x1_done, m + 1))
                act.wait_ge(ms2_done, credited(ms2_done, m))
                act.dma_start(x1_dram[b, t, :, :], x1t[:, t, :]).then_inc(x1_stored[t], 16)
                nc.scalar.activation(square_junk2[:], x1t[:, t, :], ACT.Square, accum_out=ss2[:]) \
                    .then_inc(square2_done, 1)
            if live(tile, STORE):
                b, t, m = back(b0, t0, STORE)
                act.wait_ge(xa_done, credited(xa_done, m + 1))
                act.dma_start(xa_dram[b, t, :, :, :], xa[:, t % 2, :, :]).then_inc(xa_stored[t % 2], 16)

            def act_gelu(j):
                b, t, n = back(b0, t0, UP)
                act.wait_ge(up_gate_done, 2 * n + j + 1)
                act.wait_ge(rstd_done, credited(rstd_done, n + 1))
                act.wait_ge(h_done, credited(h_done, 2 * n + j - 1))
                nc.scalar.activation(gelu[:, j, :], gate_bank[j][:], ACT.Gelu, scale=rstd[:, t % 2:t % 2 + 1]) \
                    .then_inc(gelu_done, 1)
            if live(tile, UP):
                act_gelu(0)
            if live(tile, DOWN):
                b, t, m = back(b0, t0, DOWN)
                act.wait_ge(q_transposed, credited(q_transposed, m + 1))
                act.wait_ge(down_done, credited(down_done, m))
                nc.scalar.activation(qT[:], tr_bank[:, 0:FF], ACT.Copy).then_inc(qT_copied, 1)
            if live(tile, UP):
                act_gelu(1)

        def pool_tile(pool, b0, t0, tile):
            if live(tile, 0):
                b, t, n = back(b0, t0, 0)
                pool.wait_ge(up_done, credited(up_done, n - 1))
                pool.wait_ge(x_high, n + 1)
                nc.gpsimd.tensor_tensor(xs_part[1][:, t % 2, :, :], xs[:], xs_part[0][:, t % 2, :, :].bitcast(f32),
                                        ALU.subtract).then_inc(x_split, 1)
                pool.wait_ge(gelu_done, credited(gelu_done, 2 * n - 2))
                pool.wait_ge(h_done, credited(h_done, 2 * n - 2))
                pool.wait_ge(ms_done, credited(ms_done, n + 1))
                nc.gpsimd.tensor_tensor(rstd[:, t % 2:t % 2 + 1], ms[:], minus_half[:, 0:1], ALU.pow) \
                    .then_inc(rstd_done, 1)
            if live(tile, NORM):
                b, t, m = back(b0, t0, NORM)
                if tile is None or m > 0:
                    pool.wait_ge(xn_done, m)
                pool.wait_ge(ms2_done, credited(ms2_done, m + 1))
                nc.gpsimd.tensor_tensor(rstd2[:], ms2[:], minus_half[:, 0:1], ALU.pow).then_inc(rstd2_done, 1)

        def pe_tile(pe, b0, t0, tile):
            def up(j):
                b, t, n = back(b0, t0, UP)
                for bank, col, free, full in ((gate_bank[j], FF + j * W, gelu_done, up_gate_done),
                                              (val_bank[j], j * W, h_done, up_val_done)):
                    pe.wait_ge(free, credited(free, 2 * n + j - 1))
                    steps = [(a, m, k) for k in range(KD) for a, m in PARTS]
                    for i, (a, m, k) in enumerate(steps):
                        last = nc.tensor.matmul(bank[:], xs_part[a][:, t % 2, k, :], up_w[m][:, k, col:col + W],
                                                start=(i == 0), stop=(i == len(steps) - 1))
                    last.then_inc(full, 1)
            if live(tile, UP):
                pe.wait_ge(x_split, credited(x_split, back(b0, t0, UP)[2] + 1))
                up(0)
            if live(tile, DOWN):
                b, t, m = back(b0, t0, DOWN)
                pe.wait_ge(quantised, credited(quantised, m + 1))
                pe.wait_ge(qT_copied, credited(qT_copied, m))
                for k in range(KF):
                    last = nc.tensor.transpose(tr_bank[:, k * P:(k + 1) * P], h_q[:, t % 2, k * P:(k + 1) * P],
                                               identb[:])
                last.then_inc(q_transposed, 1)
            if live(tile, UP):
                up(1)
                nc.tensor.nop().then_inc(up_done, 1)
            if live(tile, DOWN):
                b, t, m = back(b0, t0, DOWN)
                pe.wait_ge(qT_copied, credited(qT_copied, m + 1))
                pe.wait_ge(x1_done, credited(x1_done, m))
                for k in range(KF):
                    last = nc.tensor.matmul(down_bank[:, 0:D], qT[:, k * P:(k + 1) * P], down_q[:, k, :],
                                            start=(k == 0), stop=(k == KF - 1))
                last.then_inc(down_done, 1)
            if live(tile, NORM):
                b, t, m = back(b0, t0, NORM)
                pe.wait_ge(xn_done, m + 1)
                pe.wait_ge(xa_done, credited(xa_done, m))
                for k in range(KD):
                    last = nc.tensor.transpose(xn_bank[:, k * P:(k + 1) * P], xn[:, k * P:(k + 1) * P], ident[:])
                last.then_inc(xn_transposed, 1)

        def dve_tile(dve, b0, t0, tile):
            if live(tile, 0):
                b, t, n = back(b0, t0, 0)
                if t == 0:
                    dve.wait_ge(x_scaled, credited(x_scaled, n))
                    nc.vector.tensor_scalar(cur_scale[:], par[:, b, SCALE0:SCALE0 + KD], 1.0, None, ALU.mult) \
                        .then_inc(scale_ready, 1)
                dve.wait_ge(x_scaled, credited(x_scaled, n + 1))
                dve.wait_ge(up_done, credited(up_done, n - 1))
                nc.vector.tensor_copy(xs_part[0][:, t % 2, :, :], xs[:]).then_inc(x_high, 1)
                dve.wait_ge(square_done, n + 1)
                dve.wait_ge(rstd_done, credited(rstd_done, n))
                nc.vector.tensor_scalar(ms[:], ss[:], 1.0 / D, EPS, ALU.mult, ALU.add).then_inc(ms_done, 1)
            if live(tile, NORM):
                b, t, m = back(b0, t0, NORM)
                dve.wait_ge(square2_done, m + 1)
                dve.wait_ge(rstd2_done, credited(rstd2_done, m))
                nc.vector.tensor_scalar(ms2[:], ss2[:], 1.0 / D, EPS, ALU.mult, ALU.add).then_inc(ms2_done, 1)

            def gate(j):
                b, t, n = back(b0, t0, UP)
                dve.wait_ge(up_val_done, 2 * n + j + 1)
                dve.wait_ge(gelu_done, credited(gelu_done, 2 * n + j + 1))
                nc.vector.scalar_tensor_tensor(h[:, j * W:(j + 1) * W], val_bank[j][:],
                                               rstd[:, t % 2:t % 2 + 1], gelu[:, j, :], ALU.mult, ALU.mult) \
                    .then_inc(h_done, 1)
            if live(tile, UP):
                gate(0)
            if live(tile, NORM):
                b, t, m = back(b0, t0, NORM)
                dve.wait_ge(rstd2_done, credited(rstd2_done, m + 1))
                dve.wait_ge(xn_transposed, credited(xn_transposed, m))
                nc.vector.tensor_scalar(xn[:], x1t[:, t, :], rstd2[:], None, ALU.mult).then_inc(xn_done, 1)
            if live(tile, UP):
                b, t, n = back(b0, t0, UP)
                gate(1)
                dve.wait_ge(h_done, credited(h_done, 2 * n + 2))
                nc.vector.tensor_reduce(amax[:, 0:1], h[:], AX.X, ALU.max, apply_absolute_value=True) \
                    .then_inc(scale_steps, 1)
                dve.wait_ge(scale_steps, 4 * n + 1)
                nc.vector.tensor_scalar(amax[:, 1:2], amax[:, 0:1], 1e-5, None, ALU.max).then_inc(scale_steps, 1)
                dve.wait_ge(scale_steps, 4 * n + 2)
                nc.vector.reciprocal(amax[:, 2:3], amax[:, 1:2]).then_inc(scale_steps, 1)
                nc.vector.tensor_tensor(dequant[:, t % 2:t % 2 + 1], amax[:, 1:2], wdeq[:], ALU.mult) \
                    .then_inc(dequant_done, 1)
                dve.wait_ge(scale_steps, 4 * n + 3)
                nc.vector.tensor_scalar(amax[:, 3:4], amax[:, 2:3], QMAX, None, ALU.mult).then_inc(scale_steps, 1)
                dve.wait_ge(scale_steps, 4 * n + 4)
                nc.vector.tensor_scalar(h_rounded[:], h[:], amax[:, 3:4], ROUND, ALU.mult, ALU.add) \
                    .then_inc(rounded, 1)
                dve.wait_ge(rounded, n + 1)
                dve.wait_ge(q_transposed, credited(q_transposed, n - 1))
                nc.vector.tensor_scalar(h_q[:, t % 2, :], h_rounded[:], ROUND, QMAX, ALU.subtract, ALU.min) \
                    .then_inc(quantised, 1)
            if live(tile, DOWN):
                b, t, m = back(b0, t0, DOWN)
                dve.wait_ge(down_done, credited(down_done, m + 1))
                dve.wait_ge(dequant_done, m + 1)
                if tile is None or m >= T:
                    dve.wait_ge(x1_stored[t], credited(x1_stored[t], b * 16))
                nc.vector.scalar_tensor_tensor(x1t[:, t, :], down_bank[:, 0:D], dequant[:, t % 2:t % 2 + 1],
                                               xt[:, t, :], ALU.mult, ALU.add).then_inc(x1_done, 1)
            if live(tile, NORM):
                b, t, m = back(b0, t0, NORM)
                dve.wait_ge(xn_transposed, credited(xn_transposed, m + 1))
                if tile is None or m >= 2:
                    dve.wait_ge(xa_stored[t % 2], credited(xa_stored[t % 2], (b * 2 + t // 2) * 16))
                for k in range(KD):
                    last = nc.vector.tensor_scalar(xa[:, t % 2, k, :], xn_bank[:, k * P:(k + 1) * P],
                                                   par[:, b, AGAM + k:AGAM + k + 1],
                                                   par[:, b, ABET + k:ABET + k + 1], ALU.mult, ALU.add)
                last.then_inc(xa_done, 1)

        def phase1_program(eng, tile_step):
            for t in range(T):
                tile_step(eng, 0, t, t)
            with eng.Fori(1, B) as b:
                for t in range(T):
                    tile_step(eng, b, t, None)
            for t in range(STORE):
                tile_step(eng, B, t, B * T + t)

        with nc.Block() as block:
            @block.sync
            def _(sp):
                phase1_program(sp, load_tile)

            @block.scalar
            def _(act):
                phase1_program(act, act_tile)
                for t in range(T):
                    act.wait_ge(x1_stored[t], credited(x1_stored[t], B * 16))
                for s in range(2):
                    act.wait_ge(xa_stored[s], credited(xa_stored[s], B * T // 2 * 16))

            @block.gpsimd
            def _(pool):
                phase1_program(pool, pool_tile)

            @block.tensor
            def _(pe):
                phase1_program(pe, pe_tile)

            @block.vector
            def _(dve):
                phase1_program(dve, dve_tile)
        phase1.close()

        q_stack = sb(ctx, "q_stack", [P, 2 * G, S], f32r)
        k_stack = sb(ctx, "k_stack", [P, 2 * G, S], f32r)
        v_ext = sb(ctx, "v_ext", [P, T, G * J, HD + 1])
        probs = sb(ctx, "probs", [P, 2 * J, S])
        aalpha = sb(ctx, "aalpha", [P, D])
        falpha = sb(ctx, "falpha", [P, 2, D])
        x_in = sb(ctx, "x_in", [P, T, KD, P])
        xa_part = [sb(ctx, f"xa_part{i}", [P, KD, S], f32r) for i in range(2)]
        xf_part = [sb(ctx, f"xf_part{i}", [P, KD, S], f32r) for i in range(2)]
        split = sb(ctx, "split", [P, 8, S], f32r)
        x2 = sb(ctx, "x2", [P, T, D])
        rowmax = sb(ctx, "rowmax", [P, J * T])
        shift = [sb(ctx, f"shift{i}", [J * T, P], f32r) for i in range(2)]
        o_sb = sb(ctx, "o_sb", [P, S])
        o_tok = sb(ctx, "o_tok", [P, S])
        inv_sum = sb(ctx, "inv_sum", [P, S // 32, 1])
        ss3 = sb(ctx, "ss3", [P, T])
        ms3 = sb(ctx, "ms3", [P, T])
        rstd3 = sb(ctx, "rstd3", [P, T])
        scratch = [sb(ctx, f"scratch{i}", [P, W]) for i in range(2)]
        hid = [sb(ctx, f"hid{i}", [P, NH, S], f32r) for i in range(2)]
        xn3 = x_in[:].rearrange("p t k n -> p t (k n)")
        score_bank = psum[0:3]
        raw_bank = psum[3:5]
        o_bank = psum[5]
        ab = psum[6:8]
        SOFTMAX_SCALE = HD ** -0.5
        HALF = T // 2
        RAW = J * T + 1
        STACK = 12 * 16
        RESERVED = NH - 2

        def staging(m, w):
            if m == 0:
                return split[:, 2 + w, :], split[:, 6 + w, :]
            return hid[0][:, RESERVED + w, :], hid[1][:, RESERVED + w, :]

        def xa_split_act(act, c, first=False):
            act.wait_ge(xa_loaded, (c + 1) * 16)
            if not first:
                act.wait_ge(qkv_projected, c)
            nc.scalar.activation(xa_part[0][:].rearrange("p k (t n) -> p t k n", t=T), x_in[:], ACT.Copy) \
                .then_inc(q_in_high, 1)

        def xa_split_pool(pool, c):
            pool.wait_ge(q_in_high, c + 1)
            nc.gpsimd.tensor_tensor(xa_part[1][:].rearrange("p k (t n) -> p t k n", t=T), x_in[:],
                                    xa_part[0][:].rearrange("p k (t n) -> p t k n", t=T).bitcast(f32),
                                    ALU.subtract).then_inc(q_in_low, 1)

        PROJECTION = [(a, m, k) for k in range(KD) for a, m in PARTS]

        def qk_pe(pe, c, m, w, use, h):
            if h == 0:
                pe.wait_ge(q_in_low, credited(q_in_low, c + 1))
                pe.wait_ge(pair_free[w], credited(pair_free[w], use))
            weight = (wq, wk)[w]
            for i in (range(3) if h == 0 else range(3, 6)):
                a, wp, k = PROJECTION[i]
                last = nc.tensor.matmul(ab[w][:], weight[wp][:, k, m * P:(m + 1) * P], xa_part[a][:, k, :],
                                        start=(i == 0), stop=(i == 5))
            if h == 1:
                last.then_inc(pair_full[w], 1)

        def qk_act(act, m, w, use):
            act.wait_ge(pair_full[w], use + 1)
            nc.scalar.activation(staging(m, w)[0], ab[w][:], ACT.Copy, scale=SOFTMAX_SCALE if w == 0 else 1.0) \
                .then_inc(qk_high, 1)

        def qk_dve(dve, m, w, n):
            dve.wait_ge(qk_high, n + w + 1)
            high, low = staging(m, w)
            nc.vector.scalar_tensor_tensor(low, ab[w][:], SOFTMAX_SCALE if w == 0 else 1.0, high.bitcast(f32),
                                           ALU.mult, ALU.subtract).then_inc(pair_free[w], 1)

        def stack_sp(sp, m, use=None):
            for w, stack, parts in ((0, q_stack, (0, 0, 1)), (1, k_stack, (0, 1, 0))):
                if use is not None:
                    sp.wait_ge(pair_free[w], credited(pair_free[w], use + 1))
                for half in range(2):
                    for r, part in enumerate(parts):
                        sp.dma_start(stack[64 * half + HD * r:64 * half + HD * (r + 1), G * m:G * m + G, :].bitcast(f32),
                                     staging(m, w)[part][64 * half:64 * half + 64, :].bitcast(f32)) \
                            .then_inc(stacked[m], 16)

        def v_pe(pe, c, m, use, h):
            if h == 0:
                pe.wait_ge(q_in_low, credited(q_in_low, c + 1))
                pe.wait_ge(pair_free[m], credited(pair_free[m], use))
            tok = (m * HALF + h) * P
            for i, (a, wp, k) in enumerate(PROJECTION):
                last = nc.tensor.matmul(ab[m][:, h * D:(h + 1) * D], xa_part[a][:, k, tok:tok + P],
                                        wv[wp][:, k, :], start=(i == 0), stop=(i == 5))
            if h == 1:
                last.then_inc(pair_full[m], 1)

        def v_dve(dve, c, m, use):
            dve.wait_ge(pv_done, credited(pv_done, c * 16))
            dve.wait_ge(pair_full[m], use + 1)
            nc.vector.tensor_scalar(v_ext[:, m * HALF:(m + 1) * HALF, :, 0:HD],
                                    ab[m][:].rearrange("p (t h d) -> p t h d", t=HALF, d=HD), 1.0, None, ALU.mult) \
                .then_inc(pair_free[m], 1)

        def raw_score(pe, b, g, s):
            j, qt = s // T, s % T
            half, slot = j % 2, 2 * g + j // 2
            idx = RAW * g + s
            if s == 0 and g % 2 == 0:
                pe.wait_ge(stacked[g // 2], (b + 1) * STACK)
            pe.wait_ge(raw_read, credited(raw_read, b * (RAW * G) + (idx - 1)))
            rows = slice(64 * half, 64 * half + ROWS)
            nc.tensor.matmul(raw_bank[idx % 2][:], q_stack[rows, slot, qt * P:(qt + 1) * P], k_stack[rows, slot, :],
                             start=True, stop=True).then_inc(raw_full, 1)

        def maxima_transposed(pe, b, g):
            idx = RAW * g + J * T
            pe.wait_ge(raw_read, credited(raw_read, b * (RAW * G) + idx))
            nc.tensor.transpose(raw_bank[idx % 2][0:J * T, 0:P], rowmax[:], ident[:]).then_inc(raw_full, 1)

        def maximum_dve(dve, b, g, s):
            j, qt = s // T, s % T
            idx = RAW * g + s
            col = (j % 2) * 8 + (j // 2) * T + qt
            dve.wait_ge(raw_full, b * (RAW * G) + (idx + 1))
            nc.vector.reduce_max(rowmax[:, col:col + 1], raw_bank[idx % 2][:], AX.X).then_inc(raw_read, 1)

        def shift_dve(dve, b, g):
            idx = RAW * g + J * T
            dve.wait_ge(raw_full, b * (RAW * G) + (idx + 1))
            dve.wait_ge(shift_loaded, credited(shift_loaded, (b * G + g) * 64))
            src = raw_bank[idx % 2][0:J * T, 0:P]
            nc.vector.tensor_scalar(shift[0][:], src, -1.0, None, ALU.mult).then_inc(shift_high, 1)
            dve.wait_ge(shift_high, b * G + (g + 1))
            nc.vector.scalar_tensor_tensor(shift[1][:], src, -1.0, shift[0][:].bitcast(f32), ALU.mult,
                                           ALU.subtract).then_inc(raw_read, 1)

        def shift_sp(sp, b, g):
            sp.wait_ge(raw_read, credited(raw_read, b * (RAW * G) + RAW * (g + 1)))
            for half in range(2):
                for part in range(2):
                    row = 64 * half + ROWS + part
                    sp.dma_start(q_stack[row:row + 1, 2 * g:2 * g + 2, :].bitcast(f32),
                                 shift[part][8 * half:8 * half + 8, :].bitcast(f32)).then_inc(shift_loaded, 16)

        def score_pe(pe, b, g, kt, j):
            half, slot = j % 2, 2 * g + j // 2
            c = 16 * g + J * kt + j
            pe.wait_ge(exp_done, credited(exp_done, b * 64 + (c - 2 if c >= 3 else 0)))
            rows = slice(64 * half, 64 * half + SROWS)
            nc.tensor.matmul(score_bank[c % 3][:], k_stack[rows, slot, kt * P:(kt + 1) * P], q_stack[rows, slot, :],
                             start=True, stop=True).then_inc(score_full, 1)

        def exp_act(act, b, g, kt, j):
            if j == 0:
                act.wait_ge(pv_done, credited(pv_done, b * 16 + (4 * g + kt - 1)))
            c = 16 * g + J * kt + j
            act.wait_ge(score_full, b * 64 + (c + 1))
            nc.scalar.activation(probs[:, (kt % 2) * J + j, :], score_bank[c % 3][:], ACT.Exp).then_inc(exp_done, 1)

        def values_pe(pe, b, g, kt, u=None):
            if u is not None:
                for m in range(2):
                    pe.wait_ge(pair_free[m], credited(pair_free[m], u + 1))
            pe.wait_ge(exp_done, credited(exp_done, b * 64 + (16 * g + J * (kt + 1))))
            if kt == 0:
                pe.wait_ge(o_read, credited(o_read, b * G + g))
            for j in range(J):
                last = nc.tensor.matmul(o_bank[32 * j:32 * j + HD + 1, :], v_ext[:, kt, J * g + j, :],
                                        probs[:, (kt % 2) * J + j, :], start=(kt == 0), stop=(kt == T - 1))
            last.then_inc(pv_done, 1)

        def normalise_dve(dve, b, g):
            dve.wait_ge(pv_done, credited(pv_done, b * 16 + 4 * (g + 1)))
            nc.vector.transpose(o_tok[:], o_bank[:]).then_inc(o_read, 1)
            blocks = o_tok[:].rearrange("p (q d) -> p q d", d=32)
            dve.wait_ge(o_read, credited(o_read, b * G + (g + 1)))
            nc.vector.reciprocal(inv_sum[:], blocks[:, :, HD:HD + 1]).then_inc(norm_steps, 1)
            dve.wait_ge(norm_steps, b * (2 * G) + (2 * g + 1))
            nc.vector.tensor_tensor(blocks, blocks, inv_sum[:].broadcast_to([P, S // 32, 32]), ALU.mult) \
                .then_inc(norm_steps, 1)
            dve.wait_ge(norm_steps, b * (2 * G) + (2 * g + 2))
            dve.wait_ge(on_low, credited(on_low, b * G + g))
            nc.vector.transpose(o_sb[:], o_tok[:]).then_inc(on_done, 1)

        def normalise_act(act, b, g, staged):
            act.wait_ge(on_done, b * G + (g + 1))
            if g == 0:
                act.wait_ge(wo_done, credited(wo_done, b))
            if g == 2:
                act.wait_ge(stacked[0], staged * STACK)
            nc.scalar.activation(split[:, g, :], o_sb[:], ACT.Copy).then_inc(on_high, 1)

        def normalise_pool(pool, b, g):
            pool.wait_ge(on_high, b * G + (g + 1))
            nc.gpsimd.tensor_tensor(split[:, 4 + g, :], o_sb[:], split[:, g, :].bitcast(f32), ALU.subtract) \
                .then_inc(on_low, 1)

        def bank_view(m):
            return ab[m][:].rearrange("p (t n) -> p t n", t=HALF)

        def halves(tile, m):
            return tile[:, m * HALF:(m + 1) * HALF, :]

        def by_tiles(tile):
            return tile[:].rearrange("p (t n) -> p t n", t=HALF)

        def wo_pe(pe, c, t, use, h):
            m = t // HALF
            if h == 0 and t == 0:
                pe.wait_ge(on_low, credited(on_low, c * G + G))
            if h == 0 and t % HALF == 0:
                pe.wait_ge(pair_free[m], credited(pair_free[m], use))
            steps = [(a, wp, g) for g in range(G) for a, wp in PARTS]
            for i in (range(6) if h == 0 else range(6, 12)):
                a, wp, g = steps[i]
                last = nc.tensor.matmul(ab[m][:, (t % HALF) * D:(t % HALF + 1) * D],
                                        split[:, 4 * a + g, t * P:(t + 1) * P], wo[wp][:, g, :],
                                        start=(i == 0), stop=(i == len(steps) - 1))
            if h == 1 and t % HALF == HALF - 1:
                last.then_inc(pair_full[m], 1)
            if h == 1 and t == T - 1:
                nc.tensor.nop().then_inc(wo_done, 1)

        def wo_dve(dve, c, m, use):
            dve.wait_ge(aalpha_loaded, (c + 1) * 16)
            dve.wait_ge(pair_full[m], use + 1)
            dve.wait_ge(y_done, credited(y_done, 2 * c))
            nc.vector.tensor_tensor(by_tiles(scratch[m]), bank_view(m),
                                    aalpha[:].unsqueeze(1).broadcast_to([P, HALF, D]), ALU.mult) \
                .then_inc(pair_free[m], 1)
            dve.wait_ge(x1_loaded[m], (c + 1) * 16)
            dve.wait_ge(pair_free[m], credited(pair_free[m], use + 1))
            nc.vector.tensor_tensor(halves(x2, m), halves(x2, m), by_tiles(scratch[m]), ALU.add) \
                .then_inc(x2_done[m], 1)

        def squares_act(act, c):
            for t in range(T):
                m = t // HALF
                act.wait_ge(x2_done[m], credited(x2_done[m], c + 1))
                last = nc.scalar.activation(scratch[m][:, (t % HALF) * D:(t % HALF + 1) * D], x2[:, t, :], ACT.Square,
                                            accum_out=ss3[:, t:t + 1])
            last.then_inc(square3_done, 1)

        def mean_dve(dve, c):
            dve.wait_ge(square3_done, c + 1)
            nc.vector.tensor_scalar(ms3[:], ss3[:], 1.0 / D, EPS, ALU.mult, ALU.add).then_inc(ms3_done, 1)

        def rstd_pool(pool, c):
            pool.wait_ge(ms3_done, c + 1)
            nc.gpsimd.tensor_tensor(rstd3[:], ms3[:], minus_half[:], ALU.pow).then_inc(rstd3_done, 1)

        def normed_dve(dve, c, splits):
            dve.wait_ge(rstd3_done, c + 1)
            dve.wait_ge(q_in_low, credited(q_in_low, splits))
            for t in range(T):
                last = nc.vector.tensor_scalar(xn3[:, t, :], x2[:, t, :], rstd3[:, t:t + 1], None, ALU.mult)
            last.then_inc(xn3_done, 1)

        def bias_pool(pool, c):
            pool.wait_ge(falpha_loaded, (c + 1) * 16)
            pool.wait_ge(xn3_done, c + 1)
            nc.gpsimd.tensor_tensor(x2[:], x2[:], falpha[:, 1:2, :].broadcast_to([P, T, D]), ALU.add) \
                .then_inc(x2_biased, 1)

        def xf_pe(pe, c, use):
            pe.wait_ge(xn3_done, c + 1)
            for k in range(KD):
                pe.wait_ge(pair_free[k], credited(pair_free[k], use))
                for t in range(T):
                    last = nc.tensor.transpose(ab[k][:, t * P:(t + 1) * P], xn3[:, t, k * P:(k + 1) * P], ident[:])
                last.then_inc(pair_full[k], 1)

        def xf_dve(dve, c, use):
            for k in range(KD):
                dve.wait_ge(pair_full[k], use + 1)
            for k in range(KD):
                nc.vector.tensor_scalar(x_in[:, :, k, :], ab[k][:].rearrange("p (t n) -> p t n", t=T),
                                        par[:, c, FGAM + k:FGAM + k + 1], par[:, c, FBET + k:FBET + k + 1],
                                        ALU.mult, ALU.add).then_inc(pair_free[k], 1)

        def xf_act(act, c, use):
            act.wait_ge(ffn_projected, credited(ffn_projected, c))
            for k in range(KD):
                act.wait_ge(pair_free[k], credited(pair_free[k], use + 1))
                nc.scalar.activation(xf_part[0][:, k, :].rearrange("p (t n) -> p t n", t=T), x_in[:, :, k, :],
                                     ACT.Copy).then_inc(f_in_high, 1)

        def xf_pool(pool, c):
            for k in range(KD):
                pool.wait_ge(f_in_high, KD * c + (k + 1))
                nc.gpsimd.tensor_tensor(xf_part[1][:, k, :].rearrange("p (t n) -> p t n", t=T), x_in[:, :, k, :],
                                        xf_part[0][:, k, :].rearrange("p (t n) -> p t n", t=T).bitcast(f32),
                                        ALU.subtract).then_inc(f_in_low, 1)

        def hidden_pe(pe, c, n, f, use, h):
            if h == 0:
                pe.wait_ge(f_in_low, credited(f_in_low, KD * (c + 1)))
                pe.wait_ge(pair_free[n], credited(pair_free[n], use + f))
            weight = (gate_w, hidden_w)[n]
            for i in (range(3) if h == 0 else range(3, 6)):
                a, wp, k = PROJECTION[i]
                last = nc.tensor.matmul(ab[n][:], weight[wp][:, k, f * P:(f + 1) * P], xf_part[a][:, k, :],
                                        start=(i == 0), stop=(i == 5))
            if h == 1:
                last.then_inc(pair_full[n], 1)
                if n == 1 and f == NH - 1:
                    nc.tensor.nop().then_inc(ffn_projected, 1)

        def gate_act(act, c, f, use):
            act.wait_ge(pair_full[0], use + (f + 1))
            if f > 0:
                act.wait_ge(pair_free[1], credited(pair_free[1], use + f))
            nc.scalar.activation(scratch[0][:], ab[0][:], ACT.Tanh, scale=0.5).then_inc(tanh_done, 1)

        def gate_dve(dve, c, f):
            dve.wait_ge(tanh_done, c * NH + (f + 1))
            nc.vector.scalar_tensor_tensor(scratch[0][:], scratch[0][:], 1.0, ab[0][:], ALU.add, ALU.mult) \
                .then_inc(pair_free[0], 1)

        def product_dve(dve, c, f, use):
            dve.wait_ge(pair_free[0], credited(pair_free[0], use + (f + 1)))
            dve.wait_ge(prod_low, credited(prod_low, c * NH + f))
            dve.wait_ge(pair_full[1], use + (f + 1))
            nc.vector.scalar_tensor_tensor(scratch[1][:], scratch[0][:], 0.5, ab[1][:], ALU.mult, ALU.mult) \
                .then_inc(pair_free[1], 1)

        def product_act(act, c, f, use, staged):
            if f == RESERVED:
                act.wait_ge(stacked[1], staged * STACK)
            act.wait_ge(pair_free[1], credited(pair_free[1], use + (f + 1)))
            nc.scalar.activation(hid[0][:, f, :], scratch[1][:], ACT.Copy).then_inc(prod_high, 1)

        def product_pool(pool, c, f):
            pool.wait_ge(prod_high, c * NH + (f + 1))
            nc.gpsimd.tensor_tensor(hid[1][:, f, :], scratch[1][:], hid[0][:, f, :].bitcast(f32), ALU.subtract) \
                .then_inc(prod_low, 1)

        def out_pe(pe, c, t, half, use, h):
            m = t // HALF
            if h == 0 and half == 0:
                if t == 0:
                    pe.wait_ge(prod_low, credited(prod_low, c * NH + NH))
                if t % HALF == 0:
                    pe.wait_ge(pair_free[m], credited(pair_free[m], use))
            steps = [(a, wp, f) for f in range(NH) for a, wp in PARTS]
            n = len(steps) // 4
            first = (2 * half + h) * n
            for i in range(first, first + n):
                a, wp, f = steps[i]
                last = nc.tensor.matmul(ab[m][:, (t % HALF) * D:(t % HALF + 1) * D], hid[a][:, f, t * P:(t + 1) * P],
                                        out_w[wp][:, f, :], start=(i == 0), stop=(i == len(steps) - 1))
            if t % HALF == HALF - 1 and half == 1 and h == 1:
                last.then_inc(pair_full[m], 1)

        def out_dve(dve, c, m, use):
            dve.wait_ge(falpha_loaded, (c + 1) * 16)
            dve.wait_ge(prod_low, credited(prod_low, c * NH + NH))
            dve.wait_ge(pair_full[m], use + 1)
            nc.vector.tensor_tensor(by_tiles(scratch[m]), bank_view(m), falpha[:, 0:1, :].broadcast_to([P, HALF, D]),
                                    ALU.mult).then_inc(pair_free[m], 1)

        def out_pool(pool, c, m, use):
            pool.wait_ge(x2_biased, c + 1)
            pool.wait_ge(pair_free[m], credited(pair_free[m], use + 1))
            nc.gpsimd.tensor_tensor(halves(x2, m), halves(x2, m), by_tiles(scratch[m]), ALU.add).then_inc(y_done, 1)

        STEPS = G * T
        FFN_PIECES = [(what, f) for f in range(NH) for what in ("gate", "hidden")] + [("gap",)] + \
                     [("out", t, half) for t in range(T) for half in range(2)]
        HEAD = {0: [("v", 0), ("v", 1)], 1: [("qk", 1, 0), ("qk", 1, 1)], 2: [("wo", t) for t in range(T)],
                3: [("qk", 0, 0)], 4: [("qk", 0, 1), ("xf",)]}
        FIRST_FFN = 6
        RAWS = ((2, 1, 1, 1), (2, 1, 2, 1), (2, 1, 1, 1), (0, 0, 0, 0))

        def plan(ffn, following):
            table = [[] for _ in range(STEPS * J)]
            left = list(FFN_PIECES) if ffn else []
            for n in range(STEPS):
                pieces = [p for p in HEAD.get(n, []) if (ffn or p[0] not in ("wo", "xf"))
                          and (following or p[:2] != ("qk", 0))]
                if n >= FIRST_FFN and left:
                    steps_left = STEPS - n
                    take = -(-len(left) // steps_left)
                    pieces += left[:take]
                    left = left[take:]
                parts = [(p, h) for p in pieces for h in range(2)]
                for i, part in enumerate(parts):
                    table[n * J + i * J // len(parts)].append(part)
            return table

        def finished(table, lag):
            out_table = [[] for _ in range(STEPS * J + 1)]
            for pos, parts in enumerate(table):
                for p, h in parts:
                    if h == 1:
                        out_table[min(pos + lag, STEPS * J)].append(p)
            return out_table

        def uses(ffn, following):
            at, n = {}, 0
            for stage, there in (("v", True), (("qk", 1), True), ("wo", ffn), (("qk", 0), following), ("xf", ffn)):
                at[stage] = n
                n += 1 if there else 0
            at["hidden"] = n
            at["out"] = n + NH
            return at, (n + NH + 1 if ffn else n)

        BEFORE = 1
        USES_FIRST, USES_LOOP = uses(False, True)[1], uses(True, True)[1]

        def piece_pe(pe, b, u, at, p, h):
            if p[0] == "v":
                v_pe(pe, b, p[1], u + at["v"], h)
            elif p[0] == "qk":
                m, w = p[1:]
                qk_pe(pe, b if m == 1 else b + 1, m, w, u + at["qk", m], h)
                if (m, w, h) == (1, 1, 1):
                    nc.tensor.nop().then_inc(qkv_projected, 1)
            elif p[0] == "wo":
                wo_pe(pe, b - 1, p[1], u + at["wo"], h)
            elif p[0] == "xf":
                if h == 1:
                    xf_pe(pe, b - 1, u + at["xf"])
            elif p[0] == "gap":
                pass
            elif p[0] == "out":
                out_pe(pe, b - 1, p[1], p[2], u + at["out"], h)
            else:
                hidden_pe(pe, b - 1, 0 if p[0] == "gate" else 1, p[1], u + at["hidden"], h)

        def piece_act(act, b, u, at, p, staged, late):
            if p[0] == "hidden" and late:
                product_act(act, b - 1, p[1], u + at["hidden"], staged)
            elif p[0] == "gate" and not late:
                gate_act(act, b - 1, p[1], u + at["hidden"])
            elif p[0] == "qk" and not late:
                qk_act(act, p[1], p[2], u + at["qk", p[1]])

        def piece_dve(dve, b, u, at, p):
            if p[0] == "v":
                v_dve(dve, b, p[1], u + at["v"])
            elif p[0] == "qk":
                qk_dve(dve, p[1], p[2], 4 * b + (2 if p[1] == 1 else 4))
            elif p[0] == "wo" and p[1] % HALF == HALF - 1:
                wo_dve(dve, b - 1, p[1] // HALF, u + at["wo"])
            elif p[0] == "xf":
                xf_dve(dve, b - 1, u + at["xf"])
            elif p[0] == "gate":
                gate_dve(dve, b - 1, p[1])
            elif p[0] == "hidden":
                product_dve(dve, b - 1, p[1], u + at["hidden"])
            elif p[0] == "out" and p[1] % HALF == HALF - 1 and p[2] == 1:
                out_dve(dve, b - 1, p[1] // HALF, u + at["out"])

        def piece_pool(pool, b, u, at, p):
            if p[0] == "hidden":
                product_pool(pool, b - 1, p[1])
            elif p[0] == "out" and p[1] % HALF == HALF - 1 and p[2] == 1:
                out_pool(pool, b - 1, p[1] // HALF, u + at["out"])

        SPLIT_AT = 2 * J
        OPEN_AT = 2 * T * J + 2
        SQUARES_AT = 3 * J + 2
        MEAN_AT = 3 * J + 3
        NORMED_AT = 4 * J + 1
        XF_AT = 4 * J + 4

        def last_of(b, g):
            return (b, g - 1) if g > 0 else (b - 1, G - 1)

        def pe_batch(pe, b, u, ffn, following):
            table, at = plan(ffn, following), uses(ffn, following)[0]
            for pos in range(STEPS * J):
                n, j = pos // J, pos % J
                g, kt = n // T, n % T
                if pos % (T * J) == 0:
                    pe.wait_ge(shift_loaded, credited(shift_loaded, (b * G + (g + 1)) * 64))
                if pos == OPEN_AT and following:
                    for w in range(2):
                        pe.wait_ge(pair_free[w], credited(pair_free[w], u + at["qk", 0] + 1))
                score_pe(pe, b, g, kt, j)
                if pos == OPEN_AT and following:
                    nc.tensor.nop().then_inc(stack_open, 1)
                nb, ng = (b, g + 1) if g + 1 < G else (b + 1, 0)
                if g + 1 < G or following:
                    for s in raws_at(kt, j):
                        raw_score(pe, nb, ng, s)
                    if (kt, j) == (T - 1, 1):
                        maxima_transposed(pe, nb, ng)
                if j == 1 and (n > 0 or ffn):
                    pb, pg = last_of(b, g) if kt == 0 else (b, g)
                    values_pe(pe, pb, pg, (kt - 1) % T, u + at["v"] if n == 1 else None)
                for p, h in table[pos]:
                    piece_pe(pe, b, u, at, p, h)

        def raws_at(kt, j):
            first = sum(sum(r) for r in RAWS[:kt]) + sum(RAWS[kt][:j])
            return range(first, first + RAWS[kt][j])

        def act_batch(act, b, u, ffn, following):
            table, at = plan(ffn, following), uses(ffn, following)[0]
            early, late = finished(table, 0), finished(table, 1)
            for pos in range(STEPS * J + 1):
                n, j = pos // J, pos % J
                g, kt = n // T, n % T
                if n < STEPS:
                    exp_act(act, b, g, kt, j)
                    if (kt, j) == (1, 0) and (g > 0 or ffn):
                        pb, pg = last_of(b, g)
                        normalise_act(act, pb, pg, b + 2 if following else b + 1)
                if pos == SPLIT_AT and following:
                    xa_split_act(act, b + 1)
                if ffn and pos == SQUARES_AT:
                    squares_act(act, b - 1)
                if ffn and pos == XF_AT:
                    xf_act(act, b - 1, u + at["xf"])
                for p in early[pos]:
                    piece_act(act, b, u, at, p, b + 1, False)
                for p in late[pos]:
                    piece_act(act, b, u, at, p, b + 1, True)

        def dve_batch(dve, b, u, ffn, following):
            table, at = plan(ffn, following), uses(ffn, following)[0]
            done = finished(table, 1)
            for pos in range(STEPS * J + 1):
                n, j = pos // J, pos % J
                g, kt = n // T, n % T
                nb, ng = (b, g + 1) if g + 1 < G else (b + 1, 0)
                if n < STEPS and (g + 1 < G or following):
                    for s in raws_at(kt, j):
                        maximum_dve(dve, nb, ng, s)
                    if (kt, j) == (T - 1, 1):
                        shift_dve(dve, nb, ng)
                if n < STEPS and (kt, j) == (0, 2) and (g > 0 or ffn):
                    normalise_dve(dve, *last_of(b, g))
                if ffn and pos == MEAN_AT:
                    mean_dve(dve, b - 1)
                if ffn and pos == NORMED_AT:
                    normed_dve(dve, b - 1, b + 2 if following else b + 1)
                for p in done[pos]:
                    piece_dve(dve, b, u, at, p)

        def pool_batch(pool, b, u, ffn, following):
            table, at = plan(ffn, following), uses(ffn, following)[0]
            done = finished(table, 3)
            for pos in range(STEPS * J + 1):
                n, j = pos // J, pos % J
                g, kt = n // T, n % T
                if n < STEPS and (kt, j) == (1, 0) and (g > 0 or ffn):
                    normalise_pool(pool, *last_of(b, g))
                if pos == SPLIT_AT and following:
                    xa_split_pool(pool, b + 1)
                if ffn and pos == MEAN_AT:
                    rstd_pool(pool, b - 1)
                if ffn and pos == XF_AT:
                    xf_pool(pool, b - 1)
                    bias_pool(pool, b - 1)
                for p in done[pos]:
                    piece_pool(pool, b, u, at, p)

        def sp_x1(sp, c):
            for m in range(2):
                sp.wait_ge(y_stored[m], credited(y_stored[m], c * 16))
                sp.dma_start(halves(x2, m), x1_dram[c].rearrange("t p n -> p t n")[:, m * HALF:(m + 1) * HALF, :]) \
                    .then_inc(x1_loaded[m], 16)
            sp.wait_ge(x2_done[1], credited(x2_done[1], c))
            sp.dma_start(aalpha[:], alpha_dram[c, 0:D].partition_broadcast(P)).then_inc(aalpha_loaded, 16)
            sp.wait_ge(y_done, credited(y_done, 2 * c))
            sp.dma_start(falpha[:], alpha_dram[c, D:3 * D].rearrange("(a n) -> a n", a=2).partition_broadcast(P)) \
                .then_inc(falpha_loaded, 16)

        def sp_xa(sp, c):
            sp.dma_start(x_in[:], xa_dram[c].rearrange("t p k n -> p t k n")).then_inc(xa_loaded, 16)

        def sp_store(sp, c):
            for m in range(2):
                sp.wait_ge(y_done, credited(y_done, 2 * c + (m + 1)))
                sp.dma_start(out[c, m * HALF * P:(m + 1) * HALF * P, :].rearrange("(t p) n -> p t n", p=P),
                             halves(x2, m)).then_inc(y_stored[m], 16)

        def sp_batch(sp, b, u, ffn, following):
            at = uses(ffn, following)[0]
            if following:
                sp.wait_ge(q_in_low, credited(q_in_low, b + 1))
                if ffn:
                    sp.wait_ge(f_in_low, credited(f_in_low, (b - 1) * KD))
                sp_xa(sp, b + 1)
            if ffn:
                sp_x1(sp, b - 1)
            stack_sp(sp, 1, u + at["qk", 1])
            shift_sp(sp, b, 1)
            shift_sp(sp, b, 2)
            if following:
                sp.wait_ge(stack_open, b + 1)
                stack_sp(sp, 0)
            shift_sp(sp, b, 3)
            if following:
                shift_sp(sp, b + 1, 0)
            if ffn:
                sp_store(sp, b - 1)

        END = BEFORE + USES_FIRST + (B - 2) * USES_LOOP + uses(True, False)[1]

        def sp_before(sp):
            sp_xa(sp, 0)
            sp.wait_ge(ones_ready, 1)
            stack_sp(sp, 0, 0)
            shift_sp(sp, 0, 0)

        def sp_after(sp):
            sp_x1(sp, B - 1)
            sp_store(sp, B - 1)
            for m in range(2):
                sp.wait_ge(y_stored[m], credited(y_stored[m], B * 16))

        def act_before(act):
            xa_split_act(act, 0, first=True)
            for w in range(2):
                qk_act(act, 0, w, 0)

        def act_after(act):
            normalise_act(act, B - 1, G - 1, B)
            squares_act(act, B - 1)
            xf_act(act, B - 1, END + 1)
            for f in range(NH):
                gate_act(act, B - 1, f, END + 2)
                product_act(act, B - 1, f, END + 2, B)

        def pool_before(pool):
            xa_split_pool(pool, 0)

        def pool_after(pool):
            normalise_pool(pool, B - 1, G - 1)
            rstd_pool(pool, B - 1)
            xf_pool(pool, B - 1)
            bias_pool(pool, B - 1)
            for f in range(NH):
                product_pool(pool, B - 1, f)
            for m in range(2):
                out_pool(pool, B - 1, m, END + 2 + NH)

        def pe_before(pe):
            for w in range(2):
                for h in range(2):
                    qk_pe(pe, 0, 0, w, 0, h)
            for s in range(J * T):
                raw_score(pe, 0, 0, s)
            maxima_transposed(pe, 0, 0)

        def pe_after(pe):
            values_pe(pe, B - 1, G - 1, T - 1)
            for t in range(T):
                for h in range(2):
                    wo_pe(pe, B - 1, t, END, h)
            xf_pe(pe, B - 1, END + 1)
            for f in range(NH):
                for n in range(2):
                    for h in range(2):
                        hidden_pe(pe, B - 1, n, f, END + 2, h)
            for t in range(T):
                for half in range(2):
                    for h in range(2):
                        out_pe(pe, B - 1, t, half, END + 2 + NH, h)

        def dve_before(dve):
            nc.vector.memset(o_bank[:], 0.0)
            dve.wait_ge(ones_ready, 1)
            for w in range(2):
                qk_dve(dve, 0, w, 0)
            for s in range(J * T):
                maximum_dve(dve, 0, 0, s)
            shift_dve(dve, 0, 0)

        def dve_after(dve):
            normalise_dve(dve, B - 1, G - 1)
            for m in range(2):
                wo_dve(dve, B - 1, m, END)
            mean_dve(dve, B - 1)
            normed_dve(dve, B - 1, B)
            xf_dve(dve, B - 1, END + 1)
            for f in range(NH):
                gate_dve(dve, B - 1, f)
                product_dve(dve, B - 1, f, END + 2)
            for m in range(2):
                out_dve(dve, B - 1, m, END + 2 + NH)

        def phase2_program(eng, before, batch, after):
            before(eng)
            batch(eng, 0, BEFORE, False, True)
            with eng.Fori(0, B - 2) as i:
                batch(eng, i + 1, i * USES_LOOP + (BEFORE + USES_FIRST), True, True)
            batch(eng, B - 1, BEFORE + USES_FIRST + (B - 2) * USES_LOOP, True, False)
            after(eng)

        with nc.Block() as block:
            @block.sync
            def _(sp):
                phase2_program(sp, sp_before, sp_batch, sp_after)

            @block.scalar
            def _(act):
                phase2_program(act, act_before, act_batch, act_after)

            @block.gpsimd
            def _(pool):
                nc.gpsimd.memset(v_ext[:, :, :, HD:HD + 1], 1.0)
                nc.gpsimd.memset(k_stack[:].bitcast(f32), 1.0).then_inc(ones_ready, 1)
                phase2_program(pool, pool_before, pool_batch, pool_after)

            @block.tensor
            def _(pe):
                phase2_program(pe, pe_before, pe_batch, pe_after)

            @block.vector
            def _(dve):
                phase2_program(dve, dve_before, dve_batch, dve_after)


def kernel(x, cond_256, L0_cond_norm_w, L0_cond_up_w, L0_cond_down_w, L1_cond_attn_gamma_w, L1_cond_attn_beta_w,
           L1_cond_W_q, L1_cond_W_k, L1_cond_W_v, L1_cond_W_o, L1_cond_attn_alpha_w, L1_cond_ffn_gamma_w,
           L1_cond_ffn_beta_w, L1_cond_gate_w, L1_cond_hidden_w, L1_cond_out_w, L1_cond_out_b,
           L1_cond_ffn_alpha_w):
    import numpy as np
    import concourse.bacc as bacc
    from concourse.bass_utils import run_bass_kernel_spmd

    x = np.asarray(x)
    batches, tokens, width = x.shape

    def t(w):
        return np.ascontiguousarray(np.asarray(w).T)

    def by_slots(w):
        w = np.asarray(w).reshape(2, 4, 2, 16, width)
        return t(w.transpose(0, 2, 3, 1, 4).reshape(width, width))

    xT = np.ascontiguousarray(x.reshape(batches * tokens // 128, 128, width // 128, 128).transpose(0, 3, 2, 1))
    arrays = {
        "x_tok": np.ascontiguousarray(x), "xT": xT, "condT": t(cond_256), "norm_wT": t(L0_cond_norm_w),
        "up_wT": t(L0_cond_up_w), "down_wT": t(L0_cond_down_w), "agam_wT": t(L1_cond_attn_gamma_w),
        "abet_wT": t(L1_cond_attn_beta_w), "wqT": by_slots(L1_cond_W_q), "wkT": by_slots(L1_cond_W_k),
        "wvT": t(L1_cond_W_v), "woT": t(L1_cond_W_o), "aalpha_wT": t(L1_cond_attn_alpha_w),
        "fgam_wT": t(L1_cond_ffn_gamma_w), "fbet_wT": t(L1_cond_ffn_beta_w), "gate_wT": t(L1_cond_gate_w),
        "hidden_wT": t(L1_cond_hidden_w), "out_wT": t(L1_cond_out_w), "out_b": np.asarray(L1_cond_out_b),
        "falpha_wT": t(L1_cond_ffn_alpha_w),
    }
    nc = bacc.Bacc("TRN2", target_bir_lowering=False, num_devices=1)
    args = [nc.dram_tensor(name, a.shape, mybir.dt.from_np(a.dtype), kind="ExternalInput").ap()
            for name, a in arrays.items()]
    out = nc.dram_tensor("out", x.shape, mybir.dt.float32, kind="ExternalOutput").ap()
    cond_seq_kernel(nc, *args, out)
    r = run_bass_kernel_spmd(nc, [arrays], core_ids=[0])
    return r.results[0]["out"]
```

```python
import concourse.bass as bass
from concourse import mybir
from contextlib import ExitStack


def cond_seq_kernel(nc, x_tok, xT, condT, vec_wT, up_wT, down_wT, wqT, wkT, wvT, woT, gate_wT, hidden_wT,
                    out_wT, out_b, out):
    f32 = mybir.dt.float32
    f32r = mybir.dt.float32r
    bf16 = mybir.dt.bfloat16
    ALU = mybir.AluOpType
    ACT = mybir.ActivationFunctionType
    AX = mybir.AxisListType

    P = 128
    B = condT.shape[1]
    C = condT.shape[0]
    D = vec_wT.shape[2]
    KD = D // P
    S = xT.shape[0] * P // B
    T = S // P
    FF = down_wT.shape[0]
    KF = FF // P
    NH = gate_wT.shape[1] // P
    HD = 16
    G = 4
    J = 4
    W = 512
    EPS = 1e-6
    ROUND = 1.5 * 2.0 ** 23
    QMAX = 127.0
    PARTS = ((0, 0), (0, 1), (1, 0))
    ROWS = 3 * HD
    SROWS = ROWS + 2

    ctx = ExitStack()
    with ctx:
        def sb(stack, name, shape, dt=f32):
            return stack.enter_context(nc.sbuf_tensor(name, shape, dt))

        def sem(name):
            return ctx.enter_context(nc.semaphore(name))

        def dram(name, shape):
            return nc.dram_tensor(name, shape, f32, kind="Internal").ap()

        x1_dram = dram("x1_spill", (B, T, P, D))
        xa_dram = dram("xa_spill", (B, T, P, KD, P))
        alpha_dram = dram("alpha_spill", (B, 3 * D))

        psum = [ctx.enter_context(nc.psum_tensor(f"bank{i}", [P, W], f32)) for i in range(8)]

        par = sb(ctx, "par", [P, B, 5 * KD])
        SCALE0, AGAM, ABET, FGAM, FBET = (KD * n for n in range(5))
        ident = sb(ctx, "ident", [P, P])
        identb = sb(ctx, "identb", [P, P], bf16)
        minus_half = sb(ctx, "minus_half", [P, T])
        wdeq = sb(ctx, "wdeq", [P, 1])
        gate_w = [sb(ctx, f"gate_w{i}", [P, KD, NH * P], f32r) for i in range(2)]
        hidden_w = [sb(ctx, f"hidden_w{i}", [P, KD, NH * P], f32r) for i in range(2)]
        out_w = [sb(ctx, f"out_w{i}", [P, NH, D], f32r) for i in range(2)]
        wq = [sb(ctx, f"wq{i}", [P, KD, D], f32r) for i in range(2)]
        wk = [sb(ctx, f"wk{i}", [P, KD, D], f32r) for i in range(2)]
        wv = [sb(ctx, f"wv{i}", [P, KD, D], f32r) for i in range(2)]
        wo = [sb(ctx, f"wo{i}", [P, G, D], f32r) for i in range(2)]

        x_in = sb(ctx, "x_in", [P, T, KD, P])
        xa_part = [sb(ctx, f"xa_part{i}", [P, KD, S], f32r) for i in range(2)]

        phase1 = ExitStack()
        up_w = [sb(phase1, f"up_w{i}", [P, KD, 2 * FF], f32r) for i in range(2)]
        down_q = sb(phase1, "down_q", [P, KF, D], bf16)
        up_st = sb(phase1, "up_st", [P, KD, 2 * FF])
        down_st = sb(phase1, "down_st", [P, KF, D])
        gate_st = down_st[:].rearrange("p (k a) n -> p k (a n)", k=KD)
        hidden_st = up_st[:, 0, :].rearrange("p (k n) -> p k n", k=KD)
        out_st = up_st[:, 1, :].rearrange("p (k n) -> p k n", k=NH)
        q_st = sb(phase1, "q_st", [P, KD, D])
        k_st = sb(phase1, "k_st", [P, KD, D])
        v_st = sb(phase1, "v_st", [P, KD, D])
        o_st = sb(phase1, "o_st", [P, G, D])
        cond_sb = sb(phase1, "cond_sb", [C, B])
        vec_w = sb(phase1, "vec_w", [C, 7, D])
        outb_sb = sb(phase1, "outb_sb", [B, D])
        alpha_sb = sb(phase1, "alpha_sb", [B, 3, D])
        ones = sb(phase1, "ones", [P, P])
        absum = sb(phase1, "absum", [P, 1])
        mean = sb(phase1, "mean", [P, 1])
        wscale = sb(phase1, "wscale", [P, 1])

        small_loaded = sem("small_loaded")
        down_loaded = sem("down_loaded")
        weight_loaded = [sem(f"weight_loaded{i}") for i in range(7)]
        ostage_zeroed = sem("ostage_zeroed")
        consts_ready = sem("consts_ready")
        up_loaded = [sem(f"up_loaded{i}") for i in range(4)]
        up_high = sem("up_high")
        up_low = sem("up_low")
        par_ready = sem("par_ready")
        wdeq_ready = sem("wdeq_ready")
        high_done = sem("high_done")
        vectors_done = sem("vectors_done")
        alpha_done = sem("alpha_done")
        alpha_stored = sem("alpha_stored")
        down_steps = sem("down_steps")
        mean_summed = sem("mean_summed")

        late = [(q_st, wq, wqT), (k_st, wk, wkT), (v_st, wv, wvT), (o_st, wo, woT),
                (hidden_st, hidden_w, hidden_wT), (out_st, out_w, out_wT), (gate_st, gate_w, gate_wT)]
        WO = 3
        CHUNKS = [slice(FF, FF + W), slice(0, W), slice(FF + W, FF + 2 * W), slice(W, 2 * W)]

        xt_loaded = [sem(f"xt_loaded{t}") for t in range(T)]
        xk_loaded = [sem(f"xk_loaded{s}") for s in range(2)]
        scale_ready = sem("scale_ready")
        x_scaled = sem("x_scaled")
        x_high = sem("x_high")
        x_split = sem("x_split")
        square_done = sem("square_done")
        ms_done = sem("ms_done")
        rstd_done = sem("rstd_done")
        up_gate_done = sem("up_gate_done")
        up_val_done = sem("up_val_done")
        up_done = sem("up_done")
        gelu_done = sem("gelu_done")
        h_done = sem("h_done")
        scale_steps = sem("scale_steps")
        dequant_done = sem("dequant_done")
        rounded = sem("rounded")
        quantised = sem("quantised")
        q_transposed = sem("q_transposed")
        qT_copied = sem("qT_copied")
        down_done = sem("down_done")
        x1_done = sem("x1_done")
        x1_stored = [sem(f"x1_stored{t}") for t in range(T)]
        square2_done = sem("square2_done")
        ms2_done = sem("ms2_done")
        rstd2_done = sem("rstd2_done")
        xn_done = sem("xn_done")
        xn_transposed = sem("xn_transposed")
        xa_done = sem("xa_done")
        xa_stored = [sem(f"xa_stored{s}") for s in range(2)]
        CREDIT1 = {x_split: 1, x_scaled: 2, up_done: 2, gelu_done: 2, h_done: 2, quantised: 1, q_transposed: 2,
                   qT_copied: 1, down_done: 1, x1_done: 4, ms_done: 1, rstd_done: 2, ms2_done: 1,
                   rstd2_done: 1, xn_transposed: 1, xa_done: 1,
                   x1_stored[0]: 1, x1_stored[1]: 1, x1_stored[2]: 1, x1_stored[3]: 1,
                   xa_stored[0]: 1, xa_stored[1]: 1}

        vext_zeroed = sem("vext_zeroed")
        ones_ready = sem("ones_ready")
        stack_ones = sem("stack_ones")
        xa_loaded = sem("xa_loaded")
        x1_loaded = [sem(f"x1_loaded{m}") for m in range(2)]
        aalpha_loaded = sem("aalpha_loaded")
        falpha_loaded = sem("falpha_loaded")
        pair_full = [sem("bank_a_full"), sem("bank_b_full")]
        pair_free = [sem("bank_a_free"), sem("bank_b_free")]
        q_in_high = sem("q_in_high")
        q_in_low = sem("q_in_low")
        f_in_high = sem("f_in_high")
        f_in_low = sem("f_in_low")
        qkv_projected = sem("qkv_projected")
        qk_high = sem("qk_high")
        stacked = [sem(f"stacked{m}") for m in range(2)]
        raw_full = sem("raw_full")
        raw_read = sem("raw_read")
        shift_high = sem("shift_high")
        shift_loaded = sem("shift_loaded")
        score_full = sem("score_full")
        exp_done = sem("exp_done")
        pv_done = sem("pv_done")
        o_read = sem("o_read")
        norm_steps = sem("norm_steps")
        on_done = sem("on_done")
        on_high = sem("on_high")
        on_low = sem("on_low")
        wo_done = sem("wo_done")
        x2_done = [sem(f"x2_done{m}") for m in range(2)]
        square3_done = sem("square3_done")
        ms3_done = sem("ms3_done")
        rstd3_done = sem("rstd3_done")
        xn3_done = sem("xn3_done")
        x2_biased = sem("x2_biased")
        tanh_done = sem("tanh_done")
        prod_high = sem("prod_high")
        prod_low = sem("prod_low")
        ffn_projected = sem("ffn_projected")
        stack_open = sem("stack_open")
        y_done = sem("y_done")
        y_stored = [sem(f"y_stored{m}") for m in range(2)]
        CREDIT2 = {pair_free[0]: 1, pair_free[1]: 1, raw_read: 2, exp_done: 1, pv_done: 2, o_read: 1, on_low: 1,
                   shift_loaded: 1, ffn_projected: 2, wo_done: 1, prod_low: 1, q_in_low: 1, f_in_low: 2,
                   x2_done[0]: 1, x2_done[1]: 1, y_done: 2, y_stored[0]: 1, y_stored[1]: 1}

        def credited(s, value):
            return value + CREDIT1.get(s, CREDIT2.get(s, 0))

        def live(tile, lag):
            return tile is None or 0 <= tile - lag < B * T

        xt = sb(phase1, "xt", [P, T, D])
        xk = sb(phase1, "xk", [P, 2, KD, P])
        cur_scale = sb(phase1, "cur_scale", [P, KD])
        xs = sb(phase1, "xs", [P, KD, P])
        xs_part = [sb(phase1, f"xs_part{i}", [P, 2, KD, P], f32r) for i in range(2)]
        square_junk = sb(phase1, "square_junk", [P, D])
        ss = sb(phase1, "ss", [P, 1])
        ms = sb(phase1, "ms", [P, 1])
        rstd = sb(phase1, "rstd", [P, 2])
        gelu = sb(phase1, "gelu", [P, 2, W])
        h = sb(phase1, "h", [P, FF])
        amax = sb(phase1, "amax", [P, 4])
        dequant = sb(phase1, "dequant", [P, 2])
        h_rounded = sb(phase1, "h_rounded", [P, FF])
        h_q = sb(phase1, "h_q", [P, 2, FF], bf16)
        qT = sb(phase1, "qT", [P, FF], bf16)
        x1t = sb(phase1, "x1t", [P, T, D])
        square_junk2 = sb(phase1, "square_junk2", [P, D])
        ss2 = sb(phase1, "ss2", [P, 1])
        ms2 = sb(phase1, "ms2", [P, 1])
        rstd2 = sb(phase1, "rstd2", [P, 1])
        xn = sb(phase1, "xn", [P, D])
        xa = sb(phase1, "xa", [P, 2, KD, P])
        gate_bank = psum[0:2]
        val_bank = psum[2:4]
        tr_bank = psum[4][:].bitcast(bf16)
        down_bank = psum[5]
        xn_bank = psum[6]

        UP, DOWN, NORM, STORE = 1, 2, 3, 4

        def back(b, t, lag):
            return b + (t - lag) // T, (t - lag) % T, b * T + (t - lag)

        def load_tile(sp, b, t, tile):
            if live(tile, 0):
                b, t, n = back(b, t, 0)
                sp.wait_ge(x1_done, credited(x1_done, n - 3))
                sp.dma_start(xt[:, t, :], x_tok[b, t * P:(t + 1) * P, :]).then_inc(xt_loaded[t], 16)
                sp.wait_ge(x_scaled, credited(x_scaled, n - 1))
                sp.dma_start(xk[:, t % 2, :, :], xT[n, :, :, :]).then_inc(xk_loaded[t % 2], 16)

        def act_tile(act, b0, t0, tile):
            def act_gelu(j):
                b, t, n = back(b0, t0, UP)
                act.wait_ge(up_gate_done, 2 * n + j + 1)
                act.wait_ge(rstd_done, credited(rstd_done, n + 1))
                act.wait_ge(h_done, credited(h_done, 2 * n + j - 1))
                nc.scalar.activation(gelu[:, j, :], gate_bank[j][:], ACT.Gelu, scale=rstd[:, t % 2:t % 2 + 1]) \
                    .then_inc(gelu_done, 1)
            if live(tile, UP):
                act_gelu(0)
            if live(tile, 0):
                b, t, n = back(b0, t0, 0)
                act.wait_ge(scale_ready, b + 1)
                act.wait_ge(xk_loaded[t % 2], (b * 2 + t // 2 + 1) * 16)
                act.wait_ge(x_split, credited(x_split, n))
                for k in range(KD):
                    last = nc.scalar.activation(xs[:, k, :], xk[:, t % 2, k, :], ACT.Copy,
                                                scale=cur_scale[:, k:k + 1])
                last.then_inc(x_scaled, 1)
                act.wait_ge(xt_loaded[t], (b + 1) * 16)
                act.wait_ge(ms_done, credited(ms_done, n))
                nc.scalar.activation(square_junk[:], xt[:, t, :], ACT.Square, accum_out=ss[:]) \
                    .then_inc(square_done, 1)
            if live(tile, UP):
                act_gelu(1)
            if live(tile, DOWN):
                b, t, m = back(b0, t0, DOWN)
                act.wait_ge(q_transposed, credited(q_transposed, m + 1))
                act.wait_ge(down_done, credited(down_done, m))
                nc.scalar.activation(qT[:], tr_bank[:, 0:FF], ACT.Copy).then_inc(qT_copied, 1)
            if live(tile, NORM):
                b, t, m = back(b0, t0, NORM)
                act.wait_ge(x1_done, credited(x1_done, m + 1))
                act.wait_ge(ms2_done, credited(ms2_done, m))
                act.dma_start(x1_dram[b, t, :, :], x1t[:, t, :]).then_inc(x1_stored[t], 16)
                nc.scalar.activation(square_junk2[:], x1t[:, t, :], ACT.Square, accum_out=ss2[:]) \
                    .then_inc(square2_done, 1)
            if live(tile, STORE):
                b, t, m = back(b0, t0, STORE)
                act.wait_ge(xa_done, credited(xa_done, m + 1))
                act.dma_start(xa_dram[b, t, :, :, :], xa[:, t % 2, :, :]).then_inc(xa_stored[t % 2], 16)

        def pool_tile(pool, b0, t0, tile):
            if live(tile, 0):
                b, t, n = back(b0, t0, 0)
                pool.wait_ge(up_done, credited(up_done, n - 1))
                pool.wait_ge(x_high, n + 1)
                nc.gpsimd.tensor_tensor(xs_part[1][:, t % 2, :, :], xs[:], xs_part[0][:, t % 2, :, :].bitcast(f32),
                                        ALU.subtract).then_inc(x_split, 1)
                pool.wait_ge(gelu_done, credited(gelu_done, 2 * n - 2))
                pool.wait_ge(h_done, credited(h_done, 2 * n - 2))
                pool.wait_ge(ms_done, credited(ms_done, n + 1))
                nc.gpsimd.tensor_tensor(rstd[:, t % 2:t % 2 + 1], ms[:], minus_half[:, 0:1], ALU.pow) \
                    .then_inc(rstd_done, 1)
            if live(tile, NORM):
                b, t, m = back(b0, t0, NORM)
                if tile is None or m > 0:
                    pool.wait_ge(xn_done, m)
                pool.wait_ge(ms2_done, credited(ms2_done, m + 1))
                nc.gpsimd.tensor_tensor(rstd2[:], ms2[:], minus_half[:, 0:1], ALU.pow).then_inc(rstd2_done, 1)

        def pe_tile(pe, b0, t0, tile):
            def up(j, bank, col, free, full):
                b, t, n = back(b0, t0, UP)
                pe.wait_ge(free, credited(free, 2 * n + j - 1))
                steps = [(a, m, k) for k in range(KD) for a, m in PARTS]
                for i, (a, m, k) in enumerate(steps):
                    last = nc.tensor.matmul(bank[j][:], xs_part[a][:, t % 2, k, :],
                                            up_w[m][:, k, col + j * W:col + (j + 1) * W],
                                            start=(i == 0), stop=(i == len(steps) - 1))
                last.then_inc(full, 1)

            def up_gate(j):
                up(j, gate_bank, FF, gelu_done, up_gate_done)

            def up_value(j):
                up(j, val_bank, 0, h_done, up_val_done)
            if live(tile, UP):
                pe.wait_ge(x_split, credited(x_split, back(b0, t0, UP)[2] + 1))
                up_gate(0)
                up_value(0)
                up_gate(1)
            if live(tile, STORE):
                b, t, m = back(b0, t0, STORE)
                pe.wait_ge(xn_done, m + 1)
                pe.wait_ge(xa_done, credited(xa_done, m))
                for k in range(KD):
                    last = nc.tensor.transpose(xn_bank[:, k * P:(k + 1) * P], xn[:, k * P:(k + 1) * P], ident[:])
                last.then_inc(xn_transposed, 1)
            if live(tile, DOWN):
                b, t, m = back(b0, t0, DOWN)
                pe.wait_ge(quantised, credited(quantised, m + 1))
                pe.wait_ge(qT_copied, credited(qT_copied, m))
                for k in range(KF):
                    last = nc.tensor.transpose(tr_bank[:, k * P:(k + 1) * P], h_q[:, t % 2, k * P:(k + 1) * P],
                                               identb[:])
                last.then_inc(q_transposed, 1)
            if live(tile, UP):
                up_value(1)
                nc.tensor.nop().then_inc(up_done, 1)
            if live(tile, DOWN):
                b, t, m = back(b0, t0, DOWN)
                pe.wait_ge(qT_copied, credited(qT_copied, m + 1))
                if tile == DOWN:
                    pe.wait_ge(down_steps, 6)
                pe.wait_ge(x1_done, credited(x1_done, m))
                for k in range(KF):
                    last = nc.tensor.matmul(down_bank[:, 0:D], qT[:, k * P:(k + 1) * P], down_q[:, k, :],
                                            start=(k == 0), stop=(k == KF - 1))
                last.then_inc(down_done, 1)

        def dve_tile(dve, b0, t0, tile):
            if live(tile, 0):
                b, t, n = back(b0, t0, 0)
                if t == 0:
                    dve.wait_ge(x_scaled, credited(x_scaled, n))
                    nc.vector.tensor_scalar(cur_scale[:], par[:, b, SCALE0:SCALE0 + KD], 1.0, None, ALU.mult) \
                        .then_inc(scale_ready, 1)
                dve.wait_ge(x_scaled, credited(x_scaled, n + 1))
                dve.wait_ge(up_done, credited(up_done, n - 1))
                nc.vector.tensor_copy(xs_part[0][:, t % 2, :, :], xs[:]).then_inc(x_high, 1)
                dve.wait_ge(square_done, n + 1)
                dve.wait_ge(rstd_done, credited(rstd_done, n))
                nc.vector.tensor_scalar(ms[:], ss[:], 1.0 / D, EPS, ALU.mult, ALU.add).then_inc(ms_done, 1)

            def gate(j):
                b, t, n = back(b0, t0, UP)
                dve.wait_ge(up_val_done, 2 * n + j + 1)
                dve.wait_ge(gelu_done, credited(gelu_done, 2 * n + j + 1))
                nc.vector.scalar_tensor_tensor(h[:, j * W:(j + 1) * W], val_bank[j][:],
                                               rstd[:, t % 2:t % 2 + 1], gelu[:, j, :], ALU.mult, ALU.mult) \
                    .then_inc(h_done, 1)
            if live(tile, UP):
                b, t, n = back(b0, t0, UP)
                gate(0)
                gate(1)
            if live(tile, STORE):
                b, t, m = back(b0, t0, STORE)
                dve.wait_ge(xn_transposed, credited(xn_transposed, m + 1))
                if tile is None or m >= 2:
                    dve.wait_ge(xa_stored[t % 2], credited(xa_stored[t % 2], (b * 2 + t // 2) * 16))
                for k in range(KD):
                    last = nc.vector.tensor_scalar(xa[:, t % 2, k, :], xn_bank[:, k * P:(k + 1) * P],
                                                   par[:, b, AGAM + k:AGAM + k + 1],
                                                   par[:, b, ABET + k:ABET + k + 1], ALU.mult, ALU.add)
                last.then_inc(xa_done, 1)
            if live(tile, UP):
                b, t, n = back(b0, t0, UP)
                dve.wait_ge(h_done, credited(h_done, 2 * n + 2))
                nc.vector.tensor_reduce(amax[:, 0:1], h[:], AX.X, ALU.max, apply_absolute_value=True) \
                    .then_inc(scale_steps, 1)
            if live(tile, NORM):
                b, t, m = back(b0, t0, NORM)
                dve.wait_ge(square2_done, m + 1)
                dve.wait_ge(rstd2_done, credited(rstd2_done, m))
                nc.vector.tensor_scalar(ms2[:], ss2[:], 1.0 / D, EPS, ALU.mult, ALU.add).then_inc(ms2_done, 1)
            if live(tile, UP):
                b, t, n = back(b0, t0, UP)
                dve.wait_ge(scale_steps, 4 * n + 1)
                nc.vector.tensor_scalar(amax[:, 1:2], amax[:, 0:1], 1e-5, None, ALU.max).then_inc(scale_steps, 1)
                dve.wait_ge(scale_steps, 4 * n + 2)
                nc.vector.reciprocal(amax[:, 2:3], amax[:, 1:2]).then_inc(scale_steps, 1)
                nc.vector.tensor_tensor(dequant[:, t % 2:t % 2 + 1], amax[:, 1:2], wdeq[:], ALU.mult) \
                    .then_inc(dequant_done, 1)
                dve.wait_ge(scale_steps, 4 * n + 3)
                nc.vector.tensor_scalar(amax[:, 3:4], amax[:, 2:3], QMAX, None, ALU.mult).then_inc(scale_steps, 1)
                dve.wait_ge(scale_steps, 4 * n + 4)
                nc.vector.tensor_scalar(h_rounded[:], h[:], amax[:, 3:4], ROUND, ALU.mult, ALU.add) \
                    .then_inc(rounded, 1)
            if live(tile, NORM):
                b, t, m = back(b0, t0, NORM)
                dve.wait_ge(rstd2_done, credited(rstd2_done, m + 1))
                dve.wait_ge(xn_transposed, credited(xn_transposed, m))
                nc.vector.tensor_scalar(xn[:], x1t[:, t, :], rstd2[:], None, ALU.mult).then_inc(xn_done, 1)
            if live(tile, UP):
                b, t, n = back(b0, t0, UP)
                dve.wait_ge(rounded, n + 1)
                dve.wait_ge(q_transposed, credited(q_transposed, n - 1))
                nc.vector.tensor_scalar(h_q[:, t % 2, :], h_rounded[:], ROUND, QMAX, ALU.subtract, ALU.min) \
                    .then_inc(quantised, 1)
            if live(tile, DOWN):
                b, t, m = back(b0, t0, DOWN)
                dve.wait_ge(down_done, credited(down_done, m + 1))
                dve.wait_ge(dequant_done, m + 1)
                if tile is None or m >= T:
                    dve.wait_ge(x1_stored[t], credited(x1_stored[t], b * 16))
                nc.vector.scalar_tensor_tensor(x1t[:, t, :], down_bank[:, 0:D], dequant[:, t % 2:t % 2 + 1],
                                               xt[:, t, :], ALU.mult, ALU.add).then_inc(x1_done, 1)

        def load_up_sp(sp):
            src = up_wT.rearrange("(k p) n -> p k n", p=P)
            for i, cols in enumerate(CHUNKS):
                sp.dma_start(up_st[:, :, cols], src[:, :, cols]).then_inc(up_loaded[i], 16)

        def load_down_sp(sp):
            sp.dma_start(down_st[:], down_wT.rearrange("(k p) n -> p k n", p=P)).then_inc(down_loaded, 16)

        def store_alphas_sp(sp):
            sp.wait_ge(alpha_done, 3)
            sp.dma_start(alpha_dram, alpha_sb[:].rearrange("b a n -> b (a n)")).then_inc(alpha_stored, 16)

        def load_late_sp(sp, numbers):
            for n in numbers:
                dst, _, src = late[n]
                if n != WO:
                    sp.dma_start(dst[:], src.rearrange("(k p) n -> p k n", p=P)).then_inc(weight_loaded[n], 16)
                    continue
                sp.wait_ge(ostage_zeroed, 1)
                wo_rows = woT.rearrange("(g j d) n -> j d g n", g=G, j=J)
                for j in range(J):
                    sp.dma_start(o_st[32 * j:32 * j + HD, :, :], wo_rows[j]).then_inc(weight_loaded[n], 16)

        def load_small_act(act):
            act.dma_start(cond_sb[:], condT).then_inc(small_loaded, 16)
            act.dma_start(vec_w[:], vec_wT).then_inc(small_loaded, 16)
            act.dma_start(outb_sb[:], out_b.partition_broadcast(B)).then_inc(small_loaded, 16)

        def up_high_act(act):
            for i, cols in enumerate(CHUNKS):
                act.wait_ge(up_loaded[i], 16)
                nc.scalar.activation(up_w[0][:, :, cols], up_st[:, :, cols], ACT.Copy).then_inc(up_high, 1)

        def late_high_act(act, numbers):
            for n in numbers:
                src, dst, _ = late[n]
                act.wait_ge(weight_loaded[n], 64 if n == WO else 16)
                nc.scalar.activation(dst[0][:], src[:], ACT.Copy).then_inc(high_done, 1)

        def load_xa_sp(sp, c):
            sp.dma_start(x_in[:], xa_dram[c].rearrange("t p k n -> p t k n")).then_inc(xa_loaded, 16)

        def split_xa_act(act, c, first=False):
            act.wait_ge(xa_loaded, (c + 1) * 16)
            if not first:
                act.wait_ge(qkv_projected, c)
            nc.scalar.activation(xa_part[0][:].rearrange("p k (t n) -> p t k n", t=T), x_in[:], ACT.Copy) \
                .then_inc(q_in_high, 1)

        def split_xa_pool(pool, c):
            pool.wait_ge(q_in_high, c + 1)
            nc.gpsimd.tensor_tensor(xa_part[1][:].rearrange("p k (t n) -> p t k n", t=T), x_in[:],
                                    xa_part[0][:].rearrange("p k (t n) -> p t k n", t=T).bitcast(f32),
                                    ALU.subtract).then_inc(q_in_low, 1)

        def late_low(eng, ops, n):
            src, dst, _ = late[n]
            eng.wait_ge(high_done, n + 1)
            ops.tensor_tensor(dst[1][:], src[:], dst[0][:].bitcast(f32), ALU.subtract)

        def constants_pool(pool):
            for s, value in list(CREDIT1.items()) + list(CREDIT2.items()):
                nc.gpsimd.sem_inc(s, value)
            nc.gpsimd.memset(ones[:], 1.0).then_inc(consts_ready, 1)
            nc.gpsimd.memset(ident[:], 0.0).then_inc(consts_ready, 1)
            nc.gpsimd.memset(identb[:], 0.0).then_inc(consts_ready, 1)
            nc.gpsimd.memset(minus_half[:], -0.5).then_inc(consts_ready, 1)
            pool.wait_ge(consts_ready, 4)
            for m in (ident, identb):
                nc.gpsimd.affine_select(out=m[:], in_=m[:], compare_op=ALU.not_equal, fill=1.0, base=0,
                                        pattern=[[-1, P]], channel_multiplier=1).then_inc(consts_ready, 1)
            nc.gpsimd.memset(o_st[:], 0.0).then_inc(ostage_zeroed, 1)

        def vectors_pe(pe):
            pe.wait_ge(small_loaded, 16 * 3)
            for v in range(5):
                for k in range(KD):
                    last = nc.tensor.matmul(psum[7][:, (v * KD + k) * B:(v * KD + k + 1) * B],
                                            vec_w[:, v, k * P:(k + 1) * P], cond_sb[:], start=True, stop=True)
            last.then_inc(vectors_done, 1)
            for v in range(2):
                last = nc.tensor.matmul(psum[6][0:B, v * D:(v + 1) * D], cond_sb[:], vec_w[:, 5 + v, :],
                                        start=True, stop=True)
            last.then_inc(vectors_done, 1)

        def mean_pe(pe):
            pe.wait_ge(consts_ready, 6)
            pe.wait_ge(down_steps, 1)
            nc.tensor.matmul(psum[5][:, 0:1], ones[:], absum[:], start=True, stop=True).then_inc(mean_summed, 1)

        def vectors_dve(dve):
            dve.wait_ge(vectors_done, 1)
            vectors = psum[7][:, 0:5 * KD * B].rearrange("p (v b) -> p b v", b=B)
            nc.vector.tensor_scalar(par[:, :, 0:KD], vectors[:, :, 0:KD], 1.0, None, ALU.add).then_inc(par_ready, 1)
            nc.vector.tensor_copy(par[:, :, KD:], vectors[:, :, KD:]).then_inc(par_ready, 1)

        def alphas_dve(dve):
            dve.wait_ge(vectors_done, 2)
            dve.wait_ge(small_loaded, 16 * 3)
            nc.vector.tensor_copy(alpha_sb[:, 0:2, :], psum[6][0:B, :].rearrange("b (a n) -> b a n", a=2)) \
                .then_inc(alpha_done, 1)
            dve.wait_ge(alpha_done, 1)
            nc.vector.tensor_tensor(alpha_sb[:, 2, :], alpha_sb[:, 1, :], outb_sb[:], ALU.mult) \
                .then_inc(alpha_done, 2)

        def up_low_dve(dve):
            for i, cols in enumerate(CHUNKS):
                dve.wait_ge(up_high, i + 1)
                nc.vector.tensor_tensor(up_w[1][:, :, cols], up_st[:, :, cols], up_w[0][:, :, cols].bitcast(f32),
                                        ALU.subtract).then_inc(up_low, 1)

        def down_mean_dve(dve):
            dve.wait_ge(down_loaded, 16)
            nc.vector.tensor_reduce(absum[:], down_st[:], AX.XY, ALU.add, apply_absolute_value=True) \
                .then_inc(down_steps, 1)
            dve.wait_ge(mean_summed, 1)
            nc.vector.tensor_scalar(mean[:], psum[5][:, 0:1], 1.0 / (FF * D), 1e-5, ALU.mult, ALU.max) \
                .then_inc(down_steps, 1)
            dve.wait_ge(down_steps, 2)
            nc.vector.tensor_scalar(wdeq[:], mean[:], 1.0 / QMAX, None, ALU.mult).then_inc(wdeq_ready, 1)
            nc.vector.reciprocal(wscale[:], mean[:]).then_inc(down_steps, 1)
            dve.wait_ge(wdeq_ready, 1)

        def down_quantised_dve(dve):
            dve.wait_ge(down_steps, 3)
            nc.vector.tensor_scalar(down_st[:], down_st[:], wscale[:], 1.0, ALU.mult, ALU.min) \
                .then_inc(down_steps, 1)
            dve.wait_ge(down_steps, 4)
            nc.vector.tensor_scalar(down_st[:], down_st[:], -1.0, ROUND, ALU.max, ALU.add) \
                .then_inc(down_steps, 1)
            dve.wait_ge(down_steps, 5)
            nc.vector.tensor_scalar(down_q[:], down_st[:], ROUND, None, ALU.subtract).then_inc(down_steps, 1)

        def phase1_program(eng, tile_step, before, between=lambda eng: None):
            for t in range(T):
                before(eng, t)
                tile_step(eng, 0, t, t)
            between(eng)
            with eng.Fori(1, B) as b:
                for t in range(T):
                    tile_step(eng, b, t, None)
            for t in range(STORE):
                before(eng, T + t)
                tile_step(eng, B, t, B * T + t)

        SPLITS = {2: (0, 1, 2), 3: (3, 4), T: (5, 6)}
        LATE_ON_DVE = {T + 3: (5, 6)}

        def before_sp(sp, n):
            if n == 0:
                load_up_sp(sp)
            elif n == 2:
                load_down_sp(sp)
                load_late_sp(sp, (0, 1, 2, 3))
            elif n == 3:
                store_alphas_sp(sp)
                sp.wait_ge(up_low, len(CHUNKS))
                load_late_sp(sp, (4, 5))
            elif n == T:
                for s in range(2):
                    sp.wait_ge(xa_stored[s], credited(xa_stored[s], 2 * 16))
                load_xa_sp(sp, 0)

        def between_sp(sp):
            sp.wait_ge(down_steps, 6)
            load_late_sp(sp, (6,))

        def before_act(act, n):
            if n == 0:
                load_small_act(act)
                up_high_act(act)
            late_high_act(act, SPLITS.get(n, ()))
            if n == T + 2:
                split_xa_act(act, 0, first=True)

        def before_pool(pool, n):
            if n == 0:
                constants_pool(pool)
            for m in SPLITS.get(n, ()):
                if n < T:
                    late_low(pool, nc.gpsimd, m)
            if n == T + 3:
                split_xa_pool(pool, 0)

        def before_pe(pe, n):
            if n == 0:
                vectors_pe(pe)
            elif n == 1:
                mean_pe(pe)
                pe.wait_ge(up_low, len(CHUNKS))

        def before_dve(dve, n):
            if n == 0:
                up_low_dve(dve)
                vectors_dve(dve)
                dve.wait_ge(par_ready, 2)
            elif n == 1:
                down_mean_dve(dve)
                alphas_dve(dve)
            elif n == 2:
                down_quantised_dve(dve)
            for m in LATE_ON_DVE.get(n, ()):
                late_low(dve, nc.vector, m)

        with nc.Block() as block:
            @block.sync
            def _(sp):
                phase1_program(sp, load_tile, before_sp, between_sp)
                sp.wait_ge(alpha_stored, 16)

            @block.scalar
            def _(act):
                phase1_program(act, act_tile, before_act)
                for t in range(T):
                    act.wait_ge(x1_stored[t], credited(x1_stored[t], B * 16))
                for s in range(2):
                    act.wait_ge(xa_stored[s], credited(xa_stored[s], B * T // 2 * 16))

            @block.gpsimd
            def _(pool):
                phase1_program(pool, pool_tile, before_pool)

            @block.tensor
            def _(pe):
                phase1_program(pe, pe_tile, before_pe)

            @block.vector
            def _(dve):
                phase1_program(dve, dve_tile, before_dve)
        phase1.close()

        q_stack = sb(ctx, "q_stack", [P, 2 * G, S], f32r)
        k_stack = sb(ctx, "k_stack", [P, 2 * G, S], f32r)
        v_ext = sb(ctx, "v_ext", [P, T, G * J, HD + 1])
        probs = sb(ctx, "probs", [P, 2 * J, S])
        aalpha = sb(ctx, "aalpha", [P, D])
        falpha = sb(ctx, "falpha", [P, 2, D])
        xf_part = [sb(ctx, f"xf_part{i}", [P, KD, S], f32r) for i in range(2)]
        split = sb(ctx, "split", [P, 8, S], f32r)
        x2 = sb(ctx, "x2", [P, T, D])
        rowmax = sb(ctx, "rowmax", [P, J * T])
        shift = [sb(ctx, f"shift{i}", [J * T, P], f32r) for i in range(2)]
        o_sb = sb(ctx, "o_sb", [P, S])
        o_tok = sb(ctx, "o_tok", [P, S])
        inv_sum = sb(ctx, "inv_sum", [P, S // 32, 1])
        ss3 = sb(ctx, "ss3", [P, T])
        ms3 = sb(ctx, "ms3", [P, T])
        rstd3 = sb(ctx, "rstd3", [P, T])
        scratch = [sb(ctx, f"scratch{i}", [P, W]) for i in range(2)]
        hid = [sb(ctx, f"hid{i}", [P, NH, S], f32r) for i in range(2)]
        xn3 = x_in[:].rearrange("p t k n -> p t (k n)")
        score_bank = psum[0:3]
        raw_bank = psum[3:5]
        o_bank = psum[5]
        ab = psum[6:8]
        SOFTMAX_SCALE = HD ** -0.5
        HALF = T // 2
        RAW = J * T + 1
        STACK = 12 * 16
        RESERVED = NH - 2

        def staging(m, w):
            if m == 0:
                return split[:, 2 + w, :], split[:, 6 + w, :]
            return hid[0][:, RESERVED + w, :], hid[1][:, RESERVED + w, :]

        PROJECTION = [(a, m, k) for k in range(KD) for a, m in PARTS]

        def qk_pe(pe, c, m, w, use, h):
            if h == 0:
                pe.wait_ge(q_in_low, credited(q_in_low, c + 1))
                pe.wait_ge(pair_free[w], credited(pair_free[w], use))
            weight = (wq, wk)[w]
            for i in (range(3) if h == 0 else range(3, 6)):
                a, wp, k = PROJECTION[i]
                last = nc.tensor.matmul(ab[w][:], weight[wp][:, k, m * P:(m + 1) * P], xa_part[a][:, k, :],
                                        start=(i == 0), stop=(i == 5))
            if h == 1:
                last.then_inc(pair_full[w], 1)

        def qk_act(act, m, w, use):
            act.wait_ge(pair_full[w], use + 1)
            nc.scalar.activation(staging(m, w)[0], ab[w][:], ACT.Copy, scale=SOFTMAX_SCALE if w == 0 else 1.0) \
                .then_inc(qk_high, 1)

        def qk_dve(dve, m, w, n):
            dve.wait_ge(qk_high, n + w + 1)
            high, low = staging(m, w)
            nc.vector.scalar_tensor_tensor(low, ab[w][:], SOFTMAX_SCALE if w == 0 else 1.0, high.bitcast(f32),
                                           ALU.mult, ALU.subtract).then_inc(pair_free[w], 1)

        def stack_sp(sp, m, use=None):
            for w, stack, parts in ((0, q_stack, (0, 0, 1)), (1, k_stack, (0, 1, 0))):
                if use is not None:
                    sp.wait_ge(pair_free[w], credited(pair_free[w], use + 1))
                for half in range(2):
                    for r, part in enumerate(parts):
                        sp.dma_start(stack[64 * half + HD * r:64 * half + HD * (r + 1), G * m:G * m + G, :].bitcast(f32),
                                     staging(m, w)[part][64 * half:64 * half + 64, :].bitcast(f32)) \
                            .then_inc(stacked[m], 16)

        def v_pe(pe, c, m, use, h):
            if h == 0:
                pe.wait_ge(q_in_low, credited(q_in_low, c + 1))
                pe.wait_ge(pair_free[m], credited(pair_free[m], use))
            tok = (m * HALF + h) * P
            for i, (a, wp, k) in enumerate(PROJECTION):
                last = nc.tensor.matmul(ab[m][:, h * D:(h + 1) * D], xa_part[a][:, k, tok:tok + P],
                                        wv[wp][:, k, :], start=(i == 0), stop=(i == 5))
            if h == 1:
                last.then_inc(pair_full[m], 1)

        def v_dve(dve, c, m, use):
            dve.wait_ge(pv_done, credited(pv_done, c * 16))
            dve.wait_ge(pair_full[m], use + 1)
            nc.vector.tensor_scalar(v_ext[:, m * HALF:(m + 1) * HALF, :, 0:HD],
                                    ab[m][:].rearrange("p (t h d) -> p t h d", t=HALF, d=HD), 1.0, None, ALU.mult) \
                .then_inc(pair_free[m], 1)

        def raw_at(s):
            return 2 * (s // (2 * T)) + (s + 1) % 2, s % (2 * T) // 2

        def raw_score(pe, b, g, s):
            j, qt = raw_at(s)
            half, slot = j % 2, 2 * g + j // 2
            idx = RAW * g + s
            if s == 0 and g % 2 == 0:
                pe.wait_ge(stacked[g // 2], (b + 1) * STACK)
            pe.wait_ge(raw_read, credited(raw_read, b * (RAW * G) + (idx - 1)))
            rows = slice(64 * half, 64 * half + ROWS)
            nc.tensor.matmul(raw_bank[idx % 2][:], q_stack[rows, slot, qt * P:(qt + 1) * P], k_stack[rows, slot, :],
                             start=True, stop=True).then_inc(raw_full, 1)

        def maxima_transposed(pe, b, g):
            idx = RAW * g + J * T
            pe.wait_ge(raw_read, credited(raw_read, b * (RAW * G) + idx))
            nc.tensor.transpose(raw_bank[idx % 2][0:J * T, 0:P], rowmax[:], ident[:]).then_inc(raw_full, 1)

        def maximum_dve(dve, b, g, s):
            j, qt = raw_at(s)
            idx = RAW * g + s
            col = (j % 2) * 8 + (j // 2) * T + qt
            dve.wait_ge(raw_full, b * (RAW * G) + (idx + 1))
            nc.vector.reduce_max(rowmax[:, col:col + 1], raw_bank[idx % 2][:], AX.X).then_inc(raw_read, 1)

        def shift_dve(dve, b, g):
            idx = RAW * g + J * T
            dve.wait_ge(raw_full, b * (RAW * G) + (idx + 1))
            dve.wait_ge(shift_loaded, credited(shift_loaded, (b * G + g) * 32))
            src = raw_bank[idx % 2][0:J * T, 0:P]
            nc.vector.tensor_scalar(shift[0][:], src, -1.0, None, ALU.mult).then_inc(shift_high, 1)
            dve.wait_ge(shift_high, b * G + (g + 1))
            nc.vector.scalar_tensor_tensor(shift[1][:], src, -1.0, shift[0][:].bitcast(f32), ALU.mult,
                                           ALU.subtract).then_inc(raw_read, 1)

        def shift_sp(sp, b, g):
            sp.wait_ge(raw_read, credited(raw_read, b * (RAW * G) + RAW * (g + 1)))
            for part in range(2):
                row = ROWS + part
                sp.dma_start(q_stack[row:row + 65:64, 2 * g:2 * g + 2, :].bitcast(f32),
                             shift[part][:].bitcast(f32)).then_inc(shift_loaded, 16)

        def score_pe(pe, b, g, kt, j):
            half, slot = j % 2, 2 * g + j // 2
            c = 16 * g + J * kt + j
            pe.wait_ge(exp_done, credited(exp_done, b * 64 + (c - 2 if c >= 3 else 0)))
            rows = slice(64 * half, 64 * half + SROWS)
            nc.tensor.matmul(score_bank[c % 3][:], k_stack[rows, slot, kt * P:(kt + 1) * P], q_stack[rows, slot, :],
                             start=True, stop=True).then_inc(score_full, 1)

        def exp_act(act, b, g, kt, j):
            if j == 0:
                act.wait_ge(pv_done, credited(pv_done, b * 16 + (4 * g + kt - 1)))
            c = 16 * g + J * kt + j
            act.wait_ge(score_full, b * 64 + (c + 1))
            nc.scalar.activation(probs[:, (kt % 2) * J + j, :], score_bank[c % 3][:], ACT.Exp).then_inc(exp_done, 1)

        def values_pe(pe, b, g, kt, u=None):
            if u is not None:
                for m in range(2):
                    pe.wait_ge(pair_free[m], credited(pair_free[m], u + 1))
            pe.wait_ge(exp_done, credited(exp_done, b * 64 + (16 * g + J * (kt + 1))))
            if kt == 0:
                pe.wait_ge(o_read, credited(o_read, b * G + g))
            for j in range(J):
                last = nc.tensor.matmul(o_bank[32 * j:32 * j + HD + 1, :], v_ext[:, kt, J * g + j, :],
                                        probs[:, (kt % 2) * J + j, :], start=(kt == 0), stop=(kt == T - 1))
            last.then_inc(pv_done, 1)

        def normalise_dve(dve, b, g):
            sums_dve(dve, b, g)
            divide_dve(dve, b, g)
            turn_dve(dve, b, g)

        def sums_dve(dve, b, g):
            dve.wait_ge(pv_done, credited(pv_done, b * 16 + 4 * (g + 1)))
            nc.vector.transpose(o_tok[:], o_bank[:]).then_inc(o_read, 1)

        def divide_dve(dve, b, g):
            blocks = o_tok[:].rearrange("p (q d) -> p q d", d=32)
            dve.wait_ge(o_read, credited(o_read, b * G + (g + 1)))
            nc.vector.reciprocal(inv_sum[:], blocks[:, :, HD:HD + 1]).then_inc(norm_steps, 1)
            dve.wait_ge(norm_steps, b * (2 * G) + (2 * g + 1))
            nc.vector.tensor_tensor(blocks, blocks, inv_sum[:].broadcast_to([P, S // 32, 32]), ALU.mult) \
                .then_inc(norm_steps, 1)

        def turn_dve(dve, b, g):
            dve.wait_ge(norm_steps, b * (2 * G) + (2 * g + 2))
            dve.wait_ge(on_low, credited(on_low, b * G + g))
            nc.vector.transpose(o_sb[:], o_tok[:]).then_inc(on_done, 1)

        def normalise_act(act, b, g, staged):
            act.wait_ge(on_done, b * G + (g + 1))
            if g == 0:
                act.wait_ge(wo_done, credited(wo_done, b))
            if g == 2:
                act.wait_ge(stacked[0], staged * STACK)
            nc.scalar.activation(split[:, g, :], o_sb[:], ACT.Copy).then_inc(on_high, 1)

        def normalise_pool(pool, b, g):
            pool.wait_ge(on_high, b * G + (g + 1))
            nc.gpsimd.tensor_tensor(split[:, 4 + g, :], o_sb[:], split[:, g, :].bitcast(f32), ALU.subtract) \
                .then_inc(on_low, 1)

        def bank_view(m):
            return ab[m][:].rearrange("p (t n) -> p t n", t=HALF)

        def halves(tile, m):
            return tile[:, m * HALF:(m + 1) * HALF, :]

        def by_tiles(tile):
            return tile[:].rearrange("p (t n) -> p t n", t=HALF)

        def wo_pe(pe, c, t, use, h):
            m = t // HALF
            if h == 0 and t == 0:
                pe.wait_ge(on_low, credited(on_low, c * G + G))
            if h == 0 and t % HALF == 0:
                pe.wait_ge(pair_free[m], credited(pair_free[m], use))
            steps = [(a, wp, g) for g in range(G) for a, wp in PARTS]
            for i in (range(6) if h == 0 else range(6, 12)):
                a, wp, g = steps[i]
                last = nc.tensor.matmul(ab[m][:, (t % HALF) * D:(t % HALF + 1) * D],
                                        split[:, 4 * a + g, t * P:(t + 1) * P], wo[wp][:, g, :],
                                        start=(i == 0), stop=(i == len(steps) - 1))
            if h == 1 and t % HALF == HALF - 1:
                last.then_inc(pair_full[m], 1)
            if h == 1 and t == T - 1:
                nc.tensor.nop().then_inc(wo_done, 1)

        def wo_dve(dve, c, m, use):
            dve.wait_ge(aalpha_loaded, (c + 1) * 16)
            dve.wait_ge(pair_full[m], use + 1)
            dve.wait_ge(y_done, credited(y_done, 2 * c))
            nc.vector.tensor_tensor(by_tiles(scratch[m]), bank_view(m),
                                    aalpha[:].unsqueeze(1).broadcast_to([P, HALF, D]), ALU.mult) \
                .then_inc(pair_free[m], 1)
            dve.wait_ge(x1_loaded[m], (c + 1) * 16)
            dve.wait_ge(pair_free[m], credited(pair_free[m], use + 1))
            nc.vector.tensor_tensor(halves(x2, m), halves(x2, m), by_tiles(scratch[m]), ALU.add) \
                .then_inc(x2_done[m], 1)

        def squares_act(act, c):
            for t in range(T):
                m = t // HALF
                act.wait_ge(x2_done[m], credited(x2_done[m], c + 1))
                last = nc.scalar.activation(scratch[m][:, (t % HALF) * D:(t % HALF + 1) * D], x2[:, t, :], ACT.Square,
                                            accum_out=ss3[:, t:t + 1])
            last.then_inc(square3_done, 1)

        def mean_dve(dve, c):
            dve.wait_ge(square3_done, c + 1)
            nc.vector.tensor_scalar(ms3[:], ss3[:], 1.0 / D, EPS, ALU.mult, ALU.add).then_inc(ms3_done, 1)

        def rstd_pool(pool, c):
            pool.wait_ge(ms3_done, c + 1)
            nc.gpsimd.tensor_tensor(rstd3[:], ms3[:], minus_half[:], ALU.pow).then_inc(rstd3_done, 1)

        def normed_dve(dve, c, splits):
            dve.wait_ge(rstd3_done, c + 1)
            dve.wait_ge(q_in_low, credited(q_in_low, splits))
            for t in range(T):
                last = nc.vector.tensor_scalar(xn3[:, t, :], x2[:, t, :], rstd3[:, t:t + 1], None, ALU.mult)
            last.then_inc(xn3_done, 1)

        def bias_pool(pool, c):
            pool.wait_ge(falpha_loaded, (c + 1) * 16)
            pool.wait_ge(xn3_done, c + 1)
            nc.gpsimd.tensor_tensor(x2[:], x2[:], falpha[:, 1:2, :].broadcast_to([P, T, D]), ALU.add) \
                .then_inc(x2_biased, 1)

        def xf_pe(pe, c, use):
            pe.wait_ge(xn3_done, c + 1)
            for k in range(KD):
                pe.wait_ge(pair_free[k], credited(pair_free[k], use))
                for t in range(T):
                    last = nc.tensor.transpose(ab[k][:, t * P:(t + 1) * P], xn3[:, t, k * P:(k + 1) * P], ident[:])
                last.then_inc(pair_full[k], 1)

        def xf_dve(dve, c, use):
            for k in range(KD):
                dve.wait_ge(pair_full[k], use + 1)
            for k in range(KD):
                nc.vector.tensor_scalar(x_in[:, :, k, :], ab[k][:].rearrange("p (t n) -> p t n", t=T),
                                        par[:, c, FGAM + k:FGAM + k + 1], par[:, c, FBET + k:FBET + k + 1],
                                        ALU.mult, ALU.add).then_inc(pair_free[k], 1)

        def xf_act(act, c, use):
            act.wait_ge(ffn_projected, credited(ffn_projected, c))
            for k in range(KD):
                act.wait_ge(pair_free[k], credited(pair_free[k], use + 1))
                nc.scalar.activation(xf_part[0][:, k, :].rearrange("p (t n) -> p t n", t=T), x_in[:, :, k, :],
                                     ACT.Copy).then_inc(f_in_high, 1)

        def xf_pool(pool, c):
            for k in range(KD):
                pool.wait_ge(f_in_high, KD * c + (k + 1))
                nc.gpsimd.tensor_tensor(xf_part[1][:, k, :].rearrange("p (t n) -> p t n", t=T), x_in[:, :, k, :],
                                        xf_part[0][:, k, :].rearrange("p (t n) -> p t n", t=T).bitcast(f32),
                                        ALU.subtract).then_inc(f_in_low, 1)

        def hidden_pe(pe, c, n, f, use, h):
            if h == 0:
                pe.wait_ge(f_in_low, credited(f_in_low, KD * (c + 1)))
                pe.wait_ge(pair_free[n], credited(pair_free[n], use + f))
            weight = (gate_w, hidden_w)[n]
            for i in (range(3) if h == 0 else range(3, 6)):
                a, wp, k = PROJECTION[i]
                last = nc.tensor.matmul(ab[n][:], weight[wp][:, k, f * P:(f + 1) * P], xf_part[a][:, k, :],
                                        start=(i == 0), stop=(i == 5))
            if h == 1:
                last.then_inc(pair_full[n], 1)
                if n == 1 and f == NH - 1:
                    nc.tensor.nop().then_inc(ffn_projected, 1)

        def gate_act(act, c, f, use):
            act.wait_ge(pair_full[0], use + (f + 1))
            if f > 0:
                act.wait_ge(pair_free[1], credited(pair_free[1], use + f))
            nc.scalar.activation(scratch[0][:], ab[0][:], ACT.Tanh, scale=0.5).then_inc(tanh_done, 1)

        def gate_dve(dve, c, f):
            dve.wait_ge(tanh_done, c * NH + (f + 1))
            nc.vector.scalar_tensor_tensor(scratch[0][:], scratch[0][:], 1.0, ab[0][:], ALU.add, ALU.mult) \
                .then_inc(pair_free[0], 1)

        def product_dve(dve, c, f, use):
            dve.wait_ge(pair_free[0], credited(pair_free[0], use + (f + 1)))
            dve.wait_ge(prod_low, credited(prod_low, c * NH + f))
            dve.wait_ge(pair_full[1], use + (f + 1))
            nc.vector.scalar_tensor_tensor(scratch[1][:], scratch[0][:], 0.5, ab[1][:], ALU.mult, ALU.mult) \
                .then_inc(pair_free[1], 1)

        def product_act(act, c, f, use, staged):
            if f == RESERVED:
                act.wait_ge(stacked[1], staged * STACK)
            act.wait_ge(pair_free[1], credited(pair_free[1], use + (f + 1)))
            nc.scalar.activation(hid[0][:, f, :], scratch[1][:], ACT.Copy).then_inc(prod_high, 1)

        def product_pool(pool, c, f):
            pool.wait_ge(prod_high, c * NH + (f + 1))
            nc.gpsimd.tensor_tensor(hid[1][:, f, :], scratch[1][:], hid[0][:, f, :].bitcast(f32), ALU.subtract) \
                .then_inc(prod_low, 1)

        def out_pe(pe, c, t, half, use, h):
            m = t // HALF
            if h == 0 and half == 0:
                if t == 0:
                    pe.wait_ge(prod_low, credited(prod_low, c * NH + NH))
                if t % HALF == 0:
                    pe.wait_ge(pair_free[m], credited(pair_free[m], use))
            steps = [(a, wp, f) for f in range(NH) for a, wp in PARTS]
            n = len(steps) // 4
            first = (2 * half + h) * n
            for i in range(first, first + n):
                a, wp, f = steps[i]
                last = nc.tensor.matmul(ab[m][:, (t % HALF) * D:(t % HALF + 1) * D], hid[a][:, f, t * P:(t + 1) * P],
                                        out_w[wp][:, f, :], start=(i == 0), stop=(i == len(steps) - 1))
            if t % HALF == HALF - 1 and half == 1 and h == 1:
                last.then_inc(pair_full[m], 1)

        def out_dve(dve, c, m, use):
            dve.wait_ge(falpha_loaded, (c + 1) * 16)
            dve.wait_ge(prod_low, credited(prod_low, c * NH + NH))
            dve.wait_ge(pair_full[m], use + 1)
            nc.vector.tensor_tensor(by_tiles(scratch[m]), bank_view(m), falpha[:, 0:1, :].broadcast_to([P, HALF, D]),
                                    ALU.mult).then_inc(pair_free[m], 1)

        def out_pool(pool, c, m, use):
            pool.wait_ge(x2_biased, c + 1)
            pool.wait_ge(pair_free[m], credited(pair_free[m], use + 1))
            nc.gpsimd.tensor_tensor(halves(x2, m), halves(x2, m), by_tiles(scratch[m]), ALU.add).then_inc(y_done, 1)

        STEPS = G * T
        FFN_PIECES = [(what, f) for f in range(NH) for what in ("gate", "hidden")] + [("gap",)] + \
                     [("out", t, half) for t in range(T) for half in range(2)]
        HEAD = {0: [("v", 0), ("v", 1)], 1: [("qk", 1, 0), ("qk", 1, 1)], 2: [("wo", t) for t in range(T)],
                3: [("qk", 0, 0)], 4: [("qk", 0, 1), ("xf",)]}
        FIRST_FFN = 6
        RAWS = ((1, 2, 1, 0), (1, 2, 1, 2), (2, 2, 1, 1), (0, 0, 0, 0))
        MAXIMA_AT = (T - 1, 0)
        LOAD = (2, 2, 4, 2)

        def plan(ffn, following):
            table = [[] for _ in range(STEPS * J)]
            left = list(FFN_PIECES) if ffn else []
            for n in range(STEPS):
                pieces = [p for p in HEAD.get(n, []) if (ffn or p[0] not in ("wo", "xf"))
                          and (following or p[:2] != ("qk", 0))]
                if n >= FIRST_FFN and left:
                    take = LOAD[n % T]
                    pieces += left[:take]
                    left = left[take:]
                parts = [(p, h) for p in pieces for h in range(2)]
                for i, part in enumerate(parts):
                    table[n * J + i * J // len(parts)].append(part)
            return table

        def finished(table, lag):
            out_table = [[] for _ in range(STEPS * J + 1)]
            for pos, parts in enumerate(table):
                for p, h in parts:
                    if h == 1:
                        out_table[min(pos + lag, STEPS * J)].append(p)
            return out_table

        def uses(ffn, following):
            at, n = {}, 0
            for stage, there in (("v", True), (("qk", 1), True), ("wo", ffn), (("qk", 0), following), ("xf", ffn)):
                at[stage] = n
                n += 1 if there else 0
            at["hidden"] = n
            at["out"] = n + NH
            return at, (n + NH + 1 if ffn else n)

        BEFORE = 1
        USES_FIRST, USES_LOOP = uses(False, True)[1], uses(True, True)[1]

        def piece_pe(pe, b, u, at, p, h):
            if p[0] == "v":
                v_pe(pe, b, p[1], u + at["v"], h)
            elif p[0] == "qk":
                m, w = p[1:]
                qk_pe(pe, b if m == 1 else b + 1, m, w, u + at["qk", m], h)
                if (m, w, h) == (1, 1, 1):
                    nc.tensor.nop().then_inc(qkv_projected, 1)
            elif p[0] == "wo":
                wo_pe(pe, b - 1, p[1], u + at["wo"], h)
            elif p[0] == "xf":
                if h == 1:
                    xf_pe(pe, b - 1, u + at["xf"])
            elif p[0] == "gap":
                pass
            elif p[0] == "out":
                out_pe(pe, b - 1, p[1], p[2], u + at["out"], h)
            else:
                hidden_pe(pe, b - 1, 0 if p[0] == "gate" else 1, p[1], u + at["hidden"], h)

        def piece_act(act, b, u, at, p, staged, late):
            if p[0] == "hidden" and late:
                product_act(act, b - 1, p[1], u + at["hidden"], staged)
            elif p[0] == "gate" and not late:
                gate_act(act, b - 1, p[1], u + at["hidden"])
            elif p[0] == "qk" and not late:
                qk_act(act, p[1], p[2], u + at["qk", p[1]])

        def piece_dve(dve, b, u, at, p):
            if p[0] == "v":
                v_dve(dve, b, p[1], u + at["v"])
            elif p[0] == "qk":
                qk_dve(dve, p[1], p[2], 4 * b + (2 if p[1] == 1 else 4))
            elif p[0] == "wo" and p[1] % HALF == HALF - 1:
                wo_dve(dve, b - 1, p[1] // HALF, u + at["wo"])
            elif p[0] == "xf":
                xf_dve(dve, b - 1, u + at["xf"])
            elif p[0] == "gate":
                gate_dve(dve, b - 1, p[1])
            elif p[0] == "hidden":
                product_dve(dve, b - 1, p[1], u + at["hidden"])
            elif p[0] == "out" and p[1] % HALF == HALF - 1 and p[2] == 1:
                out_dve(dve, b - 1, p[1] // HALF, u + at["out"])

        def piece_pool(pool, b, u, at, p):
            if p[0] == "hidden":
                product_pool(pool, b - 1, p[1])
            elif p[0] == "out" and p[1] % HALF == HALF - 1 and p[2] == 1:
                out_pool(pool, b - 1, p[1] // HALF, u + at["out"])

        SPLIT_AT = 2 * J
        OPEN_AT = 2 * T * J + 2
        SQUARES_AT = 3 * J + 2
        MEAN_AT = 3 * J + 3
        NORMED_AT = 4 * J
        XF_AT = 4 * J + 4

        def last_of(b, g):
            return (b, g - 1) if g > 0 else (b - 1, G - 1)

        def pe_batch(pe, b, u, ffn, following):
            table, at = plan(ffn, following), uses(ffn, following)[0]
            for pos in range(STEPS * J):
                n, j = pos // J, pos % J
                g, kt = n // T, n % T
                if pos % (T * J) == 0:
                    pe.wait_ge(shift_loaded, credited(shift_loaded, (b * G + (g + 1)) * 32))
                if pos == OPEN_AT and following:
                    for w in range(2):
                        pe.wait_ge(pair_free[w], credited(pair_free[w], u + at["qk", 0] + 1))
                score_pe(pe, b, g, kt, j)
                if pos == OPEN_AT and following:
                    nc.tensor.nop().then_inc(stack_open, 1)
                nb, ng = (b, g + 1) if g + 1 < G else (b + 1, 0)
                if g + 1 < G or following:
                    for s in raws_at(kt, j):
                        raw_score(pe, nb, ng, s)
                    if (kt, j) == MAXIMA_AT:
                        maxima_transposed(pe, nb, ng)
                if j == 1 and (n > 0 or ffn):
                    pb, pg = last_of(b, g) if kt == 0 else (b, g)
                    values_pe(pe, pb, pg, (kt - 1) % T, u + at["v"] if n == 1 else None)
                for p, h in table[pos]:
                    piece_pe(pe, b, u, at, p, h)

        def raws_at(kt, j):
            first = sum(sum(r) for r in RAWS[:kt]) + sum(RAWS[kt][:j])
            return range(first, first + RAWS[kt][j])

        def act_batch(act, b, u, ffn, following):
            table, at = plan(ffn, following), uses(ffn, following)[0]
            early, late = finished(table, 0), finished(table, 1)
            for pos in range(STEPS * J + 1):
                n, j = pos // J, pos % J
                g, kt = n // T, n % T
                if n < STEPS:
                    exp_act(act, b, g, kt, j)
                    if (kt, j) == (1, 1) and (g > 0 or ffn):
                        pb, pg = last_of(b, g)
                        normalise_act(act, pb, pg, b + 2 if following else b + 1)
                if pos == SPLIT_AT and following:
                    split_xa_act(act, b + 1)
                if ffn and pos == SQUARES_AT:
                    squares_act(act, b - 1)
                if ffn and pos == XF_AT:
                    xf_act(act, b - 1, u + at["xf"])
                for p in early[pos]:
                    piece_act(act, b, u, at, p, b + 1, False)
                for p in late[pos]:
                    piece_act(act, b, u, at, p, b + 1, True)

        def dve_batch(dve, b, u, ffn, following):
            table, at = plan(ffn, following), uses(ffn, following)[0]
            done = finished(table, 1)
            for pos in range(STEPS * J + 1):
                n, j = pos // J, pos % J
                g, kt = n // T, n % T
                nb, ng = (b, g + 1) if g + 1 < G else (b + 1, 0)
                if n < STEPS and (g + 1 < G or following):
                    for s in raws_at(kt, j):
                        maximum_dve(dve, nb, ng, s)
                    if (kt, j) == MAXIMA_AT:
                        shift_dve(dve, nb, ng)
                if n < STEPS and (g > 0 or ffn):
                    if (kt, j) == (0, 1):
                        sums_dve(dve, *last_of(b, g))
                    if (kt, j) == (0, 3):
                        divide_dve(dve, *last_of(b, g))
                    if (kt, j) == (1, 0):
                        turn_dve(dve, *last_of(b, g))
                if ffn and pos == MEAN_AT:
                    mean_dve(dve, b - 1)
                if ffn and pos == NORMED_AT:
                    normed_dve(dve, b - 1, b + 2 if following else b + 1)
                for p in done[pos]:
                    piece_dve(dve, b, u, at, p)

        def pool_batch(pool, b, u, ffn, following):
            table, at = plan(ffn, following), uses(ffn, following)[0]
            done = finished(table, 3)
            for pos in range(STEPS * J + 1):
                n, j = pos // J, pos % J
                g, kt = n // T, n % T
                if n < STEPS and (kt, j) == (1, 1) and (g > 0 or ffn):
                    normalise_pool(pool, *last_of(b, g))
                if pos == SPLIT_AT and following:
                    split_xa_pool(pool, b + 1)
                if ffn and pos == MEAN_AT:
                    rstd_pool(pool, b - 1)
                if ffn and pos == XF_AT:
                    xf_pool(pool, b - 1)
                    bias_pool(pool, b - 1)
                for p in done[pos]:
                    piece_pool(pool, b, u, at, p)

        def sp_x1(sp, c):
            for m in range(2):
                sp.wait_ge(y_stored[m], credited(y_stored[m], c * 16))
                sp.dma_start(halves(x2, m), x1_dram[c].rearrange("t p n -> p t n")[:, m * HALF:(m + 1) * HALF, :]) \
                    .then_inc(x1_loaded[m], 16)
            sp.wait_ge(x2_done[1], credited(x2_done[1], c))
            sp.dma_start(aalpha[:], alpha_dram[c, 0:D].partition_broadcast(P)).then_inc(aalpha_loaded, 16)
            sp.wait_ge(y_done, credited(y_done, 2 * c))
            sp.dma_start(falpha[:], alpha_dram[c, D:3 * D].rearrange("(a n) -> a n", a=2).partition_broadcast(P)) \
                .then_inc(falpha_loaded, 16)

        def sp_store(sp, c):
            for m in range(2):
                sp.wait_ge(y_done, credited(y_done, 2 * c + (m + 1)))
                sp.dma_start(out[c, m * HALF * P:(m + 1) * HALF * P, :].rearrange("(t p) n -> p t n", p=P),
                             halves(x2, m)).then_inc(y_stored[m], 16)

        def sp_batch(sp, b, u, ffn, following):
            at = uses(ffn, following)[0]
            if following:
                sp.wait_ge(q_in_low, credited(q_in_low, b + 1))
                if ffn:
                    sp.wait_ge(f_in_low, credited(f_in_low, (b - 1) * KD))
                load_xa_sp(sp, b + 1)
            if ffn:
                sp_x1(sp, b - 1)
            stack_sp(sp, 1, u + at["qk", 1])
            shift_sp(sp, b, 1)
            shift_sp(sp, b, 2)
            if following:
                sp.wait_ge(stack_open, b + 1)
                stack_sp(sp, 0)
            shift_sp(sp, b, 3)
            if following:
                shift_sp(sp, b + 1, 0)
            if ffn:
                sp_store(sp, b - 1)

        END = BEFORE + USES_FIRST + (B - 2) * USES_LOOP + uses(True, False)[1]

        def sp_before(sp):
            sp.wait_ge(ones_ready, 2)
            sp.wait_ge(stack_ones, 1)
            stack_sp(sp, 0, 0)
            shift_sp(sp, 0, 0)

        def sp_after(sp):
            sp_x1(sp, B - 1)
            sp_store(sp, B - 1)
            for m in range(2):
                sp.wait_ge(y_stored[m], credited(y_stored[m], B * 16))

        def act_before(act):
            for w in range(2):
                qk_act(act, 0, w, 0)

        def act_after(act):
            normalise_act(act, B - 1, G - 1, B)
            squares_act(act, B - 1)
            xf_act(act, B - 1, END + 1)
            for f in range(NH):
                gate_act(act, B - 1, f, END + 2)
                product_act(act, B - 1, f, END + 2, B)

        def pool_before(pool):
            nc.gpsimd.memset(k_stack[:, G:2 * G, :].bitcast(f32), 1.0).then_inc(ones_ready, 1)
            nc.gpsimd.memset(v_ext[:, :, :, HD:HD + 1], 1.0).then_inc(ones_ready, 1)

        def pool_after(pool):
            normalise_pool(pool, B - 1, G - 1)
            rstd_pool(pool, B - 1)
            xf_pool(pool, B - 1)
            bias_pool(pool, B - 1)
            for f in range(NH):
                product_pool(pool, B - 1, f)
            for m in range(2):
                out_pool(pool, B - 1, m, END + 2 + NH)

        def pe_before(pe):
            for w in range(2):
                for h in range(2):
                    qk_pe(pe, 0, 0, w, 0, h)
            for s in range(J * T):
                raw_score(pe, 0, 0, s)
            maxima_transposed(pe, 0, 0)

        def pe_after(pe):
            values_pe(pe, B - 1, G - 1, T - 1)
            for t in range(T):
                for h in range(2):
                    wo_pe(pe, B - 1, t, END, h)
            xf_pe(pe, B - 1, END + 1)
            for f in range(NH):
                for n in range(2):
                    for h in range(2):
                        hidden_pe(pe, B - 1, n, f, END + 2, h)
            for t in range(T):
                for half in range(2):
                    for h in range(2):
                        out_pe(pe, B - 1, t, half, END + 2 + NH, h)

        def dve_before(dve):
            nc.vector.memset(k_stack[:, 0:G, :].bitcast(f32), 1.0).then_inc(stack_ones, 1)
            nc.vector.memset(o_bank[:], 0.0)
            dve.wait_ge(ones_ready, 2)
            for w in range(2):
                qk_dve(dve, 0, w, 0)
            for s in range(J * T):
                maximum_dve(dve, 0, 0, s)
            shift_dve(dve, 0, 0)

        def dve_after(dve):
            normalise_dve(dve, B - 1, G - 1)
            for m in range(2):
                wo_dve(dve, B - 1, m, END)
            mean_dve(dve, B - 1)
            normed_dve(dve, B - 1, B)
            xf_dve(dve, B - 1, END + 1)
            for f in range(NH):
                gate_dve(dve, B - 1, f)
                product_dve(dve, B - 1, f, END + 2)
            for m in range(2):
                out_dve(dve, B - 1, m, END + 2 + NH)

        def phase2_program(eng, before, batch, after):
            before(eng)
            batch(eng, 0, BEFORE, False, True)
            with eng.Fori(0, B - 2) as i:
                batch(eng, i + 1, i * USES_LOOP + (BEFORE + USES_FIRST), True, True)
            batch(eng, B - 1, BEFORE + USES_FIRST + (B - 2) * USES_LOOP, True, False)
            after(eng)

        with nc.Block() as block:
            @block.sync
            def _(sp):
                phase2_program(sp, sp_before, sp_batch, sp_after)

            @block.scalar
            def _(act):
                phase2_program(act, act_before, act_batch, act_after)

            @block.gpsimd
            def _(pool):
                phase2_program(pool, pool_before, pool_batch, pool_after)

            @block.tensor
            def _(pe):
                phase2_program(pe, pe_before, pe_batch, pe_after)

            @block.vector
            def _(dve):
                phase2_program(dve, dve_before, dve_batch, dve_after)


def kernel(x, cond_256, L0_cond_norm_w, L0_cond_up_w, L0_cond_down_w, L1_cond_attn_gamma_w, L1_cond_attn_beta_w,
           L1_cond_W_q, L1_cond_W_k, L1_cond_W_v, L1_cond_W_o, L1_cond_attn_alpha_w, L1_cond_ffn_gamma_w,
           L1_cond_ffn_beta_w, L1_cond_gate_w, L1_cond_hidden_w, L1_cond_out_w, L1_cond_out_b,
           L1_cond_ffn_alpha_w):
    import numpy as np
    import concourse.bacc as bacc
    from concourse.bass_utils import run_bass_kernel_spmd

    x = np.asarray(x)
    batches, tokens, width = x.shape

    def t(w):
        return np.ascontiguousarray(np.asarray(w).T)

    def by_slots(w):
        w = np.asarray(w).reshape(2, 4, 2, 16, width)
        return t(w.transpose(0, 2, 3, 1, 4).reshape(width, width))

    xT = np.ascontiguousarray(x.reshape(batches * tokens // 128, 128, width // 128, 128).transpose(0, 3, 2, 1))
    vectors = (L0_cond_norm_w, L1_cond_attn_gamma_w, L1_cond_attn_beta_w, L1_cond_ffn_gamma_w, L1_cond_ffn_beta_w,
               L1_cond_attn_alpha_w, L1_cond_ffn_alpha_w)
    arrays = {
        "x_tok": np.ascontiguousarray(x), "xT": xT, "condT": t(cond_256),
        "vec_wT": np.stack([t(w) for w in vectors], axis=1),
        "up_wT": t(L0_cond_up_w), "down_wT": t(L0_cond_down_w), "wqT": by_slots(L1_cond_W_q),
        "wkT": by_slots(L1_cond_W_k), "wvT": t(L1_cond_W_v), "woT": t(L1_cond_W_o), "gate_wT": t(L1_cond_gate_w),
        "hidden_wT": t(L1_cond_hidden_w), "out_wT": t(L1_cond_out_w), "out_b": np.asarray(L1_cond_out_b),
    }
    nc = bacc.Bacc("TRN2", target_bir_lowering=False, num_devices=1)
    args = [nc.dram_tensor(name, a.shape, mybir.dt.from_np(a.dtype), kind="ExternalInput").ap()
            for name, a in arrays.items()]
    out = nc.dram_tensor("out", x.shape, mybir.dt.float32, kind="ExternalOutput").ap()
    cond_seq_kernel(nc, *args, out)
    r = run_bass_kernel_spmd(nc, [arrays], core_ids=[0])
    return r.results[0]["out"]
```
